# Optimizing a Trainium2 kernel written in Bass

```python
import numpy as np
import jax
import jax.numpy as jnp

def _softmax(x, axis=-1):
    return jax.nn.softmax(x, axis=axis)

def _gelu(x):
    return jax.nn.gelu(x, approximate=True)

def _silu(x):
    return jax.nn.silu(x)

def _sigmoid(x):
    return jax.nn.sigmoid(x)

def _layernorm(x, axis=-1, eps=1e-05):
    m = jnp.mean(x, axis=axis, keepdims=True)
    v = jnp.var(x, axis=axis, keepdims=True)
    return (x - m) / jnp.sqrt(v + eps)

def _scatter_add(tgt, idx, src, axis=0):
    return tgt.at[idx].add(src)

def _segment_sum(src, seg, n):
    return jax.ops.segment_sum(src, seg, n)
kernel_name = 'mk_gnn_resnorm_d4_gnn_r32_ab9188'

def setup_inputs(seed: int=0):
    np.random.seed(seed)
    _w = jnp.asarray

    def _rec_inputs():
        import jax
        import jax.numpy as jnp
        _gk = jax.random.key(seed)
        x = -0.000202 + 1 * jax.random.normal(jax.random.fold_in(_gk, 1), (50000, 128), jnp.float32)
        src = jax.random.randint(jax.random.fold_in(_gk, 2), (25000,), 0, 50000, jnp.int32)
        dst = jnp.minimum((50000 * jax.random.uniform(jax.random.fold_in(_gk, 3), (25000,)) ** 2.0).astype(jnp.int32), 49999)
        _o = jnp.argsort(dst, stable=True)
        src = src[_o]
        dst = dst[_o]
        edge_attr_128 = 5.93493e-05 + 1.00006 * jax.random.normal(jax.random.fold_in(_gk, 12), (25000, 128), jnp.float32)
        edge_attr_16 = 6.40344e-05 + 1.00026 * jax.random.normal(jax.random.fold_in(_gk, 13), (25000, 16), jnp.float32)
        edge_attr_4 = 0.000714719 + 1.00021 * jax.random.normal(jax.random.fold_in(_gk, 14), (25000, 4), jnp.float32)
        edge_type_5 = jax.random.randint(jax.random.fold_in(_gk, 16), (25000,), 0, 5, jnp.int32)
        node_vec1 = jax.random.uniform(jax.random.fold_in(_gk, 17), (50000, 1), jnp.float32, 0.0, 0.999994)
        return (x, src, dst, edge_attr_128, edge_attr_16, edge_attr_4, edge_type_5, node_vec1)
    x, src, dst, edge_attr_128, edge_attr_16, edge_attr_4, edge_type_5, node_vec1 = _rec_inputs()

    def _L0_gnn_setup():
        import jax, jax.numpy as jnp
        import numpy as np
        N = 50000
        E = 18750
        D = 128
        L = 4
        NEG_SLOPE = 0.2
        LN_EPS = 1e-05

        def _segment_softmax(logits, dst, num_segments):
            m = jax.ops.segment_max(logits, dst, num_segments=num_segments)
            m = jnp.where(jnp.isfinite(m), m, 0.0)
            ex = jnp.exp(logits - m[dst])
            denom = jax.ops.segment_sum(ex, dst, num_segments=num_segments)
            return ex / (denom[dst] + 1e-16)

        def _gat_layer(x, src, dst, ea, W, We, a_s, a_d, a_e, b, g, beta):
            h = x @ W
            e = ea @ We
            alpha = h @ a_s
            alpha = alpha[src] + (h @ a_d)[dst] + e @ a_e
            alpha = jax.nn.leaky_relu(alpha, NEG_SLOPE)
            alpha = _segment_softmax(alpha, dst, N)
            out = jax.ops.segment_sum(h[src] * alpha[:, None], dst, num_segments=N) + b
            mu = out.mean(-1, keepdims=True)
            var = ((out - mu) ** 2).mean(-1, keepdims=True)
            return (out - mu) * jax.lax.rsqrt(var + LN_EPS) * g + beta
        key = jax.random.key(seed)
        ks = jax.random.split(key, 12)
        inp = {'x': jax.random.normal(ks[0], (N, D), dtype=jnp.float32), 'edge_index': jax.random.randint(ks[1], (2, E), 0, N, dtype=jnp.int64), 'edge_attr': jax.random.normal(ks[2], (E, D), dtype=jnp.float32)}
        s = 1.0 / np.sqrt(D)
        inp['W'] = jax.random.normal(ks[3], (L, D, D), dtype=jnp.float32) * s
        inp['We'] = jax.random.normal(ks[4], (L, D, D), dtype=jnp.float32) * s
        inp['att_src'] = jax.random.normal(ks[5], (L, D), dtype=jnp.float32) * s
        inp['att_dst'] = jax.random.normal(ks[6], (L, D), dtype=jnp.float32) * s
        inp['att_edge'] = jax.random.normal(ks[7], (L, D), dtype=jnp.float32) * s
        inp['bias'] = jnp.zeros((L, D), dtype=jnp.float32)
        inp['ln_gamma'] = jnp.ones((L, D), dtype=jnp.float32)
        inp['ln_beta'] = jnp.zeros((L, D), dtype=jnp.float32)
        return inp
    _L0_gnn_all = _L0_gnn_setup()
    _L0_gnn_in = {k: v for k, v in _L0_gnn_all.items() if k in ('W', 'We', 'att_src', 'att_dst', 'att_edge', 'bias', 'ln_gamma', 'ln_beta')}
    del _L0_gnn_all

    def _L1_gnn_setup():
        import jax, jax.numpy as jnp
        import numpy as np
        N_NODES = 1250
        N_EDGES = 20000
        DIM = 128
        N_LAYERS = 3
        N_RELS = 5
        LN_EPS = 1e-05

        def _layer_norm(x, w, b):
            mu = jnp.mean(x, axis=-1, keepdims=True)
            var = jnp.mean((x - mu) ** 2, axis=-1, keepdims=True)
            return (x - mu) * jax.lax.rsqrt(var + LN_EPS) * w + b

        def _cell(h_in, relv, W, b, src, dst, rel, n_nodes):
            msg = jax.nn.relu(h_in[src] + relv[rel])
            s = jax.ops.segment_sum(msg, dst, num_segments=n_nodes)
            cnt = jax.ops.segment_sum(jnp.ones((src.shape[0],), msg.dtype), dst, num_segments=n_nodes)
            red = s / jnp.maximum(cnt, 1.0)[:, None]
            return red @ W.T + b
        key = jax.random.key(seed)
        ks = jax.random.split(key, 8)
        h = jax.random.normal(ks[0], (N_NODES, DIM), dtype=jnp.float32)
        edge_src = jax.random.randint(ks[1], (N_EDGES,), 0, N_NODES, dtype=jnp.int32)
        edge_dst = jax.random.randint(ks[2], (N_EDGES,), 0, N_NODES, dtype=jnp.int32)
        edge_rel = jax.random.randint(ks[3], (N_EDGES,), 0, N_RELS, dtype=jnp.int32)
        relvecs = jax.random.normal(ks[4], (N_LAYERS, N_RELS, DIM), dtype=jnp.float32)
        lin_w = jax.random.normal(ks[5], (N_LAYERS, DIM, DIM), dtype=jnp.float32) / np.sqrt(DIM)
        lin_b = jax.random.normal(ks[6], (N_LAYERS, DIM), dtype=jnp.float32) * 0.01
        ln_w = jnp.ones((N_LAYERS, DIM), dtype=jnp.float32)
        ln_b = jnp.zeros((N_LAYERS, DIM), dtype=jnp.float32)
        return {'h': h, 'edge_src': edge_src, 'edge_dst': edge_dst, 'edge_rel': edge_rel, 'relvecs': relvecs, 'lin_w': lin_w, 'lin_b': lin_b, 'ln_w': ln_w, 'ln_b': ln_b}
    _L1_gnn_all = _L1_gnn_setup()
    _L1_gnn_in = {k: v for k, v in _L1_gnn_all.items() if k in ('relvecs', 'lin_w', 'lin_b', 'ln_w', 'ln_b')}
    del _L1_gnn_all

    def _L2_gnn_setup():
        import jax, jax.numpy as jnp
        import numpy as np
        N_NODES = 3125
        N_EDGES = 50000
        D_IN = 128
        D_H = 128
        D_OUT = 128

        def _sage_conv(h, src, dst, Ws, Wn, b):
            n = h.shape[0]
            msg = h[src]
            summed = jax.ops.segment_sum(msg, dst, num_segments=n)
            deg = jax.ops.segment_sum(jnp.ones(src.shape, h.dtype), dst, num_segments=n)
            neigh = summed / jnp.maximum(deg, 1.0)[:, None]
            return h @ Ws.T + neigh @ Wn.T + b
        key = jax.random.key(seed)
        ks = jax.random.split(key, 12)
        x = jax.random.normal(ks[0], (N_NODES, D_IN), dtype=jnp.float32)
        src = jax.random.randint(ks[1], (N_EDGES,), 0, N_NODES, dtype=jnp.int32)
        dst = jax.random.randint(ks[2], (N_EDGES,), 0, N_NODES, dtype=jnp.int32)

        def lin(k, dout, din):
            s = 1.0 / np.sqrt(din)
            return jax.random.uniform(k, (dout, din), jnp.float32, -s, s)
        Ws0 = lin(ks[3], D_H, D_IN)
        Wn0 = lin(ks[4], D_H, D_IN)
        b0 = jnp.zeros((D_H,), jnp.float32)
        Ws1 = lin(ks[5], D_H, D_H)
        Wn1 = lin(ks[6], D_H, D_H)
        b1 = jnp.zeros((D_H,), jnp.float32)
        Ws2 = lin(ks[7], D_OUT, D_H)
        Wn2 = lin(ks[8], D_OUT, D_H)
        b2 = jnp.zeros((D_OUT,), jnp.float32)
        return {'x': x, 'Ws0': Ws0, 'Wn0': Wn0, 'b0': b0, 'Ws1': Ws1, 'Wn1': Wn1, 'b1': b1, 'Ws2': Ws2, 'Wn2': Wn2, 'b2': b2, 'src': src, 'dst': dst}
    _L2_gnn_all = _L2_gnn_setup()
    _L2_gnn_in = {k: v for k, v in _L2_gnn_all.items() if k in ('Ws0', 'Wn0', 'b0', 'Ws1', 'Wn1', 'b1', 'Ws2', 'Wn2', 'b2')}
    del _L2_gnn_all

    def _L3_gnn_setup():
        import jax, jax.numpy as jnp
        import numpy as np
        MUL = 32
        NUM_NEIGHBORS = 16
        INV_SQRT_MUL = 1.0 / np.sqrt(MUL).astype(np.float32)
        INV_SQRT_2MUL = 1.0 / np.sqrt(2 * MUL).astype(np.float32)
        INV_SQRT3 = 1.0 / np.sqrt(3.0).astype(np.float32)
        key = jax.random.key(seed)
        ks = jax.random.split(key, 20)
        N, E = (50000, 25000)
        inp = {'x': jax.random.normal(ks[0], (N, 128), jnp.float32), 'node_attr': jax.random.uniform(ks[1], (N, 1), jnp.float32), 'edge_attr': jax.random.normal(ks[2], (E, 4), jnp.float32), 'edge_len_emb': jax.random.normal(ks[3], (E, 16), jnp.float32), 'W_sc0': jax.random.normal(ks[4], (32, 32), jnp.float32), 'W_sc1': jax.random.normal(ks[5], (32, 32), jnp.float32), 'W_l10': jax.random.normal(ks[6], (32, 32), jnp.float32), 'W_l11': jax.random.normal(ks[7], (32, 32), jnp.float32), 'W_mlp1': jax.random.normal(ks[8], (16, 64), jnp.float32), 'W_mlp2': jax.random.normal(ks[9], (64, 128), jnp.float32), 'W_l2a': jax.random.normal(ks[10], (32, 32), jnp.float32), 'W_l2b': jax.random.normal(ks[11], (32, 32), jnp.float32), 'W_l2c': jax.random.normal(ks[12], (32, 32), jnp.float32), 'W_l2d': jax.random.normal(ks[13], (32, 32), jnp.float32), 'A0': jax.random.normal(ks[14], (32, 1), jnp.float32), 'A1': jax.random.normal(ks[15], (32, 1), jnp.float32), 'edge_index': jax.random.randint(ks[16], (2, E), 0, N, jnp.int64)}
        return inp
    _L3_gnn_all = _L3_gnn_setup()
    _L3_gnn_in = {k: v for k, v in _L3_gnn_all.items() if k in ('W_sc0', 'W_sc1', 'W_l10', 'W_l11', 'W_mlp1', 'W_mlp2', 'W_l2a', 'W_l2b', 'W_l2c', 'W_l2d', 'A0', 'A1')}
    del _L3_gnn_all
    return {'x': x, 'src': src, 'dst': dst, 'edge_attr_128': edge_attr_128, 'edge_attr_16': edge_attr_16, 'edge_attr_4': edge_attr_4, 'edge_type_5': edge_type_5, 'node_vec1': node_vec1, 'L0_gnn_W': _L0_gnn_in['W'], 'L0_gnn_We': _L0_gnn_in['We'], 'L0_gnn_att_src': _L0_gnn_in['att_src'], 'L0_gnn_att_dst': _L0_gnn_in['att_dst'], 'L0_gnn_att_edge': _L0_gnn_in['att_edge'], 'L0_gnn_bias': _L0_gnn_in['bias'], 'L0_gnn_ln_gamma': _L0_gnn_in['ln_gamma'], 'L0_gnn_ln_beta': _L0_gnn_in['ln_beta'], 'L1_gnn_relvecs': _L1_gnn_in['relvecs'], 'L1_gnn_lin_w': _L1_gnn_in['lin_w'], 'L1_gnn_lin_b': _L1_gnn_in['lin_b'], 'L1_gnn_ln_w': _L1_gnn_in['ln_w'], 'L1_gnn_ln_b': _L1_gnn_in['ln_b'], 'L2_gnn_Ws0': _L2_gnn_in['Ws0'], 'L2_gnn_Wn0': _L2_gnn_in['Wn0'], 'L2_gnn_b0': _L2_gnn_in['b0'], 'L2_gnn_Ws1': _L2_gnn_in['Ws1'], 'L2_gnn_Wn1': _L2_gnn_in['Wn1'], 'L2_gnn_b1': _L2_gnn_in['b1'], 'L2_gnn_Ws2': _L2_gnn_in['Ws2'], 'L2_gnn_Wn2': _L2_gnn_in['Wn2'], 'L2_gnn_b2': _L2_gnn_in['b2'], 'L3_gnn_W_sc0': _L3_gnn_in['W_sc0'], 'L3_gnn_W_sc1': _L3_gnn_in['W_sc1'], 'L3_gnn_W_l10': _L3_gnn_in['W_l10'], 'L3_gnn_W_l11': _L3_gnn_in['W_l11'], 'L3_gnn_W_mlp1': _L3_gnn_in['W_mlp1'], 'L3_gnn_W_mlp2': _L3_gnn_in['W_mlp2'], 'L3_gnn_W_l2a': _L3_gnn_in['W_l2a'], 'L3_gnn_W_l2b': _L3_gnn_in['W_l2b'], 'L3_gnn_W_l2c': _L3_gnn_in['W_l2c'], 'L3_gnn_W_l2d': _L3_gnn_in['W_l2d'], 'L3_gnn_A0': _L3_gnn_in['A0'], 'L3_gnn_A1': _L3_gnn_in['A1']}

def reference(x, src, dst, edge_attr_128, edge_attr_16, edge_attr_4, edge_type_5, node_vec1, L0_gnn_W, L0_gnn_We, L0_gnn_att_src, L0_gnn_att_dst, L0_gnn_att_edge, L0_gnn_bias, L0_gnn_ln_gamma, L0_gnn_ln_beta, L1_gnn_relvecs, L1_gnn_lin_w, L1_gnn_lin_b, L1_gnn_ln_w, L1_gnn_ln_b, L2_gnn_Ws0, L2_gnn_Wn0, L2_gnn_b0, L2_gnn_Ws1, L2_gnn_Wn1, L2_gnn_b1, L2_gnn_Ws2, L2_gnn_Wn2, L2_gnn_b2, L3_gnn_W_sc0, L3_gnn_W_sc1, L3_gnn_W_l10, L3_gnn_W_l11, L3_gnn_W_mlp1, L3_gnn_W_mlp2, L3_gnn_W_l2a, L3_gnn_W_l2b, L3_gnn_W_l2c, L3_gnn_W_l2d, L3_gnn_A0, L3_gnn_A1):
    import jax
    import jax.numpy as jnp

    def _L0_gnn_ref(x, edge_index, edge_attr, W, We, att_src, att_dst, att_edge, bias, ln_gamma, ln_beta):
        import jax, jax.numpy as jnp
        import numpy as np
        N = 50000
        E = 18750
        D = 128
        L = 4
        NEG_SLOPE = 0.2
        LN_EPS = 1e-05

        def _segment_softmax(logits, dst, num_segments):
            m = jax.ops.segment_max(logits, dst, num_segments=num_segments)
            m = jnp.where(jnp.isfinite(m), m, 0.0)
            ex = jnp.exp(logits - m[dst])
            denom = jax.ops.segment_sum(ex, dst, num_segments=num_segments)
            return ex / (denom[dst] + 1e-16)

        def _gat_layer(x, src, dst, ea, W, We, a_s, a_d, a_e, b, g, beta):
            h = x @ W
            e = ea @ We
            alpha = h @ a_s
            alpha = alpha[src] + (h @ a_d)[dst] + e @ a_e
            alpha = jax.nn.leaky_relu(alpha, NEG_SLOPE)
            alpha = _segment_softmax(alpha, dst, N)
            out = jax.ops.segment_sum(h[src] * alpha[:, None], dst, num_segments=N) + b
            mu = out.mean(-1, keepdims=True)
            var = ((out - mu) ** 2).mean(-1, keepdims=True)
            return (out - mu) * jax.lax.rsqrt(var + LN_EPS) * g + beta
        src, dst = (edge_index[0], edge_index[1])
        esum = jax.ops.segment_sum(edge_attr, dst, num_segments=N)
        cnt = jax.ops.segment_sum(jnp.ones((src.shape[0],), edge_attr.dtype), dst, num_segments=N)
        loop_attr = esum / jnp.maximum(cnt, 1.0)[:, None]
        loop = jnp.arange(N, dtype=src.dtype)
        src_f = jnp.concatenate([src, loop])
        dst_f = jnp.concatenate([dst, loop])
        ea_f = jnp.concatenate([edge_attr, loop_attr], axis=0)
        for l in range(L):
            x = _gat_layer(x, src_f, dst_f, ea_f, W[l], We[l], att_src[l], att_dst[l], att_edge[l], bias[l], ln_gamma[l], ln_beta[l])
        return x

    def _L1_gnn_ref(h, edge_src, edge_dst, edge_rel, relvecs, lin_w, lin_b, ln_w, ln_b):
        import jax, jax.numpy as jnp
        import numpy as np
        N_NODES = 1250
        N_EDGES = 20000
        DIM = 128
        N_LAYERS = 3
        N_RELS = 5
        LN_EPS = 1e-05

        def _layer_norm(x, w, b):
            mu = jnp.mean(x, axis=-1, keepdims=True)
            var = jnp.mean((x - mu) ** 2, axis=-1, keepdims=True)
            return (x - mu) * jax.lax.rsqrt(var + LN_EPS) * w + b

        def _cell(h_in, relv, W, b, src, dst, rel, n_nodes):
            msg = jax.nn.relu(h_in[src] + relv[rel])
            s = jax.ops.segment_sum(msg, dst, num_segments=n_nodes)
            cnt = jax.ops.segment_sum(jnp.ones((src.shape[0],), msg.dtype), dst, num_segments=n_nodes)
            red = s / jnp.maximum(cnt, 1.0)[:, None]
            return red @ W.T + b
        n = h.shape[0]
        h = _cell(h, relvecs[0], lin_w[0], lin_b[0], edge_src, edge_dst, edge_rel, n)
        for l in range(1, N_LAYERS):
            h_prev = h
            _h = jax.nn.relu(_layer_norm(h, ln_w[l - 1], ln_b[l - 1]))
            new_h = _cell(_h, relvecs[l], lin_w[l], lin_b[l], edge_src, edge_dst, edge_rel, n)
            h = h_prev + new_h
        h = _layer_norm(h, ln_w[-1], ln_b[-1])
        return h

    def _L2_gnn_ref(x, Ws0, Wn0, b0, Ws1, Wn1, b1, Ws2, Wn2, b2, src, dst):
        import jax, jax.numpy as jnp
        import numpy as np
        N_NODES = 3125
        N_EDGES = 50000
        D_IN = 128
        D_H = 128
        D_OUT = 128

        def _sage_conv(h, src, dst, Ws, Wn, b):
            n = h.shape[0]
            msg = h[src]
            summed = jax.ops.segment_sum(msg, dst, num_segments=n)
            deg = jax.ops.segment_sum(jnp.ones(src.shape, h.dtype), dst, num_segments=n)
            neigh = summed / jnp.maximum(deg, 1.0)[:, None]
            return h @ Ws.T + neigh @ Wn.T + b
        h = jax.nn.relu(_sage_conv(x, src, dst, Ws0, Wn0, b0))
        prev = h
        h = _sage_conv(h, src, dst, Ws1, Wn1, b1)
        h = jax.nn.relu(h + prev)
        return _sage_conv(h, src, dst, Ws2, Wn2, b2)

    def _L3_gnn_ref(x, node_attr, edge_attr, edge_len_emb, W_sc0, W_sc1, W_l10, W_l11, W_mlp1, W_mlp2, W_l2a, W_l2b, W_l2c, W_l2d, A0, A1, edge_index):
        import jax, jax.numpy as jnp
        import numpy as np
        MUL = 32
        NUM_NEIGHBORS = 16
        INV_SQRT_MUL = 1.0 / np.sqrt(MUL).astype(np.float32)
        INV_SQRT_2MUL = 1.0 / np.sqrt(2 * MUL).astype(np.float32)
        INV_SQRT3 = 1.0 / np.sqrt(3.0).astype(np.float32)
        N = x.shape[0]
        i, j = (edge_index[0], edge_index[1])
        x0 = x[:, :MUL]
        x1 = x[:, MUL:].reshape(N, MUL, 3)
        na = node_attr
        na3 = node_attr[:, :, None]
        sc0 = x0 @ W_sc0 * na * INV_SQRT_MUL
        sc1 = jnp.einsum('num,uv->nvm', x1, W_sc1) * na3 * INV_SQRT_MUL
        f0 = x0 @ W_l10 * na * INV_SQRT_MUL
        f1 = jnp.einsum('num,uv->nvm', x1, W_l11) * na3 * INV_SQRT_MUL
        h = jax.nn.silu(edge_len_emb @ W_mlp1 * (1.0 / 4.0))
        w = h @ W_mlp2 * (1.0 / 8.0)
        w0, w1, w2, w3 = (w[:, :32], w[:, 32:64], w[:, 64:96], w[:, 96:128])
        g0 = f0[i]
        g1 = f1[i]
        sh0 = edge_attr[:, :1]
        sh1 = edge_attr[:, 1:4]
        m0a = w0 * g0 * sh0
        m0b = w3 * (g1 * sh1[:, None, :]).sum(-1) * INV_SQRT3
        m1a = w1[:, :, None] * g0[:, :, None] * sh1[:, None, :]
        m1b = w2[:, :, None] * g1 * sh0[:, :, None]
        E = g0.shape[0]
        me = jnp.concatenate([m0a, m0b, m1a.reshape(E, 96), m1b.reshape(E, 96)], axis=-1)
        n = jax.ops.segment_sum(me, j, num_segments=N) * (1.0 / np.sqrt(NUM_NEIGHBORS))
        n0a, n0b = (n[:, :32], n[:, 32:64])
        n1a = n[:, 64:160].reshape(N, MUL, 3)
        n1b = n[:, 160:256].reshape(N, MUL, 3)
        out0 = (n0a @ W_l2a + n0b @ W_l2b) * na * INV_SQRT_2MUL
        out1 = (jnp.einsum('num,uv->nvm', n1a, W_l2c) + jnp.einsum('num,uv->nvm', n1b, W_l2d)) * na3 * INV_SQRT_2MUL
        alpha = (n0a @ A0 + n0b @ A1) * na * INV_SQRT_2MUL
        res0 = sc0 + alpha * out0
        res1 = sc1 + alpha[:, :, None] * out1
        return jnp.concatenate([res0, res1.reshape(N, 96)], axis=-1)
    edge_index = jnp.stack([src, dst])
    x = _layernorm(x + _L0_gnn_ref(x, edge_index, edge_attr_128, L0_gnn_W, L0_gnn_We, L0_gnn_att_src, L0_gnn_att_dst, L0_gnn_att_edge, L0_gnn_bias, L0_gnn_ln_gamma, L0_gnn_ln_beta), axis=-1)
    x = _layernorm(x + _L1_gnn_ref(x, src, dst, edge_type_5, L1_gnn_relvecs, L1_gnn_lin_w, L1_gnn_lin_b, L1_gnn_ln_w, L1_gnn_ln_b), axis=-1)
    x = _layernorm(x + _L2_gnn_ref(x, L2_gnn_Ws0, L2_gnn_Wn0, L2_gnn_b0, L2_gnn_Ws1, L2_gnn_Wn1, L2_gnn_b1, L2_gnn_Ws2, L2_gnn_Wn2, L2_gnn_b2, src, dst), axis=-1)
    x = _layernorm(x + _L3_gnn_ref(x, node_vec1, edge_attr_4, edge_attr_16, L3_gnn_W_sc0, L3_gnn_W_sc1, L3_gnn_W_l10, L3_gnn_W_l11, L3_gnn_W_mlp1, L3_gnn_W_mlp2, L3_gnn_W_l2a, L3_gnn_W_l2b, L3_gnn_W_l2c, L3_gnn_W_l2d, L3_gnn_A0, L3_gnn_A1, edge_index), axis=-1)
    return x

_drawn_inputs = setup_inputs


def setup_inputs(seed=0):
    import zlib

    import numpy as np

    out = dict(_drawn_inputs(seed))
    spreads = {'L0_gnn_bias': (0.0, 0.1),
     'L0_gnn_ln_gamma': (1.0, 0.2),
     'L0_gnn_ln_beta': (0.0, 0.1),
     'L1_gnn_ln_w': (1.0, 0.2),
     'L1_gnn_ln_b': (0.0, 0.1),
     'L2_gnn_b0': (0.0, 0.1),
     'L2_gnn_b1': (0.0, 0.1),
     'L2_gnn_b2': (0.0, 0.1)}
    factors = {'edge_attr_16': 8.0,
     'edge_attr_4': 8.0,
     'L3_gnn_W_l10': 8.0,
     'L3_gnn_W_l11': 8.0,
     'L3_gnn_W_mlp1': 8.0,
     'L3_gnn_W_mlp2': 8.0,
     'L3_gnn_W_l2a': 8.0,
     'L3_gnn_W_l2b': 8.0,
     'L3_gnn_W_l2c': 8.0,
     'L3_gnn_W_l2d': 8.0,
     'L3_gnn_A0': 8.0,
     'L3_gnn_A1': 8.0}
    for name, (base, spread) in spreads.items():
        noise = np.random.default_rng([zlib.crc32(name.encode()), seed]).standard_normal(out[name].shape)
        drawn = base * np.exp(spread * noise) if base else spread * noise
        out[name] = jnp.asarray(drawn.astype(out[name].dtype))
    for name, factor in factors.items():
        out[name] = (out[name] * factor).astype(out[name].dtype)
    return out
```

```python
from contextlib import ExitStack

import concourse.bass as bass
from concourse import mybir

F32 = mybir.dt.float32
BF16 = mybir.dt.bfloat16
I32 = mybir.dt.int32
U32 = mybir.dt.uint32
ALU = mybir.AluOpType
ACT = mybir.ActivationFunctionType
AX_X = mybir.AxisListType.X

P = 128
D = 128
KT = 4
BLOCK = P * KT
LN_EPS = 1e-5
NEG_SLOPE = 0.2
BIG = 1e30
SKIP = 1 << 20
AW = 130
REC = 32
R_DST, R_SRC, R_TYPE, R_SH, R_LEN, R_TE = 0, 1, 2, 4, 8, 24
MUL = 32


class Chain:

    def __init__(self, eng, sem, i, per):
        self.eng, self.sem, self.base, self.per, self.k = eng, sem, i * per, per, 0

    def mark(self, ins):
        self.k += 1
        ins.then_inc(self.sem, 1)
        return self.k

    def need(self, k):
        self.eng.wait_ge(self.sem, self.base + k)

    def run(self, ins):
        self.need(self.mark(ins))

    def close(self):
        assert self.k <= self.per, self.k
        if self.k < self.per:
            self.eng.sem_inc(self.sem, self.per - self.k)


class Pass:

    def __init__(self, nc, name):
        self.nc, self.name, self.ctx, self.owned = nc, name, ExitStack(), []

    def __enter__(self):
        return self

    def __exit__(self, *e):
        self.ctx.close()
        self.nc.clear_and_free_semaphores(self.owned)
        self.nc.all_engine_barrier()

    def sb(self, name, shape, dt=F32):
        return self.ctx.enter_context(self.nc.sbuf_tensor(f"{self.name}_{name}", shape, dt))

    def ps(self, name):
        return self.ctx.enter_context(self.nc.psum_tensor(f"{self.name}_{name}", [P, 512], F32))

    def sem(self, name):
        self.owned.append(self.nc.alloc_semaphore(f"{self.name}_{name}"))
        return self.owned[-1]

    def sems(self, name, n):
        return [self.sem(f"{name}{k}") for k in range(n)]

    def block(self):
        return self.ctx.enter_context(self.nc.Block())


def spread(ap, n):
    return ap.unsqueeze(1).to_broadcast([ap.shape[0], n, ap.shape[1]])


def fan(ap, n):
    return ap.unsqueeze(2).to_broadcast([ap.shape[0], ap.shape[1], n])


def backward(ap):
    (ps, pn), (fs, fn) = ap.ap
    return bass.AP(ap.tensor, ap.offset + fs * (fn - 1), [[ps, pn], [-fs, fn]])


class Kernel:
    def __init__(self, nc, a, out, N, E):
        self.nc, self.a, self.out = nc, a, out
        self.C = C = -(-E // BLOCK) * KT
        self.G = C // KT
        self.NBLK = -(-N // BLOCK)
        self.NP = self.NBLK * BLOCK
        self.NCOL = self.NBLK * KT
        self.HALF = C // 2
        assert self.NBLK % 2 == 0 and C % 2 == 0 and self.HALF <= P and self.G % 2 == 1

    def dram(self, name, shape, dt=F32):
        return self.nc.dram_tensor(name, shape, dt, kind="Internal").ap()

    def build(self):
        nc, C, NP, NCOL, HALF = self.nc, self.C, self.NP, self.NCOL, self.HALF
        self.table = self.dram("gat_table", (NP, AW))
        self.aux = self.dram("gat_aux", (NP, 2))
        self.agg = self.dram("aggregate", (NP, AW))
        self.pre = self.dram("edge_sums", (NP, 8))
        self.rec_d = self.dram("records", (C * P, REC))
        self.dst_d = self.dram("dst_sorted", (C * P + 2,))
        nodes = [self.dram(f"nodes_{n}", (NP, D)) for n in range(5)]
        with ExitStack() as ctx:
            def keep(name, shape, dt=F32):
                return ctx.enter_context(nc.sbuf_tensor(name, shape, dt))

            self.ident = keep("ident", [P, P])
            self.same = keep("same_run", [P, C * P], BF16)
            self.src_i = keep("src_i", [P, C], U32)
            self.dst_i = keep("dst_i", [P, C], U32)
            self.put_i = keep("put_i", [P, C], U32)
            self.te = keep("te", [P, 4, C])
            self.typ = keep("typ", [P, C])
            self.cont_row = keep("cont_row", [1, C])
            self.tmean = keep("tmean", [P, 4, NCOL])
            self.inv_cnt = keep("inv_cnt", [P, NCOL])
            self.no_edge = keep("no_edge", [P, NCOL])
            self.asad = keep("asad", [P, NCOL, 2])
            self.pen = keep("pen", [HALF, 2, 2, P])
            self.pen_carry = keep("pen_carry", [HALF, 2, 2, P])
            self.pen_row = keep("pen_row", [1, 2, C])
            self.mhalf = keep("mhalf", [P, KT])
            self.neg1 = keep("neg1", [P, KT])
            self.eps_t = keep("eps_t", [P, KT])

            self.records()
            self.order()
            self.graph()
            self.edge_pass("pre", "pre", None, None)
            self.counts()
            a, n = self.a, nodes
            self.node_pass("x0", "lin", a["x"], layer=0)
            for l in range(4):
                self.self_loops(l)
                self.attention(l)
                if l < 3:
                    self.node_pass(f"g{l + 1}", "gat", None, layer=l + 1)
            self.node_pass("g4", "gat_end", a["x"], layer=4, dst=n[0])
            self.edge_pass("r0", "rel", n[0], 0)
            self.node_pass("r0n", "rel0", None, layer=0, dst=n[1], dst2=n[2])
            self.edge_pass("r1", "rel", n[2], 1)
            self.node_pass("r1n", "rel1", n[1], layer=1, dst=n[3], dst2=n[2])
            self.edge_pass("r2", "rel", n[2], 2)
            self.node_pass("r2n", "rel2", n[3], layer=2, dst=n[1], extra=n[0])
            self.edge_pass("s0", "sage", n[1], 0)
            self.node_pass("s0n", "sage0", n[1], layer=0, dst=n[2])
            self.edge_pass("s1", "sage", n[2], 1)
            self.node_pass("s1n", "sage1", n[2], layer=1, dst=n[3])
            self.edge_pass("s2", "sage", n[3], 2)
            self.node_pass("s2n", "sage2", n[3], layer=2, dst=n[0], dst2=n[2], extra=n[1])
            self.edge_pass("tp", "tp", n[2], 0)
            self.node_pass("fin", "fin", n[0], layer=0, dst=self.out)

    def records(self):
        a, C, G, NP, agg, pre, rec_d, ident = self.a, self.C, self.G, self.NP, self.agg, self.pre, self.rec_d, self.ident
        with Pass(self.nc, "rec") as q:
            zn = 14 * KT
            zero = q.sb("zero", [P, zn * AW])
            rec = q.sb("rec", [P, C, REC])
            raw = q.sb("raw", [P, 3, C], I32)
            len16 = q.sb("len16", [P, C, 16])
            sh4 = q.sb("sh4", [P, C, 4])
            ea = q.sb("ea", [P, 2, KT, D])
            junk = q.sb("junk", [P, 2, 4 * KT, D])
            dots = q.sb("dots", [P, 2, KT, 4])
            wet = q.sb("wet", [P, 4, D])
            we = q.sb("we", [P, 4, D])
            att = q.sb("att", [P, 4])
            attb = q.sb("attb", [P, 4, P])
            vte = q.sb("vte", [P, 4, D])
            pst, psv = q.ps("we_t"), q.ps("vte_p")
            ld, zs, zst, eld = q.sem("loaded"), q.sem("zeroed"), q.sem("zero_stored"), q.sems("edges_in", 2)
            idr, wt, wts = q.sem("ident_ready"), q.sem("we_turned"), q.sem("we_kept")
            vr, vs, used = q.sem("vte_made"), q.sem("vte_kept"), q.sem("edges_used")
            ch, recr, rst, ar, rz = q.sem("dve_steps"), q.sem("rec_ready"), q.sem("rec_stored"), q.sem("att_spread"), q.sem("rec_zeroed")
            block = q.block()
            e_v = a["edge_attr_128"].rearrange("(g k p) d -> g p k d", k=KT, p=P)

            @block.sync
            def _(sp):
                for n, name in enumerate(("dst", "src", "edge_type_5")):
                    sp.dma_start(raw[:, n, :], a[name]).then_inc(ld, 16)
                sp.dma_start(len16[:, :, :], a["edge_attr_16"]).then_inc(ld, 16)
                sp.dma_start(sh4[:, :, :], a["edge_attr_4"]).then_inc(ld, 16)
                sp.dma_start(we[:, :, :], a["L0_gnn_We"].rearrange("l i j -> i l j")).then_inc(ld, 16)
                sp.dma_start(att[:, :], a["L0_gnn_att_edge"]).then_inc(ld, 16)
                for g in range(2):
                    sp.dma_start(ea[:, g, :, :], e_v[g]).then_inc(eld[g], 16)
                with sp.Fori(0, (G - 3) // 2) as i:
                    for j in range(2):
                        sp.wait_ge(used, i * 2 + j + 1)
                        sp.dma_start(ea[:, j, :, :], e_v[bass.ds(i * 2 + 2 + j, 1)].rearrange("g p k d -> (g p) k d")).then_inc(eld[j], 16)
                sp.wait_ge(used, G - 2)
                sp.dma_start(ea[:, 0, :, :], e_v[G - 1]).then_inc(eld[0], 16)
                sp.wait_ge(recr, 1)
                sp.dma_start(rec_d.rearrange("(c p) w -> p c w", p=P), rec[:, :, :]).then_inc(rst, 16)
                sp.wait_ge(rst, 16)

            @block.scalar
            def _(act):
                act.wait_ge(zs, 1)
                z_v = agg.rearrange("(r p n) w -> r p (n w)", p=P, n=zn)
                for r in range(NP // P // zn):
                    act.dma_start(z_v[r], zero[:, :]).then_inc(zst, 16)
                act.dma_start(pre.rearrange("(p n) w -> p (n w)", p=P), zero[:, 0:NP // P * 8]).then_inc(zst, 16)
                act.wait_ge(wt, 1)
                act.activation(wet[:, :, :].rearrange("p l d -> p (l d)"), pst[:, :], ACT.Copy).then_inc(wts, 1)
                act.wait_ge(vr, 1)
                act.activation(vte[:, :, :].rearrange("p l d -> p (l d)"), psv[:, :], ACT.Copy).then_inc(vs, 1)
                act.wait_ge(zst, 16 * (NP // P // zn + 1))

            @block.gpsimd
            def _(pool):
                pool.memset(ident[:, :], 0.0).then_inc(idr, 1)
                pool.wait_ge(idr, 1)
                pool.affine_select(out=ident[:, :], in_=ident[:, :], compare_op=ALU.not_equal, fill=1.0,
                                   base=0, pattern=[[-1, P]], channel_multiplier=1).then_inc(idr, 1)
                pool.memset(self.mhalf[:, :], -0.5)
                pool.memset(self.neg1[:, :], -1.0)
                pool.memset(self.eps_t[:, :], LN_EPS)

            @block.tensor
            def _(pe):
                pe.wait_ge(idr, 2)
                pe.wait_ge(ld, 16 * 7)
                for l in range(4):
                    mm = pe.transpose(pst[:, l * D:(l + 1) * D], we[:, l, :], ident[:, :])
                mm.then_inc(wt, 1)
                pe.wait_ge(wts, 1)
                pe.wait_ge(ar, 1)
                for l in range(4):
                    mm = pe.matmul(psv[:, l * D:(l + 1) * D], attb[:, l, :], wet[:, l, :], start=True, stop=True)
                mm.then_inc(vr, 1)

            @block.vector
            def _(v):
                v.memset(zero[:, :], 0.0).then_inc(zs, 1)
                v.memset(rec[:, :, :], 0.0).then_inc(rz, 1)
                v.wait_ge(ld, 16 * 7)
                v.tensor_copy(attb[:, :, :], fan(att[:, :], P)).then_inc(ar, 1)
                v.wait_ge(rz, 1)
                for n, r in enumerate((R_DST, R_SRC, R_TYPE)):
                    v.tensor_copy(rec[:, :, r], raw[:, n, :])
                v.tensor_copy(rec[:, :, R_SH:R_SH + 4], sh4[:, :, :])
                v.tensor_copy(rec[:, :, R_LEN:R_LEN + 16], len16[:, :, :])
                v.wait_ge(vs, 1)

                def group(g, j, n, st):
                    v.wait_ge(eld[j], n)
                    if not isinstance(g, int) or g >= 2:
                        v.wait_ge(used, g - 1)
                    for k in range(KT):
                        for l in range(4):
                            m = st.mark(v.tensor_tensor_reduce(junk[:, j, 4 * k + l, :], ea[:, j, k, :], vte[:, l, :], 1.0, 0.0,
                                                               ALU.mult, ALU.add, dots[:, j, k, l:l + 1]))
                    st.need(m)
                    v.tensor_copy(rec[:, bass.ds(g * KT, KT), R_TE:R_TE + 4], dots[:, j]).then_inc(used, 1)

                def pair(i):
                    st = Chain(v, ch, i, 8 * KT)
                    for j in range(2):
                        group(i * 2 + j, j, (i + 1) * 16, st)
                    st.close()

                pair(0)
                with v.Fori(1, (G - 1) // 2) as i:
                    pair(i)
                group(G - 1, 0, ((G - 1) // 2 + 1) * 16, Chain(v, ch, (G - 1) // 2, 8 * KT))
                v.wait_ge(used, G)
                v.drain().then_inc(recr, 1)

    def order(self):
        a, C, G, ident, rec_d = self.a, self.C, self.G, self.ident, self.rec_d
        moved = self.dram("records_moved", (C * P, REC))
        with Pass(self.nc, "order") as q:
            pair_i = q.sb("pair_i", [P, 2, C], I32)
            pair = q.sb("pair", [P, 3, C])
            drops = q.sb("drops", [P, 1])
            ones = q.sb("ones", [P, 1])
            flag = q.sb("flag", [1, 1], I32)
            own_i = q.sb("own_i", [P, C], I32)
            own = q.sb("own", [P, C])
            number = q.sb("number", [P, C])
            rank = q.sb("rank", [P, C])
            rank_i = q.sb("rank_i", [P, C], U32)
            local = q.sb("local", [P, BLOCK])
            row_i = q.sb("row_i", [P, BLOCK], I32)
            row = q.sb("row", [P, BLOCK])
            before = q.sb("before", [P, BLOCK])
            hit = q.sb("hit", [P, 2, BLOCK])
            got = q.sb("got", [P, 1])
            rec = q.sb("rec", [P, REC])
            ix = q.sb("ix", [P, 1], U32)
            pd = q.ps("drops_sum")
            ld, on, io, dr, dm, fl = (q.sem(n) for n in ("loaded", "ones_ready", "numbers_ready", "drops_ready", "drops_summed", "flag_ready"))
            row_in, row_used, ch, ixr, rec_in, put, gate, mvd, num, vgate = (q.sem(n) for n in ("row_in", "row_used", "steps", "index_ready", "record_in",
                                                                                   "record_put", "gate", "records_moved", "numbers_less", "vector_gate"))
            block = q.block()

            @block.sync
            def _(sp):
                for o in range(2):
                    sp.dma_start(pair_i[:, o, :], a["dst_rows"][o:o + C * P].rearrange("(p c) -> p c", c=C)).then_inc(ld, 16)
                sp.dma_start(own_i[:, :], a["dst"]).then_inc(ld, 16)
                sp.wait_ge(fl, 1)
                unordered = sp.value_load(flag[0:1, 0:1], min_val=0, max_val=1)
                with sp.If(unordered > 0):
                    with sp.Fori(0, G) as g:
                        sp.wait_ge(row_used, g + 1)
                        sp.dma_start(row_i[:, :], a["dst_rows"][bass.ds(g * BLOCK, BLOCK)].partition_broadcast(P)).then_inc(row_in, 16)

                    def bring(c):
                        sp.wait_ge(put, c * 16)
                        sp.dma_start(rec[:, :], rec_d[bass.ds(c * P, P), :]).then_inc(rec_in, 16)

                    bring(0)
                    with sp.Fori(1, C) as c:
                        bring(c)
                    sp.wait_ge(put, C * 16)
                    sp.dma_start(rec_d.rearrange("(n p) w -> p n w", p=P), moved.rearrange("(n p) w -> p n w", p=P)).then_inc(mvd, 16)
                    sp.wait_ge(mvd, 16)

            @block.gpsimd
            def _(pool):
                pool.memset(ones[:, :], 1.0).then_inc(on, 1)
                pool.iota(number[:, :], [[P, C]], base=0, channel_multiplier=1, allow_small_or_imprecise_dtypes=True).then_inc(io, 1)
                pool.iota(local[:, :], [[1, BLOCK]], base=0, channel_multiplier=0, allow_small_or_imprecise_dtypes=True).then_inc(io, 1)
                bound = pool.to_reg(C * P - 1)
                pool.wait_ge(fl, 1)
                unordered = pool.value_load(flag[0:1, 0:1], min_val=0, max_val=1)
                with pool.If(unordered > 0):
                    with pool.Fori(0, C) as c:
                        pool.wait_ge(ixr, c + 1)
                        pool.sem_inc(gate, 1)
                        pool.wait_ge(rec_in, c * 16 + 16)
                        pool.sem_inc(gate, 1)
                        pool.indirect_dma_start(moved, bass.IndirectOffsetOnAxis(ix[:, 0:1], 0), rec[:, :], None,
                                                bounds_check=bound, oob_is_err=False).then_inc(put, 16)

            @block.tensor
            def _(pe):
                pe.wait_ge(on, 1)
                pe.wait_ge(dr, 1)
                pe.matmul(pd[0:1, 0:1], drops[:, :], ones[:, :], start=True, stop=True).then_inc(dm, 1)

            @block.vector
            def _(v):
                v.wait_ge(ld, 48)
                st = Chain(v, ch, 0, 10)
                v.tensor_copy(own[:, :], own_i[:, :])
                st.run(v.tensor_copy(pair[:, 0:2, :], pair_i[:, :, :]))
                st.run(v.tensor_tensor(pair[:, 2, :], pair[:, 0, :], pair[:, 1, :], ALU.is_gt))
                v.tensor_reduce(drops[:, :], pair[:, 2, :], AX_X, ALU.max).then_inc(dr, 1)
                v.wait_ge(dm, 1)
                v.wait_ge(io, 2)
                st.run(v.tensor_scalar(drops[0:1, :], pd[0:1, 0:1], 1.0, None, ALU.min))
                v.tensor_copy(flag[:, :], drops[0:1, :]).then_inc(fl, 1)
                st.run(v.memset(rank[:, :], 0.0))
                v.wait_ge(fl, 1)
                st.close()
                v.wait_ge(ch, 10)
                unordered = v.value_load(flag[0:1, 0:1], min_val=0, max_val=1)
                with v.If(unordered > 0):
                    v.sem_inc(row_used, 1)
                    with v.Fori(0, G) as g:
                        v.wait_ge(row_in, g * 16 + 16)
                        v.tensor_copy(row[:, :], row_i[:, :]).then_inc(row_used, 1)
                        v.wait_ge(row_used, g + 2)
                        v.sem_inc(vgate, 1)
                        with v.Fori(0, C) as c:
                            st = Chain(v, ch, g * C + c, 5)
                            st.base = st.base + 10
                            d_, n_, r_ = own[:, bass.ds(c, 1)], number[:, bass.ds(c, 1)], rank[:, bass.ds(c, 1)]
                            st.run(v.tensor_scalar(before[:, :], local[:, :], n_, None, ALU.is_lt))
                            st.mark(v.scalar_tensor_tensor(hit[:, 0, :], row[:, :], d_, before[:, :], ALU.is_equal, ALU.mult))
                            st.run(v.tensor_scalar(hit[:, 1, :], row[:, :], d_, None, ALU.is_lt))
                            st.run(v.tensor_reduce(got[:, :], hit[:, :, :].rearrange("p a n -> p (a n)"), AX_X, ALU.add))
                            st.run(v.tensor_tensor(r_, r_, got[:, :], ALU.add))
                        v.tensor_scalar(number[:, :], number[:, :], float(-BLOCK), None, ALU.add).then_inc(num, 1)
                        v.wait_ge(num, g + 1)
                    v.tensor_copy(rank_i[:, :], rank[:, :]).then_inc(fl, 1)
                    v.wait_ge(fl, 2)

                    def index(c):
                        v.wait_ge(put, c * 16)
                        v.tensor_copy(ix[:, :], rank_i[:, bass.ds(c, 1)]).then_inc(ixr, 1)

                    index(0)
                    with v.Fori(1, C) as c:
                        index(c)

    def graph(self):
        C, G, HALF, ident, rec_d, dst_d = self.C, self.G, self.HALF, self.ident, self.rec_d, self.dst_d
        with Pass(self.nc, "graph") as q:
            rec = q.sb("rec", [P, C, REC])
            dcol = q.sb("dcol", [P, C])
            drow = q.sb("drow", [HALF, 3, 2, P])
            flag = q.sb("flag", [HALF, 3, 2])
            edge_row = q.sb("edge_row", [1, 4, C])
            row_f = q.sb("row_f", [1, 3, C])
            put_r = q.sb("put_r", [HALF, 2, P])
            sent = q.sb("sent", [1, 1])
            wide = q.sb("wide", [P, 2, KT * P])
            psr, psc = q.ps("rows"), q.ps("cols")
            ld, rt, rk, dst_st, dl, el = q.sem("loaded"), q.sem("rows_turned"), q.sem("rows_kept"), q.sem("dst_stored"), q.sem("neighbours_in"), q.sem("edge_row_in")
            dc, pr, pt, wl, wu, sr, ch = q.sem("dcol_ready"), q.sem("put_ready"), q.sem("put_turned"), q.sems("wide_in", 2), q.sem("wide_used"), q.sem("sent_ready"), q.sem("steps")
            block = q.block()
            body = dst_d[1:1 + C * P]

            def shifted(o):
                return dst_d[o:o + C * P].rearrange("(g r p) -> r g p", g=2, p=P)

            @block.sync
            def _(sp):
                sp.dma_start(rec[:, :, :], rec_d.rearrange("(c p) w -> p c w", p=P)).then_inc(ld, 16)
                sp.wait_ge(rk, 1)
                sp.wait_ge(sr, 1)
                sp.dma_start(shifted(1), drow[:, 1, :, :]).then_inc(dst_st, 16)
                for o in (0, C * P + 1):
                    sp.dma_start(dst_d[o:o + 1].unsqueeze(0), sent[:, :]).then_inc(dst_st, 16)
                sp.wait_ge(dst_st, 48)
                for o in (0, 2):
                    sp.dma_start(drow[:, o, :, :], shifted(o)).then_inc(dl, 16)
                for n, o in enumerate((0, 1, P, P + 1)):
                    last = dst_d[o:o + (C - 1) * P + 1:P].unsqueeze(0)
                    sp.dma_start(edge_row[:, n, :].unsqueeze(2), last.unsqueeze(2), allow_slow_non_contiguous=True).then_inc(el, 16)
                for j in range(2):
                    sp.dma_start(wide[:, j, :], body[j * BLOCK:(j + 1) * BLOCK].partition_broadcast(P)).then_inc(wl[j], 16)
                with sp.Fori(0, (G - 3) // 2) as i:
                    for j in range(2):
                        sp.wait_ge(wu, i * 2 + j + 1)
                        sp.dma_start(wide[:, j, :], body[bass.ds((i * 2 + 2 + j) * BLOCK, BLOCK)].partition_broadcast(P)).then_inc(wl[j], 16)
                sp.wait_ge(wu, G - 2)
                sp.dma_start(wide[:, 0, :], body[(G - 1) * BLOCK:].partition_broadcast(P)).then_inc(wl[0], 16)

            @block.tensor
            def _(pe):
                pe.wait_ge(dc, 1)
                for g in range(2):
                    mm = pe.transpose(psr[0:HALF, g * P:(g + 1) * P], dcol[:, g * HALF:(g + 1) * HALF], ident[:, :])
                mm.then_inc(rt, 1)
                pe.wait_ge(pr, 1)
                for g in range(2):
                    mm = pe.transpose(psc[:, g * HALF:(g + 1) * HALF], put_r[:, g, :], ident[0:HALF, 0:HALF])
                mm.then_inc(pt, 1)

            @block.vector
            def _(v):
                st = Chain(v, ch, 0, 100)
                v.memset(sent[:, :], -1.0).then_inc(sr, 1)
                v.wait_ge(ld, 16)
                v.tensor_copy(dcol[:, :], rec[:, :, R_DST]).then_inc(dc, 1)
                v.tensor_copy(self.dst_i[:, :], rec[:, :, R_DST])
                v.tensor_copy(self.src_i[:, :], rec[:, :, R_SRC])
                v.tensor_copy(self.typ[:, :], rec[:, :, R_TYPE])
                v.tensor_copy(self.te[:, :, :], rec[:, :, R_TE:R_TE + 4].rearrange("p c l -> p l c"))
                v.wait_ge(rt, 1)
                v.tensor_copy(drow[:, 1, :, :].rearrange("r g p -> r (g p)"), psr[0:HALF, 0:2 * P]).then_inc(rk, 1)
                v.wait_ge(rk, 1)
                v.wait_ge(dl, 32)
                v.wait_ge(el, 64)
                st.run(v.tensor_tensor(put_r[:, :, :], drow[:, 1], drow[:, 2], ALU.is_equal))
                st.run(v.scalar_tensor_tensor(put_r[:, :, :].rearrange("r g p -> r (g p)"), put_r[:, :, :].rearrange("r g p -> r (g p)"),
                                              float(SKIP), drow[:, 1].rearrange("r g p -> r (g p)"), ALU.mult, ALU.add))
                v.sem_inc(pr, 1)
                for d, o in ((0, 0), (1, 2)):
                    st.run(v.tensor_tensor(self.pen[:, d], drow[:, 1], drow[:, o], ALU.is_equal))
                    st.run(v.tensor_tensor(flag[:, d, :].unsqueeze(2), drow[:, 1, :, (0, P - 1)[d]].unsqueeze(2),
                                           drow[:, o, :, (0, P - 1)[d]].unsqueeze(2), ALU.is_equal))
                    for g in range(2):
                        e = (0, P - 1)[d]
                        st.run(v.tensor_scalar(self.pen_carry[:, d, g, :], drow[:, 1, g, :], drow[:, 1, g, e:e + 1],
                                               flag[:, d, g:g + 1], ALU.is_equal, ALU.mult))
                    for t in (self.pen, self.pen_carry):
                        st.run(v.tensor_scalar(t[:, d], t[:, d], -1.0, BIG, ALU.add, ALU.mult))
                for n, (x, y) in enumerate(((0, 1), (3, 2), (1, 2))):
                    st.run(v.tensor_tensor(row_f[:, n, :], edge_row[:, x, :], edge_row[:, y, :], ALU.is_equal))
                st.run(v.tensor_copy(self.cont_row[:, :], row_f[:, 0, :]))
                for d in range(2):
                    st.run(v.tensor_tensor(self.pen_row[:, d, :], row_f[:, d, :], row_f[:, 2, :], ALU.mult))
                    st.run(v.tensor_scalar(self.pen_row[:, d, :], self.pen_row[:, d, :], -1.0, BIG, ALU.add, ALU.mult))
                v.wait_ge(pt, 1)
                v.tensor_copy(self.put_i[:, :], psc[:, 0:C])

                def group(g, j, n):
                    v.wait_ge(wl[j], n)
                    for k in range(KT):
                        last = v.tensor_scalar(self.same[:, bass.ds((g * KT + k) * P, P)], wide[:, j, k * P:(k + 1) * P],
                                               dcol[:, bass.ds(g * KT + k, 1)], None, ALU.is_equal)
                    last.then_inc(wu, 1)

                with v.Fori(0, (G - 1) // 2) as i:
                    for j in range(2):
                        group(i * 2 + j, j, (i + 1) * 16)
                group(G - 1, 0, ((G - 1) // 2 + 1) * 16)

    def counts(self):
        NCOL = self.NCOL
        with Pass(self.nc, "cnt") as q:
            s = q.sb("s", [P, NCOL, 8])
            c1 = q.sb("c1", [P, NCOL])
            ld, ch = q.sem("loaded"), q.sem("steps")
            block = q.block()

            @block.sync
            def _(sp):
                sp.dma_start(s[:, :, :].rearrange("p (b k) w -> p b (k w)", k=KT),
                             self.pre.rearrange("(b p k) w -> p b (k w)", p=P, k=KT)).then_inc(ld, 16)

            @block.vector
            def _(v):
                st = Chain(v, ch, 0, 100)
                v.wait_ge(ld, 16)
                st.run(v.tensor_scalar(self.no_edge[:, :], s[:, :, 4], 0.0, None, ALU.is_equal))
                st.run(v.tensor_scalar(c1[:, :], s[:, :, 4], 1.0, None, ALU.max))
                st.run(v.reciprocal(self.inv_cnt[:, :], c1[:, :]))
                for l in range(4):
                    st.run(v.tensor_tensor(self.tmean[:, l, :], s[:, :, l], self.inv_cnt[:, :], ALU.mult))

    def self_loops(self, l):
        NCOL = self.NCOL
        with Pass(self.nc, f"loop{l}") as q:
            t = q.sb("t", [P, NCOL])
            au = q.sb("au", [P, NCOL, 2])
            ch, st_ = q.sem("steps"), q.sem("stored")
            block = q.block()

            @block.vector
            def _(v):
                st = Chain(v, ch, 0, 4)
                v.tensor_copy(au[:, :, 0], self.asad[:, :, 1])
                st.run(v.tensor_tensor(t[:, :], self.asad[:, :, 0], self.asad[:, :, 1], ALU.add))
                st.run(v.tensor_tensor(t[:, :], t[:, :], self.tmean[:, l, :], ALU.add))
                st.run(v.scalar_tensor_tensor(au[:, :, 1], t[:, :], NEG_SLOPE, t[:, :], ALU.mult, ALU.max))
                v.drain().then_inc(ch, 1)

            @block.sync
            def _(sp):
                sp.wait_ge(ch, 4)
                sp.dma_start(self.aux.rearrange("(b p k) w -> p b (k w)", p=P, k=KT),
                             au[:, :, :].rearrange("p (b k) w -> p b (k w)", k=KT)).then_inc(st_, 16)
                sp.wait_ge(st_, 16)

    def attention(self, l):
        C, G, HALF, ident = self.C, self.G, self.HALF, self.ident
        with Pass(self.nc, f"att{l}") as q:
            H = q.sb("H", [P, C, AW])
            auxE = q.sb("auxE", [P, C, 2])
            lg = q.sb("lg", [P, C])
            cand = q.sb("cand", [P, C])
            pw = q.sb("pw", [P, C])
            pl = q.sb("pl", [P, C])
            with Pass(self.nc, f"gather{l}") as g_:
                hr = g_.sb("hr", [P, KT, AW])
                ar = g_.sb("ar", [P, KT, 2])
                ix = g_.sb("ix", [P, KT, 2], U32)
                gh, ga = g_.sems("h_in", KT), g_.sems("aux_in", KT)
                ixr, hk, ak, gate = g_.sem("index_ready"), g_.sem("h_kept"), g_.sem("aux_kept"), g_.sem("gate")
                block = g_.block()

                @block.gpsimd
                def _(pool):
                    bound = pool.to_reg(self.NP - 1)
                    def body(i):
                        for k in range(KT):
                            pool.wait_ge(ixr, i * KT + k + 1)
                            pool.sem_inc(gate, 1)
                            pool.wait_ge(hk, i * KT + k)
                            pool.sem_inc(gate, 1)
                            pool.wait_ge(ak, i * KT + k)
                            pool.sem_inc(gate, 1)
                            pool.indirect_dma_start(hr[:, k, :], None, self.table, bass.IndirectOffsetOnAxis(ix[:, k, 0:1], 0),
                                                    bounds_check=bound, oob_is_err=False).then_inc(gh[k], 16)
                            pool.indirect_dma_start(ar[:, k, :], None, self.aux, bass.IndirectOffsetOnAxis(ix[:, k, 1:2], 0),
                                                    bounds_check=bound, oob_is_err=False).then_inc(ga[k], 16)

                    body(0)
                    with pool.Fori(1, G) as i:
                        body(i)

                @block.scalar
                def _(act):
                    act.sem_inc(hk, KT - 1)
                    with act.Fori(0, G) as i:
                        for k in range(KT):
                            act.wait_ge(gh[k], i * 16 + 16)
                            act.activation(H[:, bass.ds(i * KT + k, 1), :], hr[:, k:k + 1, :], ACT.Copy).then_inc(hk, 1)

                @block.vector
                def _(v):
                    def index(c, k):
                        v.tensor_copy(ix[:, k, 0:1], self.src_i[:, bass.ds(c, 1)])
                        v.tensor_copy(ix[:, k, 1:2], self.dst_i[:, bass.ds(c, 1)]).then_inc(ixr, 1)

                    def body(i, last):
                        for k in range(KT):
                            v.wait_ge(ga[k], i * 16 + 16)
                            v.wait_ge(gh[k], i * 16 + 16)
                            if not last:
                                index(i * KT + KT + k, k)
                            v.tensor_copy(auxE[:, bass.ds(i * KT + k, 1), :], ar[:, k:k + 1, :]).then_inc(ak, 1)

                    v.sem_inc(ak, KT - 1)
                    for k in range(KT):
                        index(k, k)
                    with v.Fori(0, G - 1) as i:
                        body(i, False)
                    body(G - 1, True)

            with Pass(self.nc, f"soft{l}") as s_:
                lt = s_.sb("lt", [HALF, 2, P])
                F = s_.sb("F", [HALF, 2, 2, P])
                ends = s_.sb("ends", [HALF, 4])
                erow = s_.sb("erow", [1, 2, C])
                crow = s_.sb("crow", [1, 2, C + 2])
                ccol = s_.sb("ccol", [HALF, 4])
                one = s_.sb("one", [1, 2])
                psa, psb, psc, psd = (s_.ps(n) for n in ("a", "b", "c", "d"))
                ch, pe_s, ex, dn = s_.sem("steps"), s_.sem("turned"), s_.sem("exps"), s_.sem("weights_shifted")
                block = s_.block()

                @block.vector
                def _(v):
                    st = Chain(v, ch, 0, 100)
                    v.memset(one[:, :], 1.0)
                    v.memset(crow[:, :, :], -BIG)
                    st.run(v.tensor_tensor(lg[:, :], H[:, :, D], auxE[:, :, 0], ALU.add))
                    st.run(v.tensor_tensor(lg[:, :], lg[:, :], self.te[:, l, :], ALU.add))
                    st.run(v.scalar_tensor_tensor(lg[:, :], lg[:, :], NEG_SLOPE, lg[:, :], ALU.mult, ALU.max))
                    st.run(v.tensor_tensor(cand[:, :], lg[:, :], auxE[:, :, 1], ALU.max))
                    v.memset(H[:, :, D:D + 1], 1.0)
                    v.wait_ge(pe_s, 1)
                    st.run(v.tensor_copy(lt[:, :, :].rearrange("r g p -> r (g p)"), psa[0:HALF, 0:2 * P]))
                    for g in range(2):
                        v.tensor_tensor_scan(F[:, 0, g, :], self.pen[:, 0, g, :], lt[:, g, :], -BIG, ALU.add, ALU.max)
                        st.run(v.tensor_tensor_scan(backward(F[:, 1, g, :]), backward(self.pen[:, 1, g, :]), backward(lt[:, g, :]),
                                                    -BIG, ALU.add, ALU.max))
                    st.run(v.tensor_copy(ends[:, 0:2], F[:, 0, :, P - 1]))
                    st.run(v.tensor_copy(ends[:, 2:4], F[:, 1, :, 0]))
                    v.wait_ge(pe_s, 2)
                    st.run(v.tensor_copy(erow[:, :, :].rearrange("o d c -> o (d c)"), psb[0:1, 0:2 * C]))
                    v.tensor_tensor_scan(crow[:, 0, 1:C + 1], self.pen_row[:, 0, :], erow[:, 0, :], -BIG, ALU.add, ALU.max)
                    st.run(v.tensor_tensor_scan(backward(crow[:, 1, 0:C]), backward(self.pen_row[:, 1, :]), backward(erow[:, 1, :]),
                                                -BIG, ALU.add, ALU.max))
                    v.wait_ge(pe_s, 3)
                    st.run(v.tensor_copy(ccol[:, :], psc[0:HALF, 0:4]))
                    for d in range(2):
                        for g in range(2):
                            st.run(v.scalar_tensor_tensor(F[:, d, g, :], self.pen_carry[:, d, g, :], ccol[:, 2 * d + g:2 * d + g + 1],
                                                          F[:, d, g, :], ALU.add, ALU.max))
                    st.run(v.tensor_tensor(lt[:, :, :], F[:, 0], F[:, 1], ALU.max))
                    v.wait_ge(pe_s, 4)
                    v.tensor_tensor(pw[:, :], lg[:, :], psd[:, 0:C], ALU.subtract)
                    v.tensor_tensor(pl[:, :], auxE[:, :, 1], psd[:, 0:C], ALU.subtract).then_inc(dn, 1)

                @block.tensor
                def _(pe):
                    pe.wait_ge(ch, 4)
                    for g in range(2):
                        mm = pe.transpose(psa[0:HALF, g * P:(g + 1) * P], cand[:, g * HALF:(g + 1) * HALF], ident[:, :])
                    mm.then_inc(pe_s, 1)
                    pe.wait_ge(ch, 9)
                    for n in range(4):
                        mm = pe.matmul(psb[0:1, n * HALF:(n + 1) * HALF], ends[:, n:n + 1], ident[0:HALF, 0:HALF], start=True, stop=True)
                    mm.then_inc(pe_s, 1)
                    pe.wait_ge(ch, 11)
                    for d in range(2):
                        for g in range(2):
                            o = g * HALF + d
                            mm = pe.matmul(psc[0:HALF, 2 * d + g:2 * d + g + 1], crow[:, d, o:o + HALF], one[:, 0:1], start=True, stop=True)
                    mm.then_inc(pe_s, 1)
                    pe.wait_ge(ch, 17)
                    for g in range(2):
                        mm = pe.transpose(psd[:, g * HALF:(g + 1) * HALF], lt[:, g, :], ident[0:HALF, 0:HALF])
                    mm.then_inc(pe_s, 1)

                @block.scalar
                def _(act):
                    act.wait_ge(dn, 1)
                    act.activation(pw[:, :], pw[:, :], ACT.Exp)
                    act.activation(pl[:, :], pl[:, :], ACT.Exp)

            self.edge_pass(f"sum{l}", "gat", H, l, weights=pw, loop_w=pl)

    def edge_pass(self, name, kind, table, layer, weights=None, loop_w=None):
        nc, a, C, G, ident = self.nc, self.a, self.C, self.G, self.ident
        gathers = kind in ("rel", "sage", "tp")
        two_step = gathers
        side = kind in ("rel", "tp")
        halves = 2 if kind == "tp" else 1
        W = {"pre": 5, "gat": D + 1, "rel": D, "sage": D, "tp": D + 1}[kind]
        OW = 8 if kind == "pre" else AW
        dest = self.pre if kind == "pre" else self.agg
        with Pass(nc, name) as q:
            outs = q.sb("outs", [P, KT, OW])
            sf = q.sb("sf", [P, KT, P])
            s0 = q.sb("s0", [1, KT, P])
            carry = q.sb("carry", [1, 2, OW])
            pix = q.sb("pix", [P, KT], U32)
            pso = [q.ps(f"o{k}") for k in range(2)]
            psc = [q.ps(f"c{k}") for k in range(2)]
            if kind == "pre":
                m5 = q.sb("m5", [P, KT, 8])
            if gathers:
                gr = q.sb("gr", [P, KT, D])
                gix = q.sb("gix", [P, KT], U32)
                msg = q.sb("msg", [P, KT, 2 if kind == "tp" else 1, D])
                aT = q.sb("aT", [P, 2, halves * P])
                Wm = q.sb("Wm", [P, halves, W])
                psa = [q.ps(f"a{k}") for k in range(2)]
            if kind == "rel":
                relb = q.sb("relb", [KT * 8, KT * D])
                iota8 = q.sb("iota8", [P, 8])
                sd = q.sb("sd", [P, KT * 8])
                sdT = q.sb("sdT", [KT * 8, P])
                psr, pst = q.ps("rel"), q.ps("sideT")
                sw = KT * 8
            if kind == "tp":
                rec = q.sb("rec", [P, C, REC])
                sd = q.sb("sd", [P, KT * 16])
                sdT = q.sb("sdT", [KT * 16, P])
                W1 = q.sb("W1", [KT * 16, KT, 64])
                W2 = q.sb("W2", [64, D + 64])
                hs = q.sb("hs", [64, KT, P])
                tA = q.sb("tA", [P, 2, D])
                psh, pst = q.ps("hid"), q.ps("wexp")
                sw = KT * 16
            gin, sst = q.sems("rows_in", KT), q.sems("sums_stored", KT)
            gixr, gate, pgate = q.sem("gather_index"), q.sem("gate"), q.sem("tensor_gate")
            sfr, s0r, msgr, turned, kept = q.sem("same_ready"), q.sem("first_row_ready"), q.sem("messages"), q.sem("sums_turned"), q.sem("turned_kept")
            outm, carm, evac, carr = q.sem("sums_made"), q.sem("carry_made"), q.sem("sums_out"), q.sem("carry_ready")
            extra, cst, ch, added = q.sem("last_columns"), q.sem("constants"), q.sem("dve_steps"), q.sem("relation_added")
            sdr, sdt, sdk, relm, hidm, hidk, wxm, init = (q.sem(n) for n in ("side_ready", "side_turned", "side_kept", "relations",
                                                                           "hidden_made", "hidden_kept", "weights_made", "cleared"))
            block = q.block()

            @block.sync
            def _(sp):
                n = 0
                if kind == "rel":
                    sp.dma_start(relb[:, :], a["L1_gnn_relvecs"][layer]).then_inc(cst, 16)
                    sp.dma_start(Wm[:, 0, :], a["L1_gnn_lin_w"][layer]).then_inc(cst, 16)
                    sp.dma_start(iota8[:, :], a["iota8"]).then_inc(cst, 16)
                if kind == "sage":
                    sp.dma_start(Wm[:, 0, :], a[f"L2_gnn_Wn{layer}"]).then_inc(cst, 16)
                if kind == "tp":
                    sp.dma_start(rec[:, :, :], self.rec_d.rearrange("(c p) w -> p c w", p=P)).then_inc(cst, 16)
                    sp.dma_start(W1[:, :, :], a["L3_gnn_W_mlp1"]).then_inc(cst, 16)
                    sp.dma_start(W2[:, :], a["L3_gnn_W_mlp2"]).then_inc(cst, 16)
                    sp.dma_start(Wm[:, :, :], a["L3_out"]).then_inc(cst, 16)

            cleared = 2 if kind == "pre" else 1
            n_cst = {"rel": 3, "sage": 1, "tp": 4}.get(kind, 0) * 16

            @block.gpsimd
            def _(pool):
                bound_g, bound_s = pool.to_reg(self.NP - 1), pool.to_reg(self.NP - 1)

                def gather(cnt, k):
                    pool.wait_ge(gixr, cnt + 1)
                    pool.sem_inc(gate, 1)
                    if not isinstance(cnt, int) or cnt >= KT:
                        if kind == "sage":
                            pool.wait_ge(turned, cnt)
                        else:
                            pool.wait_ge(msgr, cnt - 3)
                        pool.sem_inc(gate, 1)
                    pool.indirect_dma_start(gr[:, k, :], None, table, bass.IndirectOffsetOnAxis(gix[:, k:k + 1], 0),
                                            bounds_check=bound_g, oob_is_err=False).then_inc(gin[k], 16)

                def scatter(cnt, k):
                    pool.wait_ge(extra, cnt + 1)
                    pool.sem_inc(gate, 1)
                    pool.wait_ge(evac, cnt + 3)
                    pool.sem_inc(gate, 1)
                    pool.indirect_dma_start(dest, bass.IndirectOffsetOnAxis(pix[:, k:k + 1], 0), outs[:, k, :], None,
                                            bounds_check=bound_s, oob_is_err=False).then_inc(sst[k], 16)

                if gathers:
                    for k in range(3):
                        gather(k, k)

                    def both(i):
                        for k in range(KT):
                            gather(i * KT + k + 3, (k + 3) % KT)
                            scatter(i * KT + k, k)

                    both(0)
                    with pool.Fori(1, G - 1) as i:
                        both(i)
                    gather(C - 1, KT - 1)
                    for k in range(KT):
                        scatter(C - KT + k, k)
                else:
                    with pool.Fori(0, G) as i:
                        for k in range(KT):
                            scatter(i * KT + k, k)
                for k in range(KT):
                    pool.wait_ge(sst[k], 16 * G)

            @block.vector
            def _(v):
                v.memset(outs[:, :, :], 0.0).then_inc(init, 1)
                v.memset(carry[:, :, :], 0.0).then_inc(carr, 1)
                if kind == "pre":
                    v.memset(m5[:, :, :], 1.0).then_inc(init, 1)
                v.wait_ge(init, cleared)
                if n_cst:
                    v.wait_ge(cst, n_cst)
                if kind == "tp":
                    v.tensor_scalar(Wm[:, :, :], Wm[:, :, :], 1.0 / 8 / 4 / 8, None, ALU.mult).then_inc(init, 1)
                    v.wait_ge(init, 2)
                    v.tensor_scalar(Wm[0:MUL, 1, :], Wm[0:MUL, 1, :], 3.0 ** -0.5, None, ALU.mult).then_inc(init, 1)
                    v.wait_ge(init, 3)

                def g_index(c, k):
                    v.tensor_copy(gix[:, k:k + 1], self.src_i[:, bass.ds(c, 1)]).then_inc(gixr, 1)

                def side_of(g):
                    if kind == "rel":
                        v.tensor_tensor(sd[:, :].rearrange("p (k t) -> p k t", k=KT), fan(self.typ[:, bass.ds(g * KT, KT)], 8),
                                        spread(iota8[:, :], KT), ALU.is_equal).then_inc(sdr, 1)
                    else:
                        v.tensor_copy(sd[:, :].rearrange("p (k t) -> p k t", k=KT),
                                      rec[:, bass.ds(g * KT, KT), R_LEN:R_LEN + 16]).then_inc(sdr, 1)

                PER = 4 * KT

                def body(i, last):
                    st = Chain(v, ch, i, PER) if kind == "tp" else None
                    for k in range(KT):
                        c = i * KT + k
                        if gathers:
                            v.wait_ge(gin[k], i * 16 + 16)
                            if not last:
                                g_index(c + KT, k)
                        if side and not last and k == 0:
                            v.wait_ge(sdt, i + 1)
                            side_of(i + 1)
                        if kind == "gat":
                            v.wait_ge(carm, i * KT + k)
                            v.tensor_scalar(sf[:, k, :], self.same[:, bass.ds(c * P, P)], weights[:, bass.ds(c, 1)], None,
                                            ALU.mult).then_inc(sfr, 1)
                        if kind == "pre":
                            v.wait_ge(carm, i * KT + k)
                            v.tensor_copy(m5[:, k, 0:4], self.te[:, :, bass.ds(c, 1)].rearrange("p l o -> p (l o)")).then_inc(msgr, 1)
                        if kind == "rel":
                            v.wait_ge(relm, i + 1)
                            v.wait_ge(turned, i * KT + k)
                            v.tensor_tensor(msg[:, k, 0, :], gr[:, k, :], psr[:, k * D:(k + 1) * D], ALU.add).then_inc(added, 1)
                        if kind == "tp":
                            v.wait_ge(wxm, i * KT + k + 1)
                            v.wait_ge(turned, i * KT + k)
                            wx = pst[:, 0:192]
                            sh = rec[:, bass.ds(c, 1), R_SH:R_SH + 4].rearrange("p o w -> p (o w)")
                            g1 = gr[:, k, MUL:].rearrange("p (u m) -> p u m", m=3)
                            t3 = tA[:, k % 2, MUL:].rearrange("p (u m) -> p u m", m=3)
                            n1 = st.mark(v.tensor_tensor(t3, g1, spread(sh[:, 1:4], MUL), ALU.mult))
                            n2 = st.mark(v.tensor_tensor(tA[:, k % 2, 0:MUL], gr[:, k, 0:MUL], wx[:, D + MUL:D + 2 * MUL], ALU.mult))
                            v.scalar_tensor_tensor(msg[:, k, 0, :], gr[:, k, :], sh[:, 0:1], wx[:, 0:D], ALU.mult, ALU.mult)
                            st.need(n1)
                            n3 = st.mark(v.tensor_reduce(msg[:, k, 1, 0:MUL], t3, AX_X, ALU.add))
                            st.need(n2)
                            v.tensor_tensor(msg[:, k, 1, MUL:].rearrange("p (u m) -> p u m", m=3), fan(tA[:, k % 2, 0:MUL], 3),
                                            spread(sh[:, 1:4], MUL), ALU.mult)
                            st.need(n3)
                            v.tensor_tensor(msg[:, k, 1, 0:MUL], msg[:, k, 1, 0:MUL], wx[:, D:D + MUL], ALU.mult).then_inc(msgr, 1)
                        v.wait_ge(carm, i * KT + k)
                        v.tensor_scalar(s0[:, k, :], self.same[0:1, bass.ds(c * P, P)], self.cont_row[:, bass.ds(c, 1)], None,
                                        ALU.mult).then_inc(s0r, 1)
                        v.wait_ge(sst[k], i * 16)
                        if kind == "gat":
                            v.tensor_copy(outs[:, k, D + 1:D + 2], loop_w[:, bass.ds(c, 1)])
                        v.tensor_copy(pix[:, k:k + 1], self.put_i[:, bass.ds(c, 1)]).then_inc(extra, 1)
                    if st:
                        st.close()

                if gathers:
                    for k in range(KT):
                        g_index(k, k)
                if side:
                    side_of(0)
                body(0, False)
                with v.Fori(1, G - 1) as i:
                    body(i, False)
                body(G - 1, True)

            @block.scalar
            def _(act):
                act.sem_inc(evac, 2)
                if n_cst:
                    act.wait_ge(cst, n_cst)
                act.wait_ge(init, cleared)

                def side_keep(i):
                    act.wait_ge(sdt, i + 1)
                    act.activation(sdT[:, :], (pst if kind == "rel" else psh)[0:sw, 0:P], ACT.Copy).then_inc(sdk, 1)

                def hidden(i):
                    act.wait_ge(hidm, i + 1)
                    act.activation(hs[:, :, :].rearrange("h k e -> h (k e)"), psh[0:64, :], ACT.Silu, scale=0.25).then_inc(hidk, 1)

                def prepare(c, k):
                    if kind != "gat":
                        act.wait_ge(carm, c)
                        act.activation(sf[:, k, :], self.same[:, bass.ds(c * P, P)], ACT.Copy).then_inc(sfr, 1)
                    if kind == "rel":
                        act.wait_ge(added, c + 1)
                        act.activation(msg[:, k, 0, :], msg[:, k, 0, :], ACT.Relu).then_inc(msgr, 1)

                def body(i, last):
                    for k in range(KT):
                        c = i * KT + k
                        if not (last and k == KT - 1):
                            prepare(c + 1, (k + 1) % KT)
                        if side and not last and k == 1:
                            side_keep(i + 1)
                            if kind == "tp":
                                hidden(i + 1)
                        if two_step:
                            act.wait_ge(turned, i * KT + k + KT)
                            act.activation(aT[:, k % 2, :], psa[k % 2][:, 0:halves * P], ACT.Copy).then_inc(kept, 1)
                        act.wait_ge(carm, c + KT)
                        act.activation(carry[:, (k + 1) % 2, 0:W], psc[k % 2][0:1, 0:W], ACT.Copy).then_inc(carr, 1)
                        act.wait_ge(outm, c + 1)
                        act.wait_ge(sst[k], i * 16)
                        act.activation(outs[:, k, 0:W], pso[k % 2][:, 0:W], ACT.Copy).then_inc(evac, 1)

                if side:
                    side_keep(0)
                if kind == "tp":
                    hidden(0)
                prepare(0, 0)
                body(0, False)
                with act.Fori(1, G - 1) as i:
                    body(i, False)
                body(G - 1, True)

            @block.tensor
            def _(pe):
                pe.sem_inc(carm, KT - 1)
                if two_step:
                    pe.sem_inc(turned, KT - 1)
                if n_cst:
                    pe.wait_ge(cst, n_cst)
                if kind == "tp":
                    pe.wait_ge(init, 3)

                def until(sem, n):
                    pe.wait_ge(sem, n)
                    pe.sem_inc(pgate, 1)

                def side_turn(i):
                    until(sdr, i + 1)
                    if kind == "tp":
                        until(hidk, i)
                    pe.transpose((pst if kind == "rel" else psh)[0:sw, 0:P], sd[:, :], ident[:, :]).then_inc(sdt, 1)

                def side_use(i):
                    until(sdk, i + 1)
                    if kind == "rel":
                        until(msgr, i * KT)
                        pe.matmul(psr[:, :], sdT[:, :], relb[:, :], start=True, stop=True).then_inc(relm, 1)
                    else:
                        for k in range(KT):
                            mm = pe.matmul(psh[0:64, k * P:(k + 1) * P], W1[:, k, :], sdT[:, :], start=True, stop=True)
                        mm.then_inc(hidm, 1)

                def path_weights(c, k, i):
                    if k % KT == 0:
                        until(hidk, i + 1)
                    until(msgr, c)
                    pe.matmul(pst[:, 0:192], hs[:, k % KT, :], W2[:, :], start=True, stop=True).then_inc(wxm, 1)

                def turn(c, k, it):
                    pe.wait_ge(sfr, c + 1)
                    if kind == "sage":
                        pe.wait_ge(gin[k], it * 16 + 16)
                    else:
                        pe.wait_ge(msgr, c + 1)
                    if not isinstance(c, int) or c >= 2:
                        pe.wait_ge(kept, c - 1)
                    for h in range(halves):
                        lhs = gr[:, k, :] if kind == "sage" else msg[:, k, h, :]
                        mm = pe.matmul(psa[k % 2][:, h * P:(h + 1) * P], lhs, sf[:, k, :], start=True, stop=True)
                    mm.then_inc(turned, 1)

                def sums(c, k):
                    pe.wait_ge(evac, c + 1)
                    if two_step:
                        pe.wait_ge(kept, c + 1)
                        pairs = [(aT[:, k % 2, h * P:(h + 1) * P], Wm[:, h, :]) for h in range(halves)]
                    elif kind == "gat":
                        pe.wait_ge(sfr, c + 1)
                        pairs = [(sf[:, k, :], table[:, bass.ds(c, 1), 0:W].rearrange("p o w -> p (o w)"))]
                    else:
                        pe.wait_ge(sfr, c + 1)
                        pe.wait_ge(msgr, c + 1)
                        pairs = [(sf[:, k, :], m5[:, k, 0:W])]
                    for n, (x, y) in enumerate(pairs):
                        pe.matmul(pso[k % 2][:, 0:W], x, y, start=(n == 0), stop=False)
                    for n, (x, y) in enumerate(pairs):
                        pe.matmul(psc[k % 2][0:1, 0:W], x[:, P - 1:P], y, start=(n == 0), stop=False)
                    pe.wait_ge(carr, c + 1)
                    pe.wait_ge(s0r, c + 1)
                    pe.matmul(pso[k % 2][:, 0:W], s0[:, k, :], carry[:, k % 2, 0:W], start=False, stop=True).then_inc(outm, 1)
                    pe.matmul(psc[k % 2][0:1, 0:W], s0[:, k, P - 1:P], carry[:, k % 2, 0:W], start=False, stop=True).then_inc(carm, 1)

                def body(i, last):
                    for k in range(KT):
                        c = i * KT + k
                        if side and not last and k == 0:
                            side_turn(i + 1)
                        if kind == "rel" and not last and k == 3:
                            side_use(i + 1)
                        if two_step and not (last and k == KT - 1):
                            turn(c + 1, (k + 1) % KT, i + (k + 1) // KT)
                        if kind == "tp" and not (last and k >= 2):
                            path_weights(c + 2, k + 2, i + (k + 2) // KT)
                        if kind == "tp" and not last and k == 1:
                            side_use(i + 1)
                        sums(c, k)

                if side:
                    side_turn(0)
                    side_use(0)
                if kind == "tp":
                    path_weights(0, 0, 0)
                if two_step:
                    turn(0, 0, 0)
                if kind == "tp":
                    path_weights(1, 1, 0)
                body(0, False)
                with pe.Fori(1, G - 1) as i:
                    body(i, False)
                body(G - 1, True)

    def node_pass(self, name, kind, src, layer, dst=None, dst2=None, extra=None):
        nc, a, NBLK, ident = self.nc, self.a, self.NBLK, self.ident
        nc, a, NBLK, ident = self.nc, self.a, self.NBLK, self.ident
        gat, rel, sage = kind in ("gat", "gat_end"), kind[:3] == "rel", kind[:4] == "sage"
        linear = kind in ("lin", "gat")
        two_norms = kind in ("gat_end", "rel2")
        normed = kind not in ("lin", "sage0", "sage1")
        affine = kind == "gat_end" or rel
        relu2 = kind in ("rel0", "rel1")
        src_w = AW if gat else D
        res_w = AW if linear else D
        with Pass(nc, name) as q:
            x = q.sb("x", [P, 2, KT, src_w])
            ag = q.sb("ag", [P, 2, KT, AW])
            ex = q.sb("ex", [P, 2, KT, D])
            y = q.sb("y", [P, 2, KT, D])
            z = q.sb("z", [P, 2, KT, D])
            res = q.sb("res", [P, 2, KT, res_w])
            res2 = q.sb("res2", [P, 2, KT, D])
            xT = q.sb("xT", [P, 2, KT, P])
            bn = q.sb("bn", [P, 2, 2, KT, 6])
            mv = q.sb("mv", [P, 2, 2, KT, 2])
            rs = q.sb("rs", [P, 2, 2, 4, KT])
            sm = q.sb("sm", [P, 2, 3, KT])
            bias = q.sb("bias", [P, D])
            ln_w = q.sb("ln_w", [P, 2, D])
            ln_c = q.sb("ln_c", [P, 2])
            Wn = q.sb("Wn", [P, D])
            WT = q.sb("WT", [P, D])
            att = q.sb("att", [P, 2])
            Wl = q.sb("Wl", [P, 2 * D])
            na = q.sb("na", [P, NBLK * KT])
            pT = [q.ps(f"T{j}") for j in range(2)]
            pM = [[q.ps(f"M{j}{h}") for h in range(2)] for j in range(2)]
            pN = [q.ps(f"N{j}") for j in range(2)]
            lin_, stored, stored2 = q.sems("rows_in", 2), q.sems("result_stored", 2), q.sems("second_stored", 2)
            cst, wat, wak, wam, wrd = (q.sem(n) for n in ("constants", "w_turned", "w_kept", "w_att", "w_ready"))
            ch, gch, gate = q.sem("dve_steps"), q.sem("pool_steps"), q.sem("gate")
            names = ("y_ready", "scale_ready", "normed", "affine_done", "scale2_ready", "result_ready", "second_ready",
                     "turned", "turned_kept", "product_made", "turned2", "turned2_kept", "product2_made")
            yr, sr, zr, af, sr2, rr, rr2, tr, tk, mr, tr2, tk2, mr2 = counts = [q.sem(n) for n in names]
            block = q.block()

            def done(eng, sem, n):
                eng.wait_ge(sem, n + 2)

            def free(eng, sem, n):
                eng.wait_ge(sem, n)

            consts = []
            if gat or rel:
                r, pre = (layer - 1, "L0_gnn_") if gat else (layer, "L1_gnn_")
                consts.append((bias[:, :], a[pre + ("bias" if gat else "lin_b")][r].partition_broadcast(P)))
                if affine:
                    g_, b_ = ("ln_gamma", "ln_beta") if gat else ("ln_w", "ln_b")
                    consts.append((ln_w[:, 0, :], a[pre + g_][r].partition_broadcast(P)))
                    consts.append((ln_w[:, 1, :], a[pre + b_][r].partition_broadcast(P)))
                if kind == "gat":
                    consts.append((ln_c[:, :], a["L0_ln_cols"][r]))
            if sage:
                consts.append((bias[:, :], a[f"L2_gnn_b{layer}"].partition_broadcast(P)))
                consts.append((Wn[:, :], a[f"L2_gnn_Ws{layer}"]))
            if linear:
                consts.append((Wl[:, 0:D], a["L0_gnn_W"][layer]))
                consts.append((att[:, :], a["L0_att_cols"][layer]))
            if kind == "sage2":
                consts.append((Wl[:, :], a["L3_in"]))
            if kind in ("sage2", "fin"):
                consts.append((na[:, :], a["node_vec1"]))
            loads = []
            if kind != "rel0":
                loads.append((x, self.table if gat else src, src_w))
            if kind != "lin":
                loads.append((ag, self.agg, AW))
            if extra is not None or kind == "gat_end":
                loads.append((ex, extra if extra is not None else src, D))
            last_use = tr if kind == "lin" else af if two_norms else yr
            n_stores = 0
            first = dst if not linear else self.table
            second = dst2
            first_buf = y if relu2 else res

            def at(ap, n):
                return ap.rearrange("(b p k) d -> b p k d", p=P, k=KT)[bass.ds(n, 1)].rearrange("b p k d -> (b p) k d")

            @block.sync
            def _(sp):
                for s_ in counts:
                    sp.sem_inc(s_, 1)
                for t_, s_ in consts:
                    sp.dma_start(t_, s_).then_inc(cst, 16)

                def load(n, j):
                    for buf, ap, w in loads:
                        sp.dma_start(buf[:, j, :, :], at(ap, n)).then_inc(lin_[j], 16)

                def body(i, last):
                    for j in range(2):
                        if not last:
                            done(sp, last_use, i * 2 + j)
                            load(i * 2 + 2 + j, j)
                    for j in range(2):
                        if relu2:
                            done(sp, yr, i * 2 + j)
                        elif kind == "sage2":
                            done(sp, af, i * 2 + j)
                        else:
                            done(sp, rr, i * 2 + j)
                        sp.dma_start(at(first, i * 2 + j), first_buf[:, j, :, :]).then_inc(stored[j], 16)
                        if second is not None:
                            done(sp, rr2, i * 2 + j)
                            sp.dma_start(at(second, i * 2 + j), res2[:, j, :, :]).then_inc(stored2[j], 16)

                for j in range(2):
                    load(j, j)
                body(0, False)
                with sp.Fori(1, NBLK // 2 - 1) as i:
                    body(i, False)
                body(NBLK // 2 - 1, True)
                for j in range(2):
                    sp.wait_ge(stored[j], 16 * (NBLK // 2))
                    if second is not None:
                        sp.wait_ge(stored2[j], 16 * (NBLK // 2))

            def arrived(eng, i, j):
                eng.wait_ge(lin_[j], (i + 1) * 16 * len(loads))

            def per_block(eng, steps):
                def pair(i):
                    for step in steps:
                        for j in range(2):
                            step(i, i * 2 + j, j)

                pair(0)
                with eng.Fori(1, NBLK // 2) as i:
                    pair(i)

            @block.tensor
            def _(pe):
                pe.wait_ge(cst, 16 * len(consts))
                if linear:
                    pe.transpose(pT[0][:, 0:D], Wl[:, 0:D], ident[:, :]).then_inc(wat, 1)
                    pe.wait_ge(wak, 1)
                    pe.matmul(pN[0][:, 0:2], WT[:, :], att[:, :], start=True, stop=True).then_inc(wam, 1)
                    pe.wait_ge(wrd, 1)

                def turn(buf, sem):
                    def step(i, n, j):
                        if buf is x:
                            arrived(pe, i, j)
                            free(pe, tk, n)
                        else:
                            done(pe, zr, n)
                            free(pe, tk2, n)
                        for k in range(KT):
                            mm = pe.transpose(pT[j][:, k * P:(k + 1) * P], buf[:, j, k, 0:D], ident[:, :])
                        mm.then_inc(sem, 1)
                    return step

                def own(i, n, j):
                    done(pe, tk, n)
                    free(pe, yr, n)
                    for k in range(KT):
                        mm = pe.matmul(pN[j][:, k * D:(k + 1) * D], xT[:, j, k, :], Wn[:, :], start=True, stop=True)
                    mm.then_inc(mr, 1)

                def product(kept):
                    w = AW if linear else 2 * D

                    def step(i, n, j):
                        done(pe, kept, n)
                        free(pe, rr if linear else rr2, n)
                        if kind == "sage2":
                            free(pe, af, n)
                        for k in range(KT):
                            mm = pe.matmul(pM[j][k // 2][:, (k % 2) * w:(k % 2 + 1) * w], xT[:, j, k, :], Wl[:, 0:w], start=True, stop=True)
                        mm.then_inc(mr2, 1)
                    return step

                steps = {"lin": [turn(x, tr), product(tk)], "gat": [turn(z, tr2), product(tk2)],
                         "sage0": [turn(x, tr), own], "sage1": [turn(x, tr), own],
                         "sage2": [turn(x, tr), own, turn(z, tr2), product(tk2)]}.get(kind)
                if steps:
                    per_block(pe, steps)

            @block.gpsimd
            def _(pool):
                def scale(i, n, j, stage, st):
                    done(pool, (yr, af)[stage], n)
                    m, t = mv[:, j, stage], rs[:, j, stage]
                    st.run(pool.tensor_tensor(t[:, 0, :], m[:, :, 1], self.eps_t[:, :], ALU.add))
                    st.run(pool.tensor_tensor(t[:, 1, :], t[:, 0, :], self.mhalf[:, :], ALU.pow))
                    st.run(pool.tensor_tensor(t[:, 2, :], m[:, :, 0], t[:, 1, :], ALU.mult))
                    pool.tensor_tensor(t[:, 3, :], t[:, 2, :], self.neg1[:, :], ALU.mult).then_inc((sr, sr2)[stage], 1)

                if normed:
                    def pair(i):
                        st = Chain(pool, gch, i, 12)
                        for stage in range(2 if two_norms else 1):
                            for j in range(2):
                                scale(i, i * 2 + j, j, stage, st)
                        st.close()

                    pair(0)
                    with pool.Fori(1, NBLK // 2) as i:
                        pair(i)

            @block.vector
            def _(v):
                v.wait_ge(cst, 16 * len(consts))
                if linear:
                    v.wait_ge(wat, 1)
                    v.tensor_copy(WT[:, :], pT[0][:, 0:D]).then_inc(wak, 1)
                    v.wait_ge(wam, 1)
                    v.tensor_copy(Wl[:, D:AW], pN[0][:, 0:2]).then_inc(wrd, 1)
                if kind == "sage2":
                    v.tensor_scalar(na[:, :], na[:, :], MUL ** -0.5, None, ALU.mult).then_inc(wrd, 1)
                    v.wait_ge(wrd, 1)
                if kind == "fin":
                    v.tensor_tensor(na[:, :], na[:, :], na[:, :], ALU.mult).then_inc(wrd, 1)
                    v.wait_ge(wrd, 1)

                def stats(buf, j, stage, st, sem):
                    for k in range(KT):
                        m = st.mark(v.bn_stats(bn[:, j, stage, k, :], buf[:, j, k, :]))
                    st.need(m)
                    v.sem_inc(gate, 1)
                    for k in range(KT):
                        last = v.bn_aggr(mv[:, j, stage, k, :], bn[:, j, stage, k, :])
                    last.then_inc(sem, 1)

                def combine(i, n, j, st):
                    arrived(v, i, j)
                    free(v, zr if normed else rr, n)
                    if relu2:
                        v.wait_ge(stored[j], i * 16)
                    cols = bass.ds(n * KT, KT)
                    s_ = sm[:, j]
                    if gat:
                        st.run(v.tensor_tensor(s_[:, 0, :], ag[:, j, :, D + 1], self.no_edge[:, cols], ALU.add))
                        st.run(v.scalar_tensor_tensor(s_[:, 1, :], s_[:, 0, :], 1e-16, ag[:, j, :, D], ALU.add, ALU.add))
                        m = st.mark(v.reciprocal(s_[:, 2, :], s_[:, 1, :]))
                        for k in range(KT):
                            m = st.mark(v.scalar_tensor_tensor(y[:, j, k, :], x[:, j, k, 0:D], s_[:, 0, k:k + 1], ag[:, j, k, 0:D],
                                                               ALU.mult, ALU.add))
                        st.need(m)
                        for k in range(KT):
                            m = st.mark(v.scalar_tensor_tensor(y[:, j, k, :], y[:, j, k, :], s_[:, 2, k:k + 1], bias[:, :],
                                                               ALU.mult, ALU.add))
                        st.need(m)
                    else:
                        if kind == "fin":
                            m = st.mark(v.tensor_tensor(s_[:, 0, :], ag[:, j, :, D], na[:, cols], ALU.mult))
                        else:
                            m = st.mark(v.tensor_copy(s_[:, 0, :], self.inv_cnt[:, cols]))
                        if sage:
                            done(v, mr, n)
                        st.need(m)
                        for k in range(KT):
                            own_ = {"rel0": bias[:, :], "sage0": pN[j][:, k * D:(k + 1) * D]}.get(kind)
                            if own_ is None:
                                own_ = pN[j][:, k * D:(k + 1) * D] if sage else x[:, j, k, :]
                            m = st.mark(v.scalar_tensor_tensor(y[:, j, k, :], ag[:, j, k, 0:D], s_[:, 0, k:k + 1], own_, ALU.mult, ALU.add))
                        if kind not in ("rel0", "fin"):
                            st.need(m)
                            m = st.mark(v.tensor_tensor(y[:, j], y[:, j], spread(bias[:, :], KT), ALU.add))
                        if kind in ("sage1", "sage2"):
                            st.need(m)
                            m = st.mark(v.tensor_tensor(y[:, j], y[:, j], (x if kind == "sage1" else ex)[:, j], ALU.add))
                        st.need(m)
                    if normed:
                        stats(y, j, 0, st, yr)
                    else:
                        v.sem_inc(yr, 1)

                def apply(i, n, j, st):
                    done(v, zr, n)
                    st.run(v.tensor_tensor(z[:, j], z[:, j], spread(ln_w[:, 0, :], KT), ALU.mult))
                    m = st.mark(v.tensor_tensor(z[:, j], z[:, j], spread(ln_w[:, 1, :], KT), ALU.add))
                    st.need(m)
                    if two_norms:
                        st.run(v.tensor_tensor(z[:, j], z[:, j], ex[:, j], ALU.add))
                        stats(z, j, 1, st, af)
                    else:
                        v.sem_inc(af, 1)

                def shortcut(i, n, j, st):
                    done(v, mr2, n)
                    v.wait_ge(stored[j], i * 16)
                    m = st.mark(v.tensor_copy(sm[:, j, 1, :], na[:, bass.ds(n * KT, KT)]))
                    st.need(m)
                    for k in range(KT):
                        last = v.scalar_tensor_tensor(res[:, j, k, :], pM[j][k // 2][:, (k % 2) * 2 * D:(k % 2) * 2 * D + D],
                                                      sm[:, j, 1, k:k + 1], z[:, j, k, :], ALU.mult, ALU.add)
                    last.then_inc(af, 1)

                if kind != "lin":
                    steps = [combine] + ([apply] if affine else []) + ([shortcut] if kind == "sage2" else [])

                    def pair(i):
                        st = Chain(v, ch, i, 48)
                        for step in steps:
                            for j in range(2):
                                step(i, i * 2 + j, j, st)
                        st.close()

                    pair(0)
                    with v.Fori(1, NBLK // 2) as i:
                        pair(i)

            @block.scalar
            def _(act):
                act.wait_ge(cst, 16 * len(consts))

                def keep(turned, kept):
                    def step(i, n, j):
                        done(act, turned, n)
                        o, p_ = xT[:, j].rearrange("f k n -> f (k n)"), pT[j][:, :]
                        if kind == "gat":
                            act.activation(o, p_, ACT.Identity, scale=ln_c[:, 0:1], bias=ln_c[:, 1:2]).then_inc(kept, 1)
                        else:
                            act.activation(o, p_, ACT.Copy).then_inc(kept, 1)
                    return step

                def norm(stage):
                    def step(i, n, j):
                        done(act, (sr, sr2)[stage], n)
                        to, frm, sem = (z, y, zr) if stage == 0 else (res, z, rr)
                        if kind == "fin":
                            to = res
                        if to is res:
                            act.wait_ge(stored[j], i * 16)
                        if stage == 0 and kind in ("gat", "sage2"):
                            free(act, tr2, n)
                        if kind == "sage2":
                            free(act, af, n)
                        if stage == 0 and affine:
                            free(act, rr if two_norms else rr2, n)
                        for k in range(KT):
                            last = act.activation(to[:, j, k, :], frm[:, j, k, :], ACT.Identity, scale=rs[:, j, stage, 1, k:k + 1],
                                                  bias=rs[:, j, stage, 3, k:k + 1])
                        last.then_inc(sem, 1)
                        if kind == "fin":
                            act.drain().then_inc(rr, 1)
                    return step

                def heads(i, n, j):
                    done(act, mr2, n)
                    act.wait_ge(stored[j], i * 16)
                    for h in range(2):
                        p_ = pM[j][h][:, 0:2 * AW].rearrange("p (k w) -> p k w", k=2)
                        act.activation(res[:, j, 2 * h:2 * h + 2, :], p_, ACT.Copy)
                        last = act.activation(self.asad[:, bass.ds(n * KT + 2 * h, 2), :], p_[:, :, D:AW], ACT.Copy)
                    last.then_inc(rr, 1)

                def relu(frm, ready, to, sem, st_):
                    def step(i, n, j):
                        done(act, ready, n)
                        act.wait_ge(st_[j], i * 16)
                        act.activation(to[:, j], frm[:, j], ACT.Relu).then_inc(sem, 1)
                    return step

                def features(i, n, j):
                    done(act, mr2, n)
                    done(act, af, n)
                    act.wait_ge(stored2[j], i * 16)
                    for k in range(KT):
                        last = act.activation(res2[:, j, k, :], pM[j][k // 2][:, (k % 2) * 2 * D + D:(k % 2) * 2 * D + 2 * D], ACT.Copy,
                                              scale=sm[:, j, 1, k:k + 1])
                    last.then_inc(rr2, 1)

                per_block(act, {"lin": [keep(tr, tk), heads], "gat": [norm(0), keep(tr2, tk2), heads], "gat_end": [norm(0), norm(1)],
                                "rel0": [norm(0), relu(z, af, res2, rr2, stored2)], "rel1": [norm(0), relu(z, af, res2, rr2, stored2)],
                                "rel2": [norm(0), norm(1)], "sage0": [keep(tr, tk), relu(y, yr, res, rr, stored)],
                                "sage1": [keep(tr, tk), relu(y, yr, res, rr, stored)],
                                "sage2": [keep(tr, tk), norm(0), keep(tr2, tk2), features], "fin": [norm(0)]}[kind])


def gnn_kernel(nc, a, out, N, E):
    Kernel(nc, a, out, N, E).build()


def kernel(**inputs):
    import numpy as _np
    import concourse.bacc as _bacc
    from concourse import mybir as _mybir
    from concourse.bass_utils import run_bass_kernel_spmd as _run

    t = {k: _np.asarray(v) for k, v in inputs.items()}
    N, E = t["x"].shape[0], t["src"].shape[0]
    C = -(-E // BLOCK) * KT
    NP = -(-N // BLOCK) * BLOCK

    def edges(v, fill=0):
        w = _np.full((C * P,) + v.shape[1:], fill, v.dtype)
        w[:E] = v
        return _np.ascontiguousarray(_np.moveaxis(w.reshape((C, P) + v.shape[1:]), 0, 1))

    def rows(v, n):
        w = _np.zeros((n,) + v.shape[1:], v.dtype)
        w[:v.shape[0]] = v
        return w

    def vectors(w):
        o = _np.zeros((96, 96), w.dtype)
        for m in range(3):
            o[m::3, m::3] = w
        return o

    d = {"x": rows(t["x"], NP), "src": edges(t["src"]), "dst": edges(t["dst"], NP - 1), "edge_type_5": edges(t["edge_type_5"]),
         "edge_attr_4": edges(t["edge_attr_4"]), "edge_attr_16": edges(t["edge_attr_16"]),
         "edge_attr_128": rows(t["edge_attr_128"], C * P)}
    d["node_vec1"] = _np.ascontiguousarray(rows(t["node_vec1"], NP).reshape(-1, P, KT).transpose(1, 0, 2).reshape(P, -1))
    for n in ("W", "We", "bias", "ln_gamma", "ln_beta"):
        d["L0_gnn_" + n] = t["L0_gnn_" + n]
    d["L0_gnn_att_edge"] = _np.ascontiguousarray(t["L0_gnn_att_edge"].T)
    d["L0_att_cols"] = _np.stack([t["L0_gnn_att_src"], t["L0_gnn_att_dst"]], axis=-1)
    d["L0_ln_cols"] = _np.stack([t["L0_gnn_ln_gamma"], t["L0_gnn_ln_beta"]], axis=-1)
    d["dst_rows"] = _np.concatenate([t["dst"], _np.full(C * P + 1 - E, NP - 1, t["dst"].dtype)])
    rel = t["L1_gnn_relvecs"]
    d["L1_gnn_relvecs"] = _np.zeros((rel.shape[0], KT * 8, KT * D), rel.dtype)
    for k in range(KT):
        d["L1_gnn_relvecs"][:, 8 * k:8 * k + rel.shape[1], k * D:(k + 1) * D] = rel
    d["L1_gnn_lin_w"] = _np.ascontiguousarray(t["L1_gnn_lin_w"].transpose(0, 2, 1))
    for n in ("lin_b", "ln_w", "ln_b"):
        d["L1_gnn_" + n] = t["L1_gnn_" + n]
    for l in range(3):
        d[f"L2_gnn_Ws{l}"] = _np.ascontiguousarray(t[f"L2_gnn_Ws{l}"].T)
        d[f"L2_gnn_Wn{l}"] = _np.ascontiguousarray(t[f"L2_gnn_Wn{l}"].T)
        d[f"L2_gnn_b{l}"] = t[f"L2_gnn_b{l}"]
    d["iota8"] = _np.tile(_np.arange(8, dtype=_np.float32), (P, 1))
    f32 = t["x"].dtype
    d["L3_in"] = _np.zeros((D, 2 * D), f32)
    for o, (s, v) in ((0, ("W_sc0", "W_sc1")), (D, ("W_l10", "W_l11"))):
        d["L3_in"][:MUL, o:o + MUL] = t["L3_gnn_" + s]
        d["L3_in"][MUL:, o + MUL:o + D] = vectors(t["L3_gnn_" + v])
    d["L3_out"] = _np.zeros((D, 2, D + 1), f32)
    for h, (s, v, al) in enumerate((("W_l2a", "W_l2d", "A0"), ("W_l2b", "W_l2c", "A1"))):
        d["L3_out"][:MUL, h, :MUL] = t["L3_gnn_" + s]
        d["L3_out"][MUL:, h, MUL:D] = vectors(t["L3_gnn_" + v])
        d["L3_out"][:MUL, h, D] = t["L3_gnn_" + al][:, 0]
    w1 = t["L3_gnn_W_mlp1"]
    d["L3_gnn_W_mlp1"] = _np.zeros((KT * 16, KT, 64), f32)
    for k in range(KT):
        d["L3_gnn_W_mlp1"][16 * k:16 * k + 16, k] = w1
    w2 = t["L3_gnn_W_mlp2"]
    d["L3_gnn_W_mlp2"] = _np.concatenate([w2[:, 0:32], _np.repeat(w2[:, 64:96], 3, axis=1), w2[:, 96:128], w2[:, 32:64]], axis=1)

    nc = _bacc.Bacc("TRN2", target_bir_lowering=False, num_devices=1)
    arrays, args = {}, {}
    for name, v in d.items():
        arrays[f"in_{name}"] = v
        args[name] = nc.dram_tensor(f"in_{name}", v.shape, _mybir.dt.from_np(v.dtype), kind="ExternalInput").ap()
    out = nc.dram_tensor("out_0_dram", (NP, D), F32, kind="ExternalOutput").ap()
    gnn_kernel(nc, args, out, N, E)
    r = _run(nc, [arrays], core_ids=[0])
    return r.results[0]["out_0_dram"][:N]
```

```python
from contextlib import ExitStack

import concourse.bass as bass
from concourse import mybir

F32 = mybir.dt.float32
BF16 = mybir.dt.bfloat16
I32 = mybir.dt.int32
U32 = mybir.dt.uint32
ALU = mybir.AluOpType
ACT = mybir.ActivationFunctionType
AX_X = mybir.AxisListType.X

P = 128
D = 128
KT = 4
BLOCK = P * KT
LN_EPS = 1e-5
NEG_SLOPE = 0.2
BIG = 1e30
SKIP = 1 << 20
AW = 130
REC = 32
R_DST, R_SRC, R_TYPE, R_SH, R_LEN, R_TE = 0, 1, 2, 4, 8, 24
MUL = 32
PEEL = 10
LAST = slice(96, 128)


class Chain:

    def __init__(self, eng, sem, i, per):
        self.eng, self.sem, self.base, self.per, self.k = eng, sem, i * per, per, 0

    def mark(self, ins):
        self.k += 1
        ins.then_inc(self.sem, 1)
        return self.k

    def need(self, k):
        self.eng.wait_ge(self.sem, self.base + k)

    def run(self, ins):
        self.need(self.mark(ins))

    def close(self):
        assert self.k <= self.per, self.k
        if self.k < self.per:
            self.eng.sem_inc(self.sem, self.per - self.k)


class Block:

    def __init__(self, n, i, m):
        self.n, self.s2, self.s4, self.t4 = n, m % 2, m % 4, i + m // 4


class Pass:

    def __init__(self, nc, name):
        self.nc, self.name, self.ctx, self.owned = nc, name, ExitStack(), []

    def __enter__(self):
        return self

    def __exit__(self, *e):
        self.ctx.close()
        self.nc.clear_and_free_semaphores(self.owned)
        self.nc.all_engine_barrier()

    def sb(self, name, shape, dt=F32):
        return self.ctx.enter_context(self.nc.sbuf_tensor(f"{self.name}_{name}", shape, dt))

    def ps(self, name):
        return self.ctx.enter_context(self.nc.psum_tensor(f"{self.name}_{name}", [P, 512], F32))

    def sem(self, name):
        self.owned.append(self.nc.alloc_semaphore(f"{self.name}_{name}"))
        return self.owned[-1]

    def sems(self, name, n):
        return [self.sem(f"{name}{k}") for k in range(n)]

    def block(self):
        return self.ctx.enter_context(self.nc.Block())


def spread(ap, n):
    return ap.unsqueeze(1).to_broadcast([ap.shape[0], n, ap.shape[1]])


def fan(ap, n):
    return ap.unsqueeze(2).to_broadcast([ap.shape[0], ap.shape[1], n])


def backward(ap):
    (ps, pn), (fs, fn) = ap.ap
    return bass.AP(ap.tensor, ap.offset + fs * (fn - 1), [[ps, pn], [-fs, fn]])


class Kernel:
    def __init__(self, nc, a, out, N, E):
        self.nc, self.a, self.out = nc, a, out
        self.C = C = -(-E // BLOCK) * KT
        self.G = C // KT
        self.NBLK = -(-N // BLOCK)
        self.NP = self.NBLK * BLOCK
        self.NCOL = self.NBLK * KT
        self.HALF = C // 2
        assert self.NBLK % 4 == PEEL % 4 and C % 2 == 0 and self.HALF <= P and self.G % 2 == 1

    def dram(self, name, shape, dt=F32):
        return self.nc.dram_tensor(name, shape, dt, kind="Internal").ap()

    def build(self):
        nc, C, NP, NCOL, HALF = self.nc, self.C, self.NP, self.NCOL, self.HALF
        self.table = self.dram("gat_table", (NP, AW))
        self.aux = self.dram("gat_aux", (NP, 2))
        self.agg = self.dram("aggregate", (NP, AW))
        self.pre = self.dram("edge_sums", (NP, 8))
        self.rec_d = self.dram("records", (C * P, REC))
        self.dst_d = self.dram("dst_sorted", (C * P + 2,))
        nodes = [self.dram(f"nodes_{n}", (NP, D)) for n in range(5)]
        with ExitStack() as ctx:
            def keep(name, shape, dt=F32):
                return ctx.enter_context(nc.sbuf_tensor(name, shape, dt))

            self.ident = keep("ident", [P, P])
            self.same = keep("same_run", [P, C * P], BF16)
            self.src_i = keep("src_i", [P, C], U32)
            self.dst_i = keep("dst_i", [P, C], U32)
            self.put_i = keep("put_i", [P, C], U32)
            self.te = keep("te", [P, 4, C])
            self.typ = keep("typ", [P, C])
            self.reach = keep("reach", [P, C])
            self.iota_f = keep("iota_f", [P, P])
            self.tmean = keep("tmean", [P, 4, NCOL])
            self.inv_cnt = keep("inv_cnt", [P, NCOL])
            self.no_edge = keep("no_edge", [P, NCOL])
            self.asad = keep("asad", [P, NCOL, 2])
            self.pen = keep("pen", [HALF, 2, 2, P])
            self.pen_carry = keep("pen_carry", [HALF, 2, 2, P])
            self.pen_row = keep("pen_row", [1, 2, C])
            self.mhalf = keep("mhalf", [P, KT])
            self.neg1 = keep("neg1", [P, KT])
            self.eps_t = keep("eps_t", [P, KT])

            self.records()
            self.order()
            self.graph()
            self.edge_pass("pre", "pre", None, None)
            self.counts()
            a, n = self.a, nodes
            self.node_pass("x0", "lin", a["x"], layer=0)
            for l in range(4):
                self.self_loops(l)
                self.attention(l)
                if l < 3:
                    self.node_pass(f"g{l + 1}", "gat", None, layer=l + 1)
            self.node_pass("g4", "gat_end", a["x"], layer=4, dst=n[0])
            self.edge_pass("r0", "rel", n[0], 0)
            self.node_pass("r0n", "rel0", None, layer=0, dst=n[1], dst2=n[2])
            self.edge_pass("r1", "rel", n[2], 1)
            self.node_pass("r1n", "rel1", n[1], layer=1, dst=n[3], dst2=n[2])
            self.edge_pass("r2", "rel", n[2], 2)
            self.node_pass("r2n", "rel2", n[3], layer=2, dst=n[1], extra=n[0])
            self.edge_pass("s0", "sage", n[1], 0)
            self.node_pass("s0n", "sage0", n[1], layer=0, dst=n[2])
            self.edge_pass("s1", "sage", n[2], 1)
            self.node_pass("s1n", "sage1", n[2], layer=1, dst=n[3])
            self.edge_pass("s2", "sage", n[3], 2)
            self.node_pass("s2n", "sage2", n[3], layer=2, dst=n[0], dst2=n[2], extra=n[1])
            self.edge_pass("tp", "tp", n[2], 0)
            self.node_pass("fin", "fin", n[0], layer=0, dst=self.out)

    def records(self):
        a, C, G, NP, agg, pre, rec_d, ident = self.a, self.C, self.G, self.NP, self.agg, self.pre, self.rec_d, self.ident
        with Pass(self.nc, "rec") as q:
            zn = 14 * KT
            zero = q.sb("zero", [P, zn * AW])
            rec = q.sb("rec", [P, C, REC])
            raw = q.sb("raw", [P, 3, C], I32)
            len16 = q.sb("len16", [P, C, 16])
            sh4 = q.sb("sh4", [P, C, 4])
            ea = q.sb("ea", [P, 2, KT, D])
            junk = q.sb("junk", [P, 2, 4 * KT, D])
            dots = q.sb("dots", [P, 2, KT, 4])
            wet = q.sb("wet", [P, 4, D])
            we = q.sb("we", [P, 4, D])
            att = q.sb("att", [P, 4])
            attb = q.sb("attb", [P, 4, P])
            vte = q.sb("vte", [P, 4, D])
            pst, psv = q.ps("we_t"), q.ps("vte_p")
            ld, zs, zst, eld = q.sem("loaded"), q.sem("zeroed"), q.sem("zero_stored"), q.sems("edges_in", 2)
            idr, wt, wts = q.sem("ident_ready"), q.sem("we_turned"), q.sem("we_kept")
            vr, vs, used = q.sem("vte_made"), q.sem("vte_kept"), q.sem("edges_used")
            ch, recr, rst, ar, rz = q.sem("dve_steps"), q.sem("rec_ready"), q.sem("rec_stored"), q.sem("att_spread"), q.sem("rec_zeroed")
            block = q.block()
            e_v = a["edge_attr_128"].rearrange("(g k p) d -> g p k d", k=KT, p=P)

            @block.sync
            def _(sp):
                for n, name in enumerate(("dst", "src", "edge_type_5")):
                    sp.dma_start(raw[:, n, :], a[name]).then_inc(ld, 16)
                sp.dma_start(len16[:, :, :], a["edge_attr_16"]).then_inc(ld, 16)
                sp.dma_start(sh4[:, :, :], a["edge_attr_4"]).then_inc(ld, 16)
                sp.dma_start(we[:, :, :], a["L0_gnn_We"].rearrange("l i j -> i l j")).then_inc(ld, 16)
                sp.dma_start(att[:, :], a["L0_gnn_att_edge"]).then_inc(ld, 16)
                for g in range(2):
                    sp.dma_start(ea[:, g, :, :], e_v[g]).then_inc(eld[g], 16)
                with sp.Fori(0, (G - 3) // 2) as i:
                    for j in range(2):
                        sp.wait_ge(used, i * 2 + j + 1)
                        sp.dma_start(ea[:, j, :, :], e_v[bass.ds(i * 2 + 2 + j, 1)].rearrange("g p k d -> (g p) k d")).then_inc(eld[j], 16)
                sp.wait_ge(used, G - 2)
                sp.dma_start(ea[:, 0, :, :], e_v[G - 1]).then_inc(eld[0], 16)
                sp.wait_ge(recr, 1)
                sp.dma_start(rec_d.rearrange("(c p) w -> p c w", p=P), rec[:, :, :]).then_inc(rst, 16)
                sp.wait_ge(rst, 16)

            @block.scalar
            def _(act):
                act.wait_ge(zs, 1)
                z_v = agg.rearrange("(r p n) w -> r p (n w)", p=P, n=zn)
                for r in range(NP // P // zn):
                    act.dma_start(z_v[r], zero[:, :]).then_inc(zst, 16)
                act.dma_start(pre.rearrange("(p n) w -> p (n w)", p=P), zero[:, 0:NP // P * 8]).then_inc(zst, 16)
                act.wait_ge(wt, 1)
                act.activation(wet[:, :, :].rearrange("p l d -> p (l d)"), pst[:, :], ACT.Copy).then_inc(wts, 1)
                act.wait_ge(vr, 1)
                act.activation(vte[:, :, :].rearrange("p l d -> p (l d)"), psv[:, :], ACT.Copy).then_inc(vs, 1)
                act.wait_ge(zst, 16 * (NP // P // zn + 1))

            @block.gpsimd
            def _(pool):
                pool.memset(ident[:, :], 0.0).then_inc(idr, 1)
                pool.wait_ge(idr, 1)
                pool.affine_select(out=ident[:, :], in_=ident[:, :], compare_op=ALU.not_equal, fill=1.0,
                                   base=0, pattern=[[-1, P]], channel_multiplier=1).then_inc(idr, 1)
                pool.iota(self.iota_f[:, :], [[1, P]], base=0, channel_multiplier=0, allow_small_or_imprecise_dtypes=True)
                pool.memset(self.mhalf[:, :], -0.5)
                pool.memset(self.neg1[:, :], -1.0)
                pool.memset(self.eps_t[:, :], LN_EPS)

            @block.tensor
            def _(pe):
                pe.wait_ge(idr, 2)
                pe.wait_ge(ld, 16 * 7)
                for l in range(4):
                    mm = pe.transpose(pst[:, l * D:(l + 1) * D], we[:, l, :], ident[:, :])
                mm.then_inc(wt, 1)
                pe.wait_ge(wts, 1)
                pe.wait_ge(ar, 1)
                for l in range(4):
                    mm = pe.matmul(psv[:, l * D:(l + 1) * D], attb[:, l, :], wet[:, l, :], start=True, stop=True)
                mm.then_inc(vr, 1)

            @block.vector
            def _(v):
                v.memset(zero[:, :], 0.0).then_inc(zs, 1)
                v.memset(rec[:, :, :], 0.0).then_inc(rz, 1)
                v.wait_ge(ld, 16 * 7)
                v.tensor_copy(attb[:, :, :], fan(att[:, :], P)).then_inc(ar, 1)
                v.wait_ge(rz, 1)
                for n, r in enumerate((R_DST, R_SRC, R_TYPE)):
                    v.tensor_copy(rec[:, :, r], raw[:, n, :])
                v.tensor_copy(rec[:, :, R_SH:R_SH + 4], sh4[:, :, :])
                v.tensor_copy(rec[:, :, R_LEN:R_LEN + 16], len16[:, :, :])
                v.wait_ge(vs, 1)

                def group(g, j, n, st):
                    v.wait_ge(eld[j], n)
                    if not isinstance(g, int) or g >= 2:
                        v.wait_ge(used, g - 1)
                    for k in range(KT):
                        for l in range(4):
                            m = st.mark(v.tensor_tensor_reduce(junk[:, j, 4 * k + l, :], ea[:, j, k, :], vte[:, l, :], 1.0, 0.0,
                                                               ALU.mult, ALU.add, dots[:, j, k, l:l + 1]))
                    st.need(m)
                    v.tensor_copy(rec[:, bass.ds(g * KT, KT), R_TE:R_TE + 4], dots[:, j]).then_inc(used, 1)

                def pair(i):
                    st = Chain(v, ch, i, 8 * KT)
                    for j in range(2):
                        group(i * 2 + j, j, (i + 1) * 16, st)
                    st.close()

                pair(0)
                with v.Fori(1, (G - 1) // 2) as i:
                    pair(i)
                group(G - 1, 0, ((G - 1) // 2 + 1) * 16, Chain(v, ch, (G - 1) // 2, 8 * KT))
                v.wait_ge(used, G)
                v.drain().then_inc(recr, 1)

    def order(self):
        a, C, G, ident, rec_d = self.a, self.C, self.G, self.ident, self.rec_d
        moved = self.dram("records_moved", (C * P, REC))
        with Pass(self.nc, "order") as q:
            pair_i = q.sb("pair_i", [P, 2, C], I32)
            pair = q.sb("pair", [P, 3, C])
            drops = q.sb("drops", [P, 1])
            ones = q.sb("ones", [P, 1])
            flag = q.sb("flag", [1, 1], I32)
            own_i = q.sb("own_i", [P, C], I32)
            own = q.sb("own", [P, C])
            number = q.sb("number", [P, C])
            rank = q.sb("rank", [P, C])
            rank_i = q.sb("rank_i", [P, C], U32)
            local = q.sb("local", [P, BLOCK])
            row_i = q.sb("row_i", [P, BLOCK], I32)
            row = q.sb("row", [P, BLOCK])
            before = q.sb("before", [P, BLOCK])
            hit = q.sb("hit", [P, 2, BLOCK])
            got = q.sb("got", [P, 1])
            rec = q.sb("rec", [P, REC])
            ix = q.sb("ix", [P, 1], U32)
            pd = q.ps("drops_sum")
            ld, on, io, dr, dm, fl = (q.sem(n) for n in ("loaded", "ones_ready", "numbers_ready", "drops_ready", "drops_summed", "flag_ready"))
            row_in, row_used, ch, ixr, rec_in, put, gate, mvd, num, vgate = (q.sem(n) for n in ("row_in", "row_used", "steps", "index_ready", "record_in",
                                                                                   "record_put", "gate", "records_moved", "numbers_less", "vector_gate"))
            block = q.block()

            @block.sync
            def _(sp):
                for o in range(2):
                    sp.dma_start(pair_i[:, o, :], a["dst_rows"][o:o + C * P].rearrange("(p c) -> p c", c=C)).then_inc(ld, 16)
                sp.dma_start(own_i[:, :], a["dst"]).then_inc(ld, 16)
                sp.wait_ge(fl, 1)
                unordered = sp.value_load(flag[0:1, 0:1], min_val=0, max_val=1)
                with sp.If(unordered > 0):
                    with sp.Fori(0, G) as g:
                        sp.wait_ge(row_used, g + 1)
                        sp.dma_start(row_i[:, :], a["dst_rows"][bass.ds(g * BLOCK, BLOCK)].partition_broadcast(P)).then_inc(row_in, 16)

                    def bring(c):
                        sp.wait_ge(put, c * 16)
                        sp.dma_start(rec[:, :], rec_d[bass.ds(c * P, P), :]).then_inc(rec_in, 16)

                    bring(0)
                    with sp.Fori(1, C) as c:
                        bring(c)
                    sp.wait_ge(put, C * 16)
                    sp.dma_start(rec_d.rearrange("(n p) w -> p n w", p=P), moved.rearrange("(n p) w -> p n w", p=P)).then_inc(mvd, 16)
                    sp.wait_ge(mvd, 16)

            @block.gpsimd
            def _(pool):
                pool.memset(ones[:, :], 1.0).then_inc(on, 1)
                pool.iota(number[:, :], [[P, C]], base=0, channel_multiplier=1, allow_small_or_imprecise_dtypes=True).then_inc(io, 1)
                pool.iota(local[:, :], [[1, BLOCK]], base=0, channel_multiplier=0, allow_small_or_imprecise_dtypes=True).then_inc(io, 1)
                bound = pool.to_reg(C * P - 1)
                pool.wait_ge(fl, 1)
                unordered = pool.value_load(flag[0:1, 0:1], min_val=0, max_val=1)
                with pool.If(unordered > 0):
                    with pool.Fori(0, C) as c:
                        pool.wait_ge(ixr, c + 1)
                        pool.sem_inc(gate, 1)
                        pool.wait_ge(rec_in, c * 16 + 16)
                        pool.sem_inc(gate, 1)
                        pool.indirect_dma_start(moved, bass.IndirectOffsetOnAxis(ix[:, 0:1], 0), rec[:, :], None,
                                                bounds_check=bound, oob_is_err=False).then_inc(put, 16)

            @block.tensor
            def _(pe):
                pe.wait_ge(on, 1)
                pe.wait_ge(dr, 1)
                pe.matmul(pd[0:1, 0:1], drops[:, :], ones[:, :], start=True, stop=True).then_inc(dm, 1)

            @block.vector
            def _(v):
                v.wait_ge(ld, 48)
                st = Chain(v, ch, 0, 10)
                v.tensor_copy(own[:, :], own_i[:, :])
                st.run(v.tensor_copy(pair[:, 0:2, :], pair_i[:, :, :]))
                st.run(v.tensor_tensor(pair[:, 2, :], pair[:, 0, :], pair[:, 1, :], ALU.is_gt))
                v.tensor_reduce(drops[:, :], pair[:, 2, :], AX_X, ALU.max).then_inc(dr, 1)
                v.wait_ge(dm, 1)
                v.wait_ge(io, 2)
                st.run(v.tensor_scalar(drops[0:1, :], pd[0:1, 0:1], 1.0, None, ALU.min))
                v.tensor_copy(flag[:, :], drops[0:1, :]).then_inc(fl, 1)
                st.run(v.memset(rank[:, :], 0.0))
                v.wait_ge(fl, 1)
                st.close()
                v.wait_ge(ch, 10)
                unordered = v.value_load(flag[0:1, 0:1], min_val=0, max_val=1)
                with v.If(unordered > 0):
                    v.sem_inc(row_used, 1)
                    with v.Fori(0, G) as g:
                        v.wait_ge(row_in, g * 16 + 16)
                        v.tensor_copy(row[:, :], row_i[:, :]).then_inc(row_used, 1)
                        v.wait_ge(row_used, g + 2)
                        v.sem_inc(vgate, 1)
                        with v.Fori(0, C) as c:
                            st = Chain(v, ch, g * C + c, 5)
                            st.base = st.base + 10
                            d_, n_, r_ = own[:, bass.ds(c, 1)], number[:, bass.ds(c, 1)], rank[:, bass.ds(c, 1)]
                            st.run(v.tensor_scalar(before[:, :], local[:, :], n_, None, ALU.is_lt))
                            st.mark(v.scalar_tensor_tensor(hit[:, 0, :], row[:, :], d_, before[:, :], ALU.is_equal, ALU.mult))
                            st.run(v.tensor_scalar(hit[:, 1, :], row[:, :], d_, None, ALU.is_lt))
                            st.run(v.tensor_reduce(got[:, :], hit[:, :, :].rearrange("p a n -> p (a n)"), AX_X, ALU.add))
                            st.run(v.tensor_tensor(r_, r_, got[:, :], ALU.add))
                        v.tensor_scalar(number[:, :], number[:, :], float(-BLOCK), None, ALU.add).then_inc(num, 1)
                        v.wait_ge(num, g + 1)
                    v.tensor_copy(rank_i[:, :], rank[:, :]).then_inc(fl, 1)
                    v.wait_ge(fl, 2)

                    def index(c):
                        v.wait_ge(put, c * 16)
                        v.tensor_copy(ix[:, :], rank_i[:, bass.ds(c, 1)]).then_inc(ixr, 1)

                    index(0)
                    with v.Fori(1, C) as c:
                        index(c)

    def graph(self):
        C, G, HALF, ident, rec_d, dst_d = self.C, self.G, self.HALF, self.ident, self.rec_d, self.dst_d
        with Pass(self.nc, "graph") as q:
            rec = q.sb("rec", [P, C, REC])
            dcol = q.sb("dcol", [P, C])
            drow = q.sb("drow", [HALF, 3, 2, P])
            flag = q.sb("flag", [HALF, 3, 2])
            edge_row = q.sb("edge_row", [1, 4, C])
            row_f = q.sb("row_f", [1, 3, C])
            put_r = q.sb("put_r", [HALF, 2, P])
            last_col = q.sb("last_col", [HALF, 2, P])
            sent = q.sb("sent", [1, 1])
            wide = q.sb("wide", [P, 2, KT * P])
            psr, psc, psl = q.ps("rows"), q.ps("cols"), q.ps("reach_t")
            ld, rt, rk, dst_st, dl, el = q.sem("loaded"), q.sem("rows_turned"), q.sem("rows_kept"), q.sem("dst_stored"), q.sem("neighbours_in"), q.sem("edge_row_in")
            dc, pr, pt, wl, wu, sr, ch = q.sem("dcol_ready"), q.sem("put_ready"), q.sem("put_turned"), q.sems("wide_in", 2), q.sem("wide_used"), q.sem("sent_ready"), q.sem("steps")
            lr = q.sem("reach_ready")
            block = q.block()
            body = dst_d[1:1 + C * P]

            def shifted(o):
                return dst_d[o:o + C * P].rearrange("(g r p) -> r g p", g=2, p=P)

            @block.sync
            def _(sp):
                sp.dma_start(rec[:, :, :], rec_d.rearrange("(c p) w -> p c w", p=P)).then_inc(ld, 16)
                sp.wait_ge(rk, 1)
                sp.wait_ge(sr, 1)
                sp.dma_start(shifted(1), drow[:, 1, :, :]).then_inc(dst_st, 16)
                for o in (0, C * P + 1):
                    sp.dma_start(dst_d[o:o + 1].unsqueeze(0), sent[:, :]).then_inc(dst_st, 16)
                sp.wait_ge(dst_st, 48)
                for o in (0, 2):
                    sp.dma_start(drow[:, o, :, :], shifted(o)).then_inc(dl, 16)
                for n, o in enumerate((0, 1, P, P + 1)):
                    last = dst_d[o:o + (C - 1) * P + 1:P].unsqueeze(0)
                    sp.dma_start(edge_row[:, n, :].unsqueeze(2), last.unsqueeze(2), allow_slow_non_contiguous=True).then_inc(el, 16)
                for j in range(2):
                    sp.dma_start(wide[:, j, :], body[j * BLOCK:(j + 1) * BLOCK].partition_broadcast(P)).then_inc(wl[j], 16)
                with sp.Fori(0, (G - 3) // 2) as i:
                    for j in range(2):
                        sp.wait_ge(wu, i * 2 + j + 1)
                        sp.dma_start(wide[:, j, :], body[bass.ds((i * 2 + 2 + j) * BLOCK, BLOCK)].partition_broadcast(P)).then_inc(wl[j], 16)
                sp.wait_ge(wu, G - 2)
                sp.dma_start(wide[:, 0, :], body[(G - 1) * BLOCK:].partition_broadcast(P)).then_inc(wl[0], 16)

            @block.tensor
            def _(pe):
                pe.wait_ge(dc, 1)
                for g in range(2):
                    mm = pe.transpose(psr[0:HALF, g * P:(g + 1) * P], dcol[:, g * HALF:(g + 1) * HALF], ident[:, :])
                mm.then_inc(rt, 1)
                pe.wait_ge(pr, 1)
                for g in range(2):
                    mm = pe.transpose(psc[:, g * HALF:(g + 1) * HALF], put_r[:, g, :], ident[0:HALF, 0:HALF])
                mm.then_inc(pt, 1)
                pe.wait_ge(lr, 1)
                for g in range(2):
                    mm = pe.transpose(psl[:, g * HALF:(g + 1) * HALF], last_col[:, g, :], ident[0:HALF, 0:HALF])
                mm.then_inc(pt, 1)

            @block.vector
            def _(v):
                st = Chain(v, ch, 0, 100)
                v.memset(sent[:, :], -1.0).then_inc(sr, 1)
                v.wait_ge(ld, 16)
                v.tensor_copy(dcol[:, :], rec[:, :, R_DST]).then_inc(dc, 1)
                v.tensor_copy(self.dst_i[:, :], rec[:, :, R_DST])
                v.tensor_copy(self.src_i[:, :], rec[:, :, R_SRC])
                v.tensor_copy(self.typ[:, :], rec[:, :, R_TYPE])
                v.tensor_copy(self.te[:, :, :], rec[:, :, R_TE:R_TE + 4].rearrange("p c l -> p l c"))
                v.wait_ge(rt, 1)
                v.tensor_copy(drow[:, 1, :, :].rearrange("r g p -> r (g p)"), psr[0:HALF, 0:2 * P]).then_inc(rk, 1)
                v.wait_ge(rk, 1)
                v.wait_ge(dl, 32)
                v.wait_ge(el, 64)
                st.run(v.tensor_tensor(put_r[:, :, :], drow[:, 1], drow[:, 2], ALU.is_equal))
                st.run(v.scalar_tensor_tensor(put_r[:, :, :].rearrange("r g p -> r (g p)"), put_r[:, :, :].rearrange("r g p -> r (g p)"),
                                              float(SKIP), drow[:, 1].rearrange("r g p -> r (g p)"), ALU.mult, ALU.add))
                v.sem_inc(pr, 1)
                for d, o in ((0, 0), (1, 2)):
                    st.run(v.tensor_tensor(self.pen[:, d], drow[:, 1], drow[:, o], ALU.is_equal))
                    st.run(v.tensor_tensor(flag[:, d, :].unsqueeze(2), drow[:, 1, :, (0, P - 1)[d]].unsqueeze(2),
                                           drow[:, o, :, (0, P - 1)[d]].unsqueeze(2), ALU.is_equal))
                    for g in range(2):
                        e = (0, P - 1)[d]
                        st.run(v.tensor_scalar(self.pen_carry[:, d, g, :], drow[:, 1, g, :], drow[:, 1, g, e:e + 1],
                                               flag[:, d, g:g + 1], ALU.is_equal, ALU.mult))
                    if d == 0:
                        st.run(v.memset(last_col[:, :, :], 0.0))
                        for g in range(2):
                            last = v.tensor_reduce(last_col[:, g, P - 1:P], self.pen_carry[:, 0, g, :], AX_X, ALU.add)
                        last.then_inc(lr, 1)
                    for t in (self.pen, self.pen_carry):
                        st.run(v.tensor_scalar(t[:, d], t[:, d], -1.0, BIG, ALU.add, ALU.mult))
                for n, (x, y) in enumerate(((0, 1), (3, 2), (1, 2))):
                    st.run(v.tensor_tensor(row_f[:, n, :], edge_row[:, x, :], edge_row[:, y, :], ALU.is_equal))
                for d in range(2):
                    st.run(v.tensor_tensor(self.pen_row[:, d, :], row_f[:, d, :], row_f[:, 2, :], ALU.mult))
                    st.run(v.tensor_scalar(self.pen_row[:, d, :], self.pen_row[:, d, :], -1.0, BIG, ALU.add, ALU.mult))
                v.wait_ge(pt, 2)
                v.tensor_copy(self.put_i[:, :], psc[:, 0:C])
                v.tensor_copy(self.reach[:, :], psl[:, 0:C])

                def group(g, j, n):
                    v.wait_ge(wl[j], n)
                    for k in range(KT):
                        last = v.tensor_scalar(self.same[:, bass.ds((g * KT + k) * P, P)], wide[:, j, k * P:(k + 1) * P],
                                               dcol[:, bass.ds(g * KT + k, 1)], None, ALU.is_equal)
                    last.then_inc(wu, 1)

                with v.Fori(0, (G - 1) // 2) as i:
                    for j in range(2):
                        group(i * 2 + j, j, (i + 1) * 16)
                group(G - 1, 0, ((G - 1) // 2 + 1) * 16)

    def counts(self):
        NCOL = self.NCOL
        with Pass(self.nc, "cnt") as q:
            s = q.sb("s", [P, NCOL, 8])
            c1 = q.sb("c1", [P, NCOL])
            ld, ch = q.sem("loaded"), q.sem("steps")
            block = q.block()

            @block.sync
            def _(sp):
                sp.dma_start(s[:, :, :].rearrange("p (b k) w -> p b (k w)", k=KT),
                             self.pre.rearrange("(b p k) w -> p b (k w)", p=P, k=KT)).then_inc(ld, 16)

            @block.vector
            def _(v):
                st = Chain(v, ch, 0, 100)
                v.wait_ge(ld, 16)
                st.run(v.tensor_scalar(self.no_edge[:, :], s[:, :, 4], 0.0, None, ALU.is_equal))
                st.run(v.tensor_scalar(c1[:, :], s[:, :, 4], 1.0, None, ALU.max))
                st.run(v.reciprocal(self.inv_cnt[:, :], c1[:, :]))
                for l in range(4):
                    st.run(v.tensor_tensor(self.tmean[:, l, :], s[:, :, l], self.inv_cnt[:, :], ALU.mult))

    def self_loops(self, l):
        NCOL = self.NCOL
        with Pass(self.nc, f"loop{l}") as q:
            t = q.sb("t", [P, NCOL])
            au = q.sb("au", [P, NCOL, 2])
            ch, st_ = q.sem("steps"), q.sem("stored")
            block = q.block()

            @block.vector
            def _(v):
                st = Chain(v, ch, 0, 4)
                v.tensor_copy(au[:, :, 0], self.asad[:, :, 1])
                st.run(v.tensor_tensor(t[:, :], self.asad[:, :, 0], self.asad[:, :, 1], ALU.add))
                st.run(v.tensor_tensor(t[:, :], t[:, :], self.tmean[:, l, :], ALU.add))
                st.run(v.scalar_tensor_tensor(au[:, :, 1], t[:, :], NEG_SLOPE, t[:, :], ALU.mult, ALU.max))
                v.drain().then_inc(ch, 1)

            @block.sync
            def _(sp):
                sp.wait_ge(ch, 4)
                sp.dma_start(self.aux.rearrange("(b p k) w -> p b (k w)", p=P, k=KT),
                             au[:, :, :].rearrange("p (b k) w -> p b (k w)", k=KT)).then_inc(st_, 16)
                sp.wait_ge(st_, 16)

    def attention(self, l):
        C, G, HALF, ident = self.C, self.G, self.HALF, self.ident
        with Pass(self.nc, f"att{l}") as q:
            H = q.sb("H", [P, C, AW])
            auxE = q.sb("auxE", [P, C, 2])
            lg = q.sb("lg", [P, C])
            cand = q.sb("cand", [P, C])
            pw = q.sb("pw", [P, C])
            pl = q.sb("pl", [P, C])
            with Pass(self.nc, f"gather{l}") as g_:
                hr = g_.sb("hr", [P, KT, AW])
                ar = g_.sb("ar", [P, KT, 2])
                ix = g_.sb("ix", [P, KT, 2], U32)
                gh, ga = g_.sems("h_in", KT), g_.sems("aux_in", KT)
                ixr, hk, ak, gate = g_.sem("index_ready"), g_.sem("h_kept"), g_.sem("aux_kept"), g_.sem("gate")
                block = g_.block()

                @block.gpsimd
                def _(pool):
                    bound = pool.to_reg(self.NP - 1)
                    def body(i):
                        for k in range(KT):
                            pool.wait_ge(ixr, i * KT + k + 1)
                            pool.sem_inc(gate, 1)
                            pool.wait_ge(hk, i * KT + k)
                            pool.sem_inc(gate, 1)
                            pool.wait_ge(ak, i * KT + k)
                            pool.sem_inc(gate, 1)
                            pool.indirect_dma_start(hr[:, k, :], None, self.table, bass.IndirectOffsetOnAxis(ix[:, k, 0:1], 0),
                                                    bounds_check=bound, oob_is_err=False).then_inc(gh[k], 16)
                            pool.indirect_dma_start(ar[:, k, :], None, self.aux, bass.IndirectOffsetOnAxis(ix[:, k, 1:2], 0),
                                                    bounds_check=bound, oob_is_err=False).then_inc(ga[k], 16)

                    body(0)
                    with pool.Fori(1, G) as i:
                        body(i)

                @block.scalar
                def _(act):
                    act.sem_inc(hk, KT - 1)
                    with act.Fori(0, G) as i:
                        for k in range(KT):
                            act.wait_ge(gh[k], i * 16 + 16)
                            act.activation(H[:, bass.ds(i * KT + k, 1), :], hr[:, k:k + 1, :], ACT.Copy).then_inc(hk, 1)

                @block.vector
                def _(v):
                    def index(c, k):
                        v.tensor_copy(ix[:, k, 0:1], self.src_i[:, bass.ds(c, 1)])
                        v.tensor_copy(ix[:, k, 1:2], self.dst_i[:, bass.ds(c, 1)]).then_inc(ixr, 1)

                    def body(i, last):
                        for k in range(KT):
                            v.wait_ge(ga[k], i * 16 + 16)
                            v.wait_ge(gh[k], i * 16 + 16)
                            if not last:
                                index(i * KT + KT + k, k)
                            v.tensor_copy(auxE[:, bass.ds(i * KT + k, 1), :], ar[:, k:k + 1, :]).then_inc(ak, 1)

                    v.sem_inc(ak, KT - 1)
                    for k in range(KT):
                        index(k, k)
                    with v.Fori(0, G - 1) as i:
                        body(i, False)
                    body(G - 1, True)

            with Pass(self.nc, f"soft{l}") as s_:
                lt = s_.sb("lt", [HALF, 2, P])
                F = s_.sb("F", [HALF, 2, 2, P])
                ends = s_.sb("ends", [HALF, 4])
                erow = s_.sb("erow", [1, 2, C])
                crow = s_.sb("crow", [1, 2, C + 2])
                ccol = s_.sb("ccol", [HALF, 4])
                one = s_.sb("one", [1, 2])
                psa, psb, psc, psd = (s_.ps(n) for n in ("a", "b", "c", "d"))
                ch, pe_s, ex, dn = s_.sem("steps"), s_.sem("turned"), s_.sem("exps"), s_.sem("weights_shifted")
                block = s_.block()

                @block.vector
                def _(v):
                    st = Chain(v, ch, 0, 100)
                    v.memset(one[:, :], 1.0)
                    v.memset(crow[:, :, :], -BIG)
                    st.run(v.tensor_tensor(lg[:, :], H[:, :, D], auxE[:, :, 0], ALU.add))
                    st.run(v.tensor_tensor(lg[:, :], lg[:, :], self.te[:, l, :], ALU.add))
                    st.run(v.scalar_tensor_tensor(lg[:, :], lg[:, :], NEG_SLOPE, lg[:, :], ALU.mult, ALU.max))
                    st.run(v.tensor_tensor(cand[:, :], lg[:, :], auxE[:, :, 1], ALU.max))
                    v.memset(H[:, :, D:D + 1], 1.0)
                    v.wait_ge(pe_s, 1)
                    st.run(v.tensor_copy(lt[:, :, :].rearrange("r g p -> r (g p)"), psa[0:HALF, 0:2 * P]))
                    for g in range(2):
                        v.tensor_tensor_scan(F[:, 0, g, :], self.pen[:, 0, g, :], lt[:, g, :], -BIG, ALU.add, ALU.max)
                        st.run(v.tensor_tensor_scan(backward(F[:, 1, g, :]), backward(self.pen[:, 1, g, :]), backward(lt[:, g, :]),
                                                    -BIG, ALU.add, ALU.max))
                    st.run(v.tensor_copy(ends[:, 0:2], F[:, 0, :, P - 1]))
                    st.run(v.tensor_copy(ends[:, 2:4], F[:, 1, :, 0]))
                    v.wait_ge(pe_s, 2)
                    st.run(v.tensor_copy(erow[:, :, :].rearrange("o d c -> o (d c)"), psb[0:1, 0:2 * C]))
                    v.tensor_tensor_scan(crow[:, 0, 1:C + 1], self.pen_row[:, 0, :], erow[:, 0, :], -BIG, ALU.add, ALU.max)
                    st.run(v.tensor_tensor_scan(backward(crow[:, 1, 0:C]), backward(self.pen_row[:, 1, :]), backward(erow[:, 1, :]),
                                                -BIG, ALU.add, ALU.max))
                    v.wait_ge(pe_s, 3)
                    st.run(v.tensor_copy(ccol[:, :], psc[0:HALF, 0:4]))
                    for d in range(2):
                        for g in range(2):
                            st.run(v.scalar_tensor_tensor(F[:, d, g, :], self.pen_carry[:, d, g, :], ccol[:, 2 * d + g:2 * d + g + 1],
                                                          F[:, d, g, :], ALU.add, ALU.max))
                    st.run(v.tensor_tensor(lt[:, :, :], F[:, 0], F[:, 1], ALU.max))
                    v.wait_ge(pe_s, 4)
                    v.tensor_tensor(pw[:, :], lg[:, :], psd[:, 0:C], ALU.subtract)
                    v.tensor_tensor(pl[:, :], auxE[:, :, 1], psd[:, 0:C], ALU.subtract).then_inc(dn, 1)

                @block.tensor
                def _(pe):
                    pe.wait_ge(ch, 4)
                    for g in range(2):
                        mm = pe.transpose(psa[0:HALF, g * P:(g + 1) * P], cand[:, g * HALF:(g + 1) * HALF], ident[:, :])
                    mm.then_inc(pe_s, 1)
                    pe.wait_ge(ch, 9)
                    for n in range(4):
                        mm = pe.matmul(psb[0:1, n * HALF:(n + 1) * HALF], ends[:, n:n + 1], ident[0:HALF, 0:HALF], start=True, stop=True)
                    mm.then_inc(pe_s, 1)
                    pe.wait_ge(ch, 11)
                    for d in range(2):
                        for g in range(2):
                            o = g * HALF + d
                            mm = pe.matmul(psc[0:HALF, 2 * d + g:2 * d + g + 1], crow[:, d, o:o + HALF], one[:, 0:1], start=True, stop=True)
                    mm.then_inc(pe_s, 1)
                    pe.wait_ge(ch, 17)
                    for g in range(2):
                        mm = pe.transpose(psd[:, g * HALF:(g + 1) * HALF], lt[:, g, :], ident[0:HALF, 0:HALF])
                    mm.then_inc(pe_s, 1)

                @block.scalar
                def _(act):
                    act.wait_ge(dn, 1)
                    act.activation(pw[:, :], pw[:, :], ACT.Exp)
                    act.activation(pl[:, :], pl[:, :], ACT.Exp)

            self.edge_pass(f"sum{l}", "gat", H, l, weights=pw, loop_w=pl)

    def edge_pass(self, name, kind, table, layer, weights=None, loop_w=None):
        nc, a, C, G, ident = self.nc, self.a, self.C, self.G, self.ident
        gathers = kind in ("rel", "sage", "tp")
        two_step = gathers
        side = kind in ("rel", "tp")
        halves = 2 if kind == "tp" else 1
        W = {"pre": 5, "gat": D + 1, "rel": D, "sage": D, "tp": D + 1}[kind]
        OW = 8 if kind == "pre" else AW
        dest = self.pre if kind == "pre" else self.agg
        with Pass(nc, name) as q:
            outs = q.sb("outs", [P, KT, OW])
            sf = q.sb("sf", [P, KT, P])
            link = q.sb("link", [P, KT, P])
            pix = q.sb("pix", [P, KT], U32)
            pso = [q.ps(f"o{k}") for k in range(2)]
            if kind == "pre":
                m5 = q.sb("m5", [P, KT, 8])
            if gathers:
                gr = q.sb("gr", [P, KT, D])
                gix = q.sb("gix", [P, KT], U32)
                msg = q.sb("msg", [P, KT, 2 if kind == "tp" else 1, D])
                aT = q.sb("aT", [P, 2, halves * P])
                Wm = q.sb("Wm", [P, halves, W])
                psa = [q.ps(f"a{k}") for k in range(2)]
            if kind == "rel":
                relb = q.sb("relb", [KT * 8, KT * D])
                iota8 = q.sb("iota8", [P, 8])
                sd = q.sb("sd", [P, KT * 8])
                sdT = q.sb("sdT", [KT * 8, P])
                psr, pst = q.ps("rel"), q.ps("sideT")
                sw = KT * 8
            if kind == "tp":
                rec = q.sb("rec", [P, C, REC])
                sd = q.sb("sd", [P, KT * 16])
                sdT = q.sb("sdT", [KT * 16, P])
                W1 = q.sb("W1", [KT * 16, KT, 64])
                W2 = q.sb("W2", [64, D + 64])
                hs = q.sb("hs", [64, KT, P])
                tA = q.sb("tA", [P, 2, D])
                psh, pst = q.ps("hid"), q.ps("wexp")
                sw = KT * 16
            gin, sst = q.sems("rows_in", KT), q.sems("sums_stored", KT)
            gixr, gate, pgate = q.sem("gather_index"), q.sem("gate"), q.sem("tensor_gate")
            sfr, linkr, msgr, turned, kept = q.sem("same_ready"), q.sem("link_ready"), q.sem("messages"), q.sem("sums_turned"), q.sem("turned_kept")
            outm, evac = q.sem("sums_made"), q.sem("sums_out")
            extra, cst, ch, added = q.sem("last_columns"), q.sem("constants"), q.sem("dve_steps"), q.sem("relation_added")
            sdr, sdt, sdk, relm, hidm, hidk, wxm, init = (q.sem(n) for n in ("side_ready", "side_turned", "side_kept", "relations",
                                                                           "hidden_made", "hidden_kept", "weights_made", "cleared"))
            block = q.block()

            @block.sync
            def _(sp):
                n = 0
                if kind == "rel":
                    sp.dma_start(relb[:, :], a["L1_gnn_relvecs"][layer]).then_inc(cst, 16)
                    sp.dma_start(Wm[:, 0, :], a["L1_gnn_lin_w"][layer]).then_inc(cst, 16)
                    sp.dma_start(iota8[:, :], a["iota8"]).then_inc(cst, 16)
                if kind == "sage":
                    sp.dma_start(Wm[:, 0, :], a[f"L2_gnn_Wn{layer}"]).then_inc(cst, 16)
                if kind == "tp":
                    sp.dma_start(rec[:, :, :], self.rec_d.rearrange("(c p) w -> p c w", p=P)).then_inc(cst, 16)
                    sp.dma_start(W1[:, :, :], a["L3_gnn_W_mlp1"]).then_inc(cst, 16)
                    sp.dma_start(W2[:, :], a["L3_gnn_W_mlp2"]).then_inc(cst, 16)
                    sp.dma_start(Wm[:, :, :], a["L3_out"]).then_inc(cst, 16)

            cleared = 2 if kind == "pre" else 1
            n_cst = {"rel": 3, "sage": 1, "tp": 4}.get(kind, 0) * 16

            @block.gpsimd
            def _(pool):
                bound_g, bound_s = pool.to_reg(self.NP - 1), pool.to_reg(self.NP - 1)

                def gather(cnt, k):
                    pool.wait_ge(gixr, cnt + 1)
                    pool.sem_inc(gate, 1)
                    if not isinstance(cnt, int) or cnt >= KT:
                        if kind == "sage":
                            pool.wait_ge(turned, cnt)
                        else:
                            pool.wait_ge(msgr, cnt - 3)
                        pool.sem_inc(gate, 1)
                    pool.indirect_dma_start(gr[:, k, :], None, table, bass.IndirectOffsetOnAxis(gix[:, k:k + 1], 0),
                                            bounds_check=bound_g, oob_is_err=False).then_inc(gin[k], 16)

                def scatter(cnt, k):
                    pool.wait_ge(extra, cnt + 1)
                    pool.sem_inc(gate, 1)
                    pool.wait_ge(evac, cnt + 3)
                    pool.sem_inc(gate, 1)
                    pool.indirect_dma_start(dest, bass.IndirectOffsetOnAxis(pix[:, k:k + 1], 0), outs[:, k, :], None,
                                            bounds_check=bound_s, oob_is_err=False).then_inc(sst[k], 16)

                if gathers:
                    for k in range(3):
                        gather(k, k)

                    def both(i):
                        for k in range(KT):
                            gather(i * KT + k + 3, (k + 3) % KT)
                            scatter(i * KT + k, k)

                    both(0)
                    with pool.Fori(1, G - 1) as i:
                        both(i)
                    gather(C - 1, KT - 1)
                    for k in range(KT):
                        scatter(C - KT + k, k)
                else:
                    with pool.Fori(0, G) as i:
                        for k in range(KT):
                            scatter(i * KT + k, k)
                for k in range(KT):
                    pool.wait_ge(sst[k], 16 * G)

            @block.vector
            def _(v):
                v.memset(outs[:, :, :], 0.0).then_inc(init, 1)
                if kind == "pre":
                    v.memset(m5[:, :, :], 1.0).then_inc(init, 1)
                v.wait_ge(init, cleared)
                if n_cst:
                    v.wait_ge(cst, n_cst)
                if kind == "tp":
                    v.tensor_scalar(Wm[:, :, :], Wm[:, :, :], 1.0 / 8 / 4 / 8, None, ALU.mult).then_inc(init, 1)
                    v.wait_ge(init, 2)
                    v.tensor_scalar(Wm[0:MUL, 1, :], Wm[0:MUL, 1, :], 3.0 ** -0.5, None, ALU.mult).then_inc(init, 1)
                    v.wait_ge(init, 3)

                def g_index(c, k):
                    v.tensor_copy(gix[:, k:k + 1], self.src_i[:, bass.ds(c, 1)]).then_inc(gixr, 1)

                def side_of(g):
                    if kind == "rel":
                        v.tensor_tensor(sd[:, :].rearrange("p (k t) -> p k t", k=KT), fan(self.typ[:, bass.ds(g * KT, KT)], 8),
                                        spread(iota8[:, :], KT), ALU.is_equal).then_inc(sdr, 1)
                    else:
                        v.tensor_copy(sd[:, :].rearrange("p (k t) -> p k t", k=KT),
                                      rec[:, bass.ds(g * KT, KT), R_LEN:R_LEN + 16]).then_inc(sdr, 1)

                PER = 4 * KT

                def body(i, last):
                    st = Chain(v, ch, i, PER) if kind == "tp" else None
                    for k in range(KT):
                        c = i * KT + k
                        if gathers:
                            v.wait_ge(gin[k], i * 16 + 16)
                            if not last:
                                g_index(c + KT, k)
                        if side and not last and k == 0:
                            v.wait_ge(sdt, i + 1)
                            side_of(i + 1)
                        if kind == "gat":
                            v.wait_ge(outm, i * KT + k)
                            v.tensor_scalar(sf[:, k, :], self.same[:, bass.ds(c * P, P)], weights[:, bass.ds(c, 1)], None,
                                            ALU.mult).then_inc(sfr, 1)
                        if kind == "pre":
                            v.wait_ge(outm, i * KT + k)
                            v.tensor_copy(m5[:, k, 0:4], self.te[:, :, bass.ds(c, 1)].rearrange("p l o -> p (l o)")).then_inc(msgr, 1)
                        if kind == "rel":
                            v.wait_ge(relm, i + 1)
                            v.wait_ge(turned, i * KT + k)
                            v.tensor_tensor(msg[:, k, 0, :], gr[:, k, :], psr[:, k * D:(k + 1) * D], ALU.add).then_inc(added, 1)
                        if kind == "tp":
                            v.wait_ge(wxm, i * KT + k + 1)
                            v.wait_ge(turned, i * KT + k)
                            wx = pst[:, 0:192]
                            sh = rec[:, bass.ds(c, 1), R_SH:R_SH + 4].rearrange("p o w -> p (o w)")
                            g1 = gr[:, k, MUL:].rearrange("p (u m) -> p u m", m=3)
                            t3 = tA[:, k % 2, MUL:].rearrange("p (u m) -> p u m", m=3)
                            n1 = st.mark(v.tensor_tensor(t3, g1, spread(sh[:, 1:4], MUL), ALU.mult))
                            n2 = st.mark(v.tensor_tensor(tA[:, k % 2, 0:MUL], gr[:, k, 0:MUL], wx[:, D + MUL:D + 2 * MUL], ALU.mult))
                            v.scalar_tensor_tensor(msg[:, k, 0, :], gr[:, k, :], sh[:, 0:1], wx[:, 0:D], ALU.mult, ALU.mult)
                            st.need(n1)
                            n3 = st.mark(v.tensor_reduce(msg[:, k, 1, 0:MUL], t3, AX_X, ALU.add))
                            st.need(n2)
                            v.tensor_tensor(msg[:, k, 1, MUL:].rearrange("p (u m) -> p u m", m=3), fan(tA[:, k % 2, 0:MUL], 3),
                                            spread(sh[:, 1:4], MUL), ALU.mult)
                            st.need(n3)
                            v.tensor_tensor(msg[:, k, 1, 0:MUL], msg[:, k, 1, 0:MUL], wx[:, D:D + MUL], ALU.mult).then_inc(msgr, 1)
                        v.wait_ge(outm, i * KT + k)
                        v.tensor_scalar(link[LAST, k, :], self.iota_f[LAST, :], self.reach[LAST, bass.ds(c, 1)], None,
                                        ALU.is_lt).then_inc(linkr, 1)
                        v.wait_ge(sst[k], i * 16)
                        if kind == "gat":
                            v.tensor_copy(outs[:, k, D + 1:D + 2], loop_w[:, bass.ds(c, 1)])
                        v.tensor_copy(pix[:, k:k + 1], self.put_i[:, bass.ds(c, 1)]).then_inc(extra, 1)
                    if st:
                        st.close()

                if gathers:
                    for k in range(KT):
                        g_index(k, k)
                if side:
                    side_of(0)
                body(0, False)
                with v.Fori(1, G - 1) as i:
                    body(i, False)
                body(G - 1, True)

            @block.scalar
            def _(act):
                act.sem_inc(evac, 2)
                if n_cst:
                    act.wait_ge(cst, n_cst)
                act.wait_ge(init, cleared)

                def side_keep(i):
                    act.wait_ge(sdt, i + 1)
                    act.activation(sdT[:, :], (pst if kind == "rel" else psh)[0:sw, 0:P], ACT.Copy).then_inc(sdk, 1)

                def hidden(i):
                    act.wait_ge(hidm, i + 1)
                    act.activation(hs[:, :, :].rearrange("h k e -> h (k e)"), psh[0:64, :], ACT.Silu, scale=0.25).then_inc(hidk, 1)

                def prepare(c, k):
                    if kind != "gat":
                        act.wait_ge(outm, c)
                        act.activation(sf[:, k, :], self.same[:, bass.ds(c * P, P)], ACT.Copy).then_inc(sfr, 1)
                    if kind == "rel":
                        act.wait_ge(added, c + 1)
                        act.activation(msg[:, k, 0, :], msg[:, k, 0, :], ACT.Relu).then_inc(msgr, 1)

                def body(i, last):
                    for k in range(KT):
                        c = i * KT + k
                        if not (last and k == KT - 1):
                            prepare(c + 1, (k + 1) % KT)
                        if side and not last and k == 1:
                            side_keep(i + 1)
                            if kind == "tp":
                                hidden(i + 1)
                        if two_step:
                            act.wait_ge(turned, i * KT + k + KT)
                            act.activation(aT[:, k % 2, :], psa[k % 2][:, 0:halves * P], ACT.Copy).then_inc(kept, 1)
                        act.wait_ge(outm, c + KT)
                        act.wait_ge(sst[k], i * 16)
                        act.activation(outs[:, k, 0:W], pso[k % 2][:, 0:W], ACT.Copy).then_inc(evac, 1)

                if side:
                    side_keep(0)
                if kind == "tp":
                    hidden(0)
                prepare(0, 0)
                body(0, False)
                with act.Fori(1, G - 1) as i:
                    body(i, False)
                body(G - 1, True)

            @block.tensor
            def _(pe):
                pe.sem_inc(outm, KT - 1)
                pe.wait_ge(init, cleared)
                if two_step:
                    pe.sem_inc(turned, KT - 1)
                if n_cst:
                    pe.wait_ge(cst, n_cst)
                if kind == "tp":
                    pe.wait_ge(init, 3)

                def until(sem, n):
                    pe.wait_ge(sem, n)
                    pe.sem_inc(pgate, 1)

                def side_turn(i):
                    until(sdr, i + 1)
                    if kind == "tp":
                        until(hidk, i)
                    pe.transpose((pst if kind == "rel" else psh)[0:sw, 0:P], sd[:, :], ident[:, :]).then_inc(sdt, 1)

                def side_use(i):
                    until(sdk, i + 1)
                    if kind == "rel":
                        until(msgr, i * KT)
                        pe.matmul(psr[:, :], sdT[:, :], relb[:, :], start=True, stop=True).then_inc(relm, 1)
                    else:
                        for k in range(KT):
                            mm = pe.matmul(psh[0:64, k * P:(k + 1) * P], W1[:, k, :], sdT[:, :], start=True, stop=True)
                        mm.then_inc(hidm, 1)

                def path_weights(c, k, i):
                    if k % KT == 0:
                        until(hidk, i + 1)
                    until(msgr, c)
                    pe.matmul(pst[:, 0:192], hs[:, k % KT, :], W2[:, :], start=True, stop=True).then_inc(wxm, 1)

                def turn(c, k, it):
                    pe.wait_ge(sfr, c + 1)
                    if kind == "sage":
                        pe.wait_ge(gin[k], it * 16 + 16)
                    else:
                        pe.wait_ge(msgr, c + 1)
                    if not isinstance(c, int) or c >= 2:
                        pe.wait_ge(kept, c - 1)
                    for h in range(halves):
                        lhs = gr[:, k, :] if kind == "sage" else msg[:, k, h, :]
                        mm = pe.matmul(psa[k % 2][:, h * P:(h + 1) * P], lhs, sf[:, k, :], start=True, stop=True)
                    mm.then_inc(turned, 1)

                def sums(c, k):
                    pe.wait_ge(evac, c + 1)
                    if two_step:
                        pe.wait_ge(kept, c + 1)
                        pairs = [(aT[:, k % 2, h * P:(h + 1) * P], Wm[:, h, :]) for h in range(halves)]
                    elif kind == "gat":
                        pe.wait_ge(sfr, c + 1)
                        pairs = [(sf[:, k, :], table[:, bass.ds(c, 1), 0:W].rearrange("p o w -> p (o w)"))]
                    else:
                        pe.wait_ge(sfr, c + 1)
                        pe.wait_ge(msgr, c + 1)
                        pairs = [(sf[:, k, :], m5[:, k, 0:W])]
                    for n, (x, y) in enumerate(pairs):
                        pe.matmul(pso[k % 2][:, 0:W], x, y, start=(n == 0), stop=False)
                    pe.wait_ge(evac, c + 2)
                    pe.wait_ge(linkr, c + 1)
                    pe.matmul(pso[k % 2][:, 0:W], link[LAST, k, :], outs[LAST, (k - 1) % KT, 0:W], start=False, stop=True).then_inc(outm, 1)

                def body(i, last):
                    for k in range(KT):
                        c = i * KT + k
                        if side and not last and k == 0:
                            side_turn(i + 1)
                        if kind == "rel" and not last and k == 3:
                            side_use(i + 1)
                        if two_step and not (last and k == KT - 1):
                            turn(c + 1, (k + 1) % KT, i + (k + 1) // KT)
                        if kind == "tp" and not (last and k >= 2):
                            path_weights(c + 2, k + 2, i + (k + 2) // KT)
                        if kind == "tp" and not last and k == 1:
                            side_use(i + 1)
                        sums(c, k)

                if side:
                    side_turn(0)
                    side_use(0)
                if kind == "tp":
                    path_weights(0, 0, 0)
                if two_step:
                    turn(0, 0, 0)
                if kind == "tp":
                    path_weights(1, 1, 0)
                body(0, False)
                with pe.Fori(1, G - 1) as i:
                    body(i, False)
                body(G - 1, True)

    def node_pass(self, name, kind, src, layer, dst=None, dst2=None, extra=None):
        nc, a, NBLK, ident = self.nc, self.a, self.NBLK, self.ident
        gat, rel, sage = kind in ("gat", "gat_end"), kind[:3] == "rel", kind[:4] == "sage"
        linear = kind in ("lin", "gat")
        two_norms = kind in ("gat_end", "rel2")
        normed = kind not in ("lin", "sage0", "sage1")
        affine = kind == "gat_end" or rel
        relu2 = kind in ("rel0", "rel1")
        src_w = AW if gat else D
        res_w = AW if linear else D
        with Pass(nc, name) as q:
            x = q.sb("x", [P, 4, KT, src_w])
            ag = q.sb("ag", [P, 4, KT, AW])
            ex = q.sb("ex", [P, 4, KT, D])
            y = q.sb("y", [P, 4, KT, D])
            z = q.sb("z", [P, 4, KT, D])
            res = q.sb("res", [P, 4, KT, res_w])
            res2 = q.sb("res2", [P, 4, KT, D])
            xT = q.sb("xT", [P, 2, KT, P])
            zT = q.sb("zT", [P, 2, KT, P])
            bn = q.sb("bn", [P, 4, 2, KT, 6])
            mv = q.sb("mv", [P, 4, 2, KT, 2])
            rs = q.sb("rs", [P, 4, 2, 4, KT])
            sm = q.sb("sm", [P, 4, 3, KT])
            bias = q.sb("bias", [P, D])
            ln_w = q.sb("ln_w", [P, 2, D])
            ln_c = q.sb("ln_c", [P, 2])
            Wn = q.sb("Wn", [P, D])
            WT = q.sb("WT", [P, D])
            att = q.sb("att", [P, 2])
            Wl = q.sb("Wl", [P, 2 * D])
            na = q.sb("na", [P, NBLK * KT])
            pT = [q.ps(f"T{j}") for j in range(2)]
            pM = [[q.ps(f"M{j}{h}") for h in range(2)] for j in range(2)]
            pN = [q.ps(f"N{j}") for j in range(2)]
            lin_, stored, stored2 = q.sems("rows_in", 4), q.sems("result_stored", 4), q.sems("second_stored", 4)
            cst, wat, wak, wam, wrd = (q.sem(n) for n in ("constants", "w_turned", "w_kept", "w_att", "w_ready"))
            ch, gch, gate = q.sem("dve_steps"), q.sem("pool_steps"), q.sem("gate")
            names = ("y_ready", "scale_ready", "normed", "affine_done", "scale2_ready", "result_ready", "second_ready",
                     "turned", "turned_kept", "product_made", "turned2", "turned2_kept", "product2_made", "bias_added")
            yr, sr, zr, af, sr2, rr, rr2, tr, tk, mr, tr2, tk2, mr2, bx = [q.sem(n) for n in names]
            block = q.block()

            def done(eng, sem, b, back=0):
                if not isinstance(b.n, int) or b.n >= back:
                    eng.wait_ge(sem, b.n + (1 - back))

            def stored_all(eng, sems, b):
                if not isinstance(b.n, int) or b.n >= 4:
                    eng.wait_ge(sems[b.s4], b.t4 * 16)

            def times(eng, steps, per=None, chain=None):
                span = max(lag for _, lag in steps)

                def at_time(t, i=None, m=0):
                    st = Chain(eng, chain, t, per) if chain else None
                    for step, lag in steps:
                        if i is None:
                            if 0 <= t - lag < NBLK:
                                step(Block(t - lag, 0, t - lag), st)
                        else:
                            step(Block(t - lag, i, m - lag), st)
                    if st:
                        st.close()

                for t in range(PEEL):
                    at_time(t)
                with eng.Fori(0, (NBLK - PEEL) // 4) as i:
                    for u in range(4):
                        at_time(i * 4 + (PEEL + u), i, PEEL + u)
                for t in range(NBLK, NBLK + span):
                    at_time(t)

            consts = []
            if gat or rel:
                r, pre = (layer - 1, "L0_gnn_") if gat else (layer, "L1_gnn_")
                consts.append((bias[:, :], a[pre + ("bias" if gat else "lin_b")][r].partition_broadcast(P)))
                if affine:
                    g_, b_ = ("ln_gamma", "ln_beta") if gat else ("ln_w", "ln_b")
                    consts.append((ln_w[:, 0, :], a[pre + g_][r].partition_broadcast(P)))
                    consts.append((ln_w[:, 1, :], a[pre + b_][r].partition_broadcast(P)))
                if kind == "gat":
                    consts.append((ln_c[:, :], a["L0_ln_cols"][r]))
            if sage:
                consts.append((bias[:, :], a[f"L2_gnn_b{layer}"].partition_broadcast(P)))
                consts.append((Wn[:, :], a[f"L2_gnn_Ws{layer}"]))
            if linear:
                consts.append((Wl[:, 0:D], a["L0_gnn_W"][layer]))
                consts.append((att[:, :], a["L0_att_cols"][layer]))
            if kind == "sage2":
                consts.append((Wl[:, :], a["L3_in"]))
            if kind in ("sage2", "fin"):
                consts.append((na[:, :], a["node_vec1"]))
            loads = []
            if kind != "rel0":
                loads.append((x, self.table if gat else src, src_w))
            if kind != "lin":
                loads.append((ag, self.agg, AW))
            if extra is not None or kind == "gat_end":
                loads.append((ex, extra if extra is not None else src, D))
            last_use = tr if kind == "lin" else af if two_norms else yr
            lag_store = 8 if kind == "sage2" else 5
            first = dst if not linear else self.table
            second = dst2
            first_buf = y if relu2 else res

            def at(ap, n):
                return ap.rearrange("(b p k) d -> b p k d", p=P, k=KT)[bass.ds(n, 1)].rearrange("b p k d -> (b p) k d")

            @block.sync
            def _(sp):
                for t_, s_ in consts:
                    sp.dma_start(t_, s_).then_inc(cst, 16)

                def load(b, st):
                    done(sp, last_use, b, 4)
                    for buf, ap, w in loads:
                        sp.dma_start(buf[:, b.s4, :, :], at(ap, b.n)).then_inc(lin_[b.s4], 16)

                def store(b, st):
                    done(sp, yr if relu2 else af if kind == "sage2" else rr, b)
                    sp.dma_start(at(first, b.n), first_buf[:, b.s4, :, :]).then_inc(stored[b.s4], 16)
                    if second is not None:
                        done(sp, rr2, b)
                        sp.dma_start(at(second, b.n), res2[:, b.s4, :, :]).then_inc(stored2[b.s4], 16)

                times(sp, [(load, 0), (store, lag_store)])
                for j in range(4):
                    n = len(range(j, NBLK, 4)) * 16
                    sp.wait_ge(stored[j], n)
                    if second is not None:
                        sp.wait_ge(stored2[j], n)

            def arrived(eng, b):
                eng.wait_ge(lin_[b.s4], (b.t4 + 1) * 16 * len(loads))

            @block.tensor
            def _(pe):
                pe.wait_ge(cst, 16 * len(consts))
                if linear:
                    pe.transpose(pT[0][:, 0:D], Wl[:, 0:D], ident[:, :]).then_inc(wat, 1)
                    pe.wait_ge(wak, 1)
                    pe.matmul(pN[0][:, 0:2], WT[:, :], att[:, :], start=True, stop=True).then_inc(wam, 1)
                    pe.wait_ge(wrd, 1)

                def turn_x(b, st):
                    arrived(pe, b)
                    done(pe, tk, b, 2)
                    if kind == "sage2":
                        done(pe, tk2, b, 4)
                    for k in range(KT):
                        mm = pe.transpose(pT[b.s2][:, k * P:(k + 1) * P], x[:, b.s4, k, 0:D], ident[:, :])
                    mm.then_inc(tr, 1)

                def turn_z(b, st):
                    done(pe, zr, b)
                    done(pe, tk2, b, 2)
                    for k in range(KT):
                        mm = pe.transpose(pT[b.s2][:, k * P:(k + 1) * P], z[:, b.s4, k, :], ident[:, :])
                    mm.then_inc(tr2, 1)

                def own(b, st):
                    done(pe, tk, b)
                    done(pe, yr, b, 2)
                    for k in range(KT):
                        mm = pe.matmul(pN[b.s2][:, k * D:(k + 1) * D], xT[:, b.s2, k, :], Wn[:, :], start=True, stop=True)
                    mm.then_inc(mr, 1)

                def product(b, st):
                    w = AW if linear else 2 * D
                    done(pe, tk if kind == "lin" else tk2, b)
                    done(pe, rr if linear else rr2, b, 2)
                    if kind == "sage2":
                        done(pe, af, b, 2)
                    for k in range(KT):
                        mm = pe.matmul(pM[b.s2][k // 2][:, (k % 2) * w:(k % 2 + 1) * w], (xT if kind == "lin" else zT)[:, b.s2, k, :],
                                       Wl[:, 0:w], start=True, stop=True)
                    mm.then_inc(mr2, 1)

                steps = {"lin": [(turn_x, 0), (product, 1)], "gat": [(turn_z, 0), (product, 0)],
                         "sage0": [(turn_x, 0), (own, 1)], "sage1": [(turn_x, 0), (own, 1)],
                         "sage2": [(turn_x, 0), (own, 1), (turn_z, 3), (product, 4)]}.get(kind)
                if steps:
                    times(pe, steps)

            @block.gpsimd
            def _(pool):
                def scale(stage):
                    def step(b, st):
                        done(pool, (yr, af)[stage], b)
                        m, t = mv[:, b.s4, stage], rs[:, b.s4, stage]
                        st.run(pool.tensor_tensor(t[:, 0, :], m[:, :, 1], self.eps_t[:, :], ALU.add))
                        st.run(pool.tensor_tensor(t[:, 1, :], t[:, 0, :], self.mhalf[:, :], ALU.pow))
                        st.run(pool.tensor_tensor(t[:, 2, :], m[:, :, 0], t[:, 1, :], ALU.mult))
                        pool.tensor_tensor(t[:, 3, :], t[:, 2, :], self.neg1[:, :], ALU.mult).then_inc((sr, sr2)[stage], 1)
                    return step

                def add_bias(b, st):
                    arrived(pool, b)
                    pool.tensor_tensor(ex[:, b.s4], ex[:, b.s4], spread(ln_w[:, 1, :], KT), ALU.add).then_inc(bx, 1)

                if two_norms:
                    pool.wait_ge(cst, 16 * len(consts))
                    times(pool, [(scale(0), 0), (scale(1), 1), (add_bias, 0)], 6, gch)
                elif normed:
                    times(pool, [(scale(0), 1 if sage else 0)], 3, gch)

            @block.vector
            def _(v):
                v.wait_ge(cst, 16 * len(consts))
                if linear:
                    v.wait_ge(wat, 1)
                    v.tensor_copy(WT[:, :], pT[0][:, 0:D]).then_inc(wak, 1)
                    v.wait_ge(wam, 1)
                    v.tensor_copy(Wl[:, D:AW], pN[0][:, 0:2]).then_inc(wrd, 1)
                if kind == "sage2":
                    v.tensor_scalar(na[:, :], na[:, :], MUL ** -0.5, None, ALU.mult).then_inc(wrd, 1)
                    v.wait_ge(wrd, 1)
                if kind == "fin":
                    v.tensor_tensor(na[:, :], na[:, :], na[:, :], ALU.mult).then_inc(wrd, 1)
                    v.wait_ge(wrd, 1)

                def stats(buf, j, stage, st, sem):
                    for k in range(KT):
                        m = st.mark(v.bn_stats(bn[:, j, stage, k, :], buf[:, j, k, :]))
                    st.need(m)
                    v.sem_inc(gate, 1)
                    for k in range(KT):
                        last = v.bn_aggr(mv[:, j, stage, k, :], bn[:, j, stage, k, :])
                    last.then_inc(sem, 1)

                def combine(b, st):
                    n, j = b.n, b.s4
                    arrived(v, b)
                    done(v, zr if normed and kind != "fin" else rr, b, 4)
                    if relu2:
                        stored_all(v, stored, b)
                    cols = bass.ds(n * KT, KT)
                    s_ = sm[:, j]
                    if gat:
                        st.run(v.tensor_tensor(s_[:, 0, :], ag[:, j, :, D + 1], self.no_edge[:, cols], ALU.add))
                        st.run(v.scalar_tensor_tensor(s_[:, 1, :], s_[:, 0, :], 1e-16, ag[:, j, :, D], ALU.add, ALU.add))
                        m = st.mark(v.reciprocal(s_[:, 2, :], s_[:, 1, :]))
                        for k in range(KT):
                            m = st.mark(v.scalar_tensor_tensor(y[:, j, k, :], x[:, j, k, 0:D], s_[:, 0, k:k + 1], ag[:, j, k, 0:D],
                                                               ALU.mult, ALU.add))
                        st.need(m)
                        for k in range(KT):
                            m = st.mark(v.scalar_tensor_tensor(y[:, j, k, :], y[:, j, k, :], s_[:, 2, k:k + 1], bias[:, :],
                                                               ALU.mult, ALU.add))
                        st.need(m)
                    else:
                        if kind == "fin":
                            m = st.mark(v.tensor_tensor(s_[:, 0, :], ag[:, j, :, D], na[:, cols], ALU.mult))
                        else:
                            m = st.mark(v.tensor_copy(s_[:, 0, :], self.inv_cnt[:, cols]))
                        if sage:
                            done(v, mr, b)
                        st.need(m)
                        for k in range(KT):
                            own_ = {"rel0": bias[:, :], "sage0": pN[b.s2][:, k * D:(k + 1) * D]}.get(kind)
                            if own_ is None:
                                own_ = pN[b.s2][:, k * D:(k + 1) * D] if sage else x[:, j, k, :]
                            m = st.mark(v.scalar_tensor_tensor(y[:, j, k, :], ag[:, j, k, 0:D], s_[:, 0, k:k + 1], own_, ALU.mult, ALU.add))
                        if kind not in ("rel0", "fin"):
                            st.need(m)
                            m = st.mark(v.tensor_tensor(y[:, j], y[:, j], spread(bias[:, :], KT), ALU.add))
                        if kind in ("sage1", "sage2"):
                            st.need(m)
                            m = st.mark(v.tensor_tensor(y[:, j], y[:, j], (x if kind == "sage1" else ex)[:, j], ALU.add))
                        st.need(m)
                    if normed:
                        stats(y, j, 0, st, yr)
                    else:
                        v.sem_inc(yr, 1)

                def apply(b, st):
                    j = b.s4
                    done(v, zr, b)
                    st.run(v.tensor_tensor(z[:, j], z[:, j], spread(ln_w[:, 0, :], KT), ALU.mult))
                    if two_norms:
                        done(v, bx, b)
                        st.run(v.tensor_tensor(z[:, j], z[:, j], ex[:, j], ALU.add))
                        stats(z, j, 1, st, af)
                    else:
                        v.tensor_tensor(z[:, j], z[:, j], spread(ln_w[:, 1, :], KT), ALU.add).then_inc(af, 1)

                def shortcut(b, st):
                    n, j = b.n, b.s4
                    done(v, mr2, b)
                    stored_all(v, stored, b)
                    m = st.mark(v.tensor_copy(sm[:, j, 1, :], na[:, bass.ds(n * KT, KT)]))
                    st.need(m)
                    for k in range(KT):
                        last = v.scalar_tensor_tensor(res[:, j, k, :], pM[b.s2][k // 2][:, (k % 2) * 2 * D:(k % 2) * 2 * D + D],
                                                      sm[:, j, 1, k:k + 1], z[:, j, k, :], ALU.mult, ALU.add)
                    last.then_inc(af, 1)

                if kind != "lin":
                    times(v, [(combine, 1 if sage else 0)] + ([(apply, 1)] if affine else []) + ([(shortcut, 4)] if kind == "sage2" else []),
                          24, ch)

            @block.scalar
            def _(act):
                act.wait_ge(cst, 16 * len(consts))

                def keep_x(b, st):
                    done(act, tr, b)
                    act.activation(xT[:, b.s2].rearrange("f k n -> f (k n)"), pT[b.s2][:, :], ACT.Copy).then_inc(tk, 1)

                def keep_z(b, st):
                    done(act, tr2, b)
                    o, p_ = zT[:, b.s2].rearrange("f k n -> f (k n)"), pT[b.s2][:, :]
                    done(act, mr2, b, 2)
                    if kind == "gat":
                        act.activation(o, p_, ACT.Identity, scale=ln_c[:, 0:1], bias=ln_c[:, 1:2]).then_inc(tk2, 1)
                    else:
                        act.activation(o, p_, ACT.Copy).then_inc(tk2, 1)

                def norm(stage):
                    def step(b, st):
                        j = b.s4
                        done(act, (sr, sr2)[stage], b)
                        to, frm, sem = (z, y, zr) if stage == 0 else (res, z, rr)
                        if kind == "fin":
                            to, sem = res, rr
                        if to is res:
                            stored_all(act, stored, b)
                        elif kind in ("gat", "sage2"):
                            done(act, tr2, b, 4)
                            if kind == "sage2":
                                done(act, af, b, 4)
                        else:
                            done(act, rr if two_norms else rr2, b, 4)
                        for k in range(KT):
                            last = act.activation(to[:, j, k, :], frm[:, j, k, :], ACT.Identity, scale=rs[:, j, stage, 1, k:k + 1],
                                                  bias=rs[:, j, stage, 3, k:k + 1])
                        last.then_inc(sem, 1)
                    return step

                def heads(b, st):
                    done(act, mr2, b)
                    stored_all(act, stored, b)
                    for h in range(2):
                        p_ = pM[b.s2][h][:, 0:2 * AW].rearrange("p (k w) -> p k w", k=2)
                        act.activation(res[:, b.s4, 2 * h:2 * h + 2, :], p_, ACT.Copy)
                        last = act.activation(self.asad[:, bass.ds(b.n * KT + 2 * h, 2), :], p_[:, :, D:AW], ACT.Copy)
                    last.then_inc(rr, 1)

                def relu_affine(b, st):
                    done(act, af, b)
                    stored_all(act, stored2, b)
                    act.activation(res2[:, b.s4], z[:, b.s4], ACT.Relu).then_inc(rr2, 1)

                def relu_sum(b, st):
                    done(act, yr, b)
                    stored_all(act, stored, b)
                    act.activation(res[:, b.s4], y[:, b.s4], ACT.Relu).then_inc(rr, 1)

                def features(b, st):
                    done(act, mr2, b)
                    done(act, af, b)
                    stored_all(act, stored2, b)
                    for k in range(KT):
                        last = act.activation(res2[:, b.s4, k, :], pM[b.s2][k // 2][:, (k % 2) * 2 * D + D:(k % 2) * 2 * D + 2 * D],
                                              ACT.Copy, scale=sm[:, b.s4, 1, k:k + 1])
                    last.then_inc(rr2, 1)

                times(act, {"lin": [(keep_x, 0), (heads, 1)], "gat": [(norm(0), 0), (heads, 2), (keep_z, 0)],
                            "gat_end": [(norm(0), 0), (norm(1), 1)], "rel0": [(norm(0), 0), (relu_affine, 1)],
                            "rel1": [(norm(0), 0), (relu_affine, 1)], "rel2": [(norm(0), 0), (norm(1), 1)],
                            "sage0": [(keep_x, 0), (relu_sum, 2)], "sage1": [(keep_x, 0), (relu_sum, 2)],
                            "sage2": [(keep_x, 0), (norm(0), 2), (keep_z, 3), (features, 4)], "fin": [(norm(0), 0)]}[kind])


def gnn_kernel(nc, a, out, N, E):
    Kernel(nc, a, out, N, E).build()


def kernel(**inputs):
    import numpy as _np
    import concourse.bacc as _bacc
    from concourse import mybir as _mybir
    from concourse.bass_utils import run_bass_kernel_spmd as _run

    t = {k: _np.asarray(v) for k, v in inputs.items()}
    N, E = t["x"].shape[0], t["src"].shape[0]
    C = -(-E // BLOCK) * KT
    NP = -(-N // BLOCK) * BLOCK

    def edges(v, fill=0):
        w = _np.full((C * P,) + v.shape[1:], fill, v.dtype)
        w[:E] = v
        return _np.ascontiguousarray(_np.moveaxis(w.reshape((C, P) + v.shape[1:]), 0, 1))

    def rows(v, n):
        w = _np.zeros((n,) + v.shape[1:], v.dtype)
        w[:v.shape[0]] = v
        return w

    def vectors(w):
        o = _np.zeros((96, 96), w.dtype)
        for m in range(3):
            o[m::3, m::3] = w
        return o

    d = {"x": rows(t["x"], NP), "src": edges(t["src"]), "dst": edges(t["dst"], NP - 1), "edge_type_5": edges(t["edge_type_5"]),
         "edge_attr_4": edges(t["edge_attr_4"]), "edge_attr_16": edges(t["edge_attr_16"]),
         "edge_attr_128": rows(t["edge_attr_128"], C * P)}
    d["node_vec1"] = _np.ascontiguousarray(rows(t["node_vec1"], NP).reshape(-1, P, KT).transpose(1, 0, 2).reshape(P, -1))
    for n in ("W", "We", "bias", "ln_gamma", "ln_beta"):
        d["L0_gnn_" + n] = t["L0_gnn_" + n]
    d["L0_gnn_att_edge"] = _np.ascontiguousarray(t["L0_gnn_att_edge"].T)
    d["L0_att_cols"] = _np.stack([t["L0_gnn_att_src"], t["L0_gnn_att_dst"]], axis=-1)
    d["L0_ln_cols"] = _np.stack([t["L0_gnn_ln_gamma"], t["L0_gnn_ln_beta"]], axis=-1)
    d["dst_rows"] = _np.concatenate([t["dst"], _np.full(C * P + 1 - E, NP - 1, t["dst"].dtype)])
    rel = t["L1_gnn_relvecs"]
    d["L1_gnn_relvecs"] = _np.zeros((rel.shape[0], KT * 8, KT * D), rel.dtype)
    for k in range(KT):
        d["L1_gnn_relvecs"][:, 8 * k:8 * k + rel.shape[1], k * D:(k + 1) * D] = rel
    d["L1_gnn_lin_w"] = _np.ascontiguousarray(t["L1_gnn_lin_w"].transpose(0, 2, 1))
    for n in ("lin_b", "ln_w", "ln_b"):
        d["L1_gnn_" + n] = t["L1_gnn_" + n]
    for l in range(3):
        d[f"L2_gnn_Ws{l}"] = _np.ascontiguousarray(t[f"L2_gnn_Ws{l}"].T)
        d[f"L2_gnn_Wn{l}"] = _np.ascontiguousarray(t[f"L2_gnn_Wn{l}"].T)
        d[f"L2_gnn_b{l}"] = t[f"L2_gnn_b{l}"]
    d["iota8"] = _np.tile(_np.arange(8, dtype=_np.float32), (P, 1))
    f32 = t["x"].dtype
    d["L3_in"] = _np.zeros((D, 2 * D), f32)
    for o, (s, v) in ((0, ("W_sc0", "W_sc1")), (D, ("W_l10", "W_l11"))):
        d["L3_in"][:MUL, o:o + MUL] = t["L3_gnn_" + s]
        d["L3_in"][MUL:, o + MUL:o + D] = vectors(t["L3_gnn_" + v])
    d["L3_out"] = _np.zeros((D, 2, D + 1), f32)
    for h, (s, v, al) in enumerate((("W_l2a", "W_l2d", "A0"), ("W_l2b", "W_l2c", "A1"))):
        d["L3_out"][:MUL, h, :MUL] = t["L3_gnn_" + s]
        d["L3_out"][MUL:, h, MUL:D] = vectors(t["L3_gnn_" + v])
        d["L3_out"][:MUL, h, D] = t["L3_gnn_" + al][:, 0]
    w1 = t["L3_gnn_W_mlp1"]
    d["L3_gnn_W_mlp1"] = _np.zeros((KT * 16, KT, 64), f32)
    for k in range(KT):
        d["L3_gnn_W_mlp1"][16 * k:16 * k + 16, k] = w1
    w2 = t["L3_gnn_W_mlp2"]
    d["L3_gnn_W_mlp2"] = _np.concatenate([w2[:, 0:32], _np.repeat(w2[:, 64:96], 3, axis=1), w2[:, 96:128], w2[:, 32:64]], axis=1)

    nc = _bacc.Bacc("TRN2", target_bir_lowering=False, num_devices=1)
    arrays, args = {}, {}
    for name, v in d.items():
        arrays[f"in_{name}"] = v
        args[name] = nc.dram_tensor(f"in_{name}", v.shape, _mybir.dt.from_np(v.dtype), kind="ExternalInput").ap()
    out = nc.dram_tensor("out_0_dram", (NP, D), F32, kind="ExternalOutput").ap()
    gnn_kernel(nc, args, out, N, E)
    r = _run(nc, [arrays], core_ids=[0])
    return r.results[0]["out_0_dram"][:N]
```

```python
from contextlib import ExitStack

import concourse.bass as bass
from concourse import mybir

F32 = mybir.dt.float32
BF16 = mybir.dt.bfloat16
I32 = mybir.dt.int32
U32 = mybir.dt.uint32
ALU = mybir.AluOpType
ACT = mybir.ActivationFunctionType
AX_X = mybir.AxisListType.X

P = 128
D = 128
KT = 4
BLOCK = P * KT
LN_EPS = 1e-5
NEG_SLOPE = 0.2
BIG = 1e30
SKIP = 1 << 20
AW = 130
REC = 32
R_DST, R_SRC, R_TYPE, R_SH, R_LEN, R_TE = 0, 1, 2, 4, 8, 24
MUL = 32
PEEL = 10
LATE = 1
LAST = slice(96, 128)


class Chain:

    def __init__(self, eng, sem, i, per):
        self.eng, self.sem, self.base, self.per, self.k = eng, sem, i * per, per, 0

    def mark(self, ins):
        self.k += 1
        ins.then_inc(self.sem, 1)
        return self.k

    def need(self, k):
        self.eng.wait_ge(self.sem, self.base + k)

    def run(self, ins):
        self.need(self.mark(ins))

    def close(self):
        assert self.k <= self.per, self.k
        if self.k < self.per:
            self.eng.sem_inc(self.sem, self.per - self.k)


class Block:

    def __init__(self, n, i, m):
        self.n, self.s2, self.s4, self.t4 = n, m % 2, m % 4, i + m // 4


class Pass:

    def __init__(self, nc, name):
        self.nc, self.name, self.ctx, self.owned = nc, name, ExitStack(), []

    def __enter__(self):
        return self

    def __exit__(self, *e):
        self.ctx.close()
        self.nc.clear_and_free_semaphores(self.owned)
        self.nc.all_engine_barrier()

    def sb(self, name, shape, dt=F32):
        return self.ctx.enter_context(self.nc.sbuf_tensor(f"{self.name}_{name}", shape, dt))

    def ps(self, name):
        return self.ctx.enter_context(self.nc.psum_tensor(f"{self.name}_{name}", [P, 512], F32))

    def sem(self, name):
        self.owned.append(self.nc.alloc_semaphore(f"{self.name}_{name}"))
        return self.owned[-1]

    def sems(self, name, n):
        return [self.sem(f"{name}{k}") for k in range(n)]

    def block(self):
        return self.ctx.enter_context(self.nc.Block())


def spread(ap, n):
    return ap.unsqueeze(1).to_broadcast([ap.shape[0], n, ap.shape[1]])


def fan(ap, n):
    return ap.unsqueeze(2).to_broadcast([ap.shape[0], ap.shape[1], n])


def backward(ap):
    (ps, pn), (fs, fn) = ap.ap
    return bass.AP(ap.tensor, ap.offset + fs * (fn - 1), [[ps, pn], [-fs, fn]])


class Kernel:
    def __init__(self, nc, a, out, N, E):
        self.nc, self.a, self.out = nc, a, out
        self.C = C = -(-E // BLOCK) * KT
        self.G = C // KT
        self.NBLK = -(-N // BLOCK)
        self.NP = self.NBLK * BLOCK
        self.NCOL = self.NBLK * KT
        self.HALF = C // 2
        assert self.NBLK % 4 == PEEL % 4 and C % 2 == 0 and self.HALF <= P and self.G % 2 == 1

    def dram(self, name, shape, dt=F32):
        return self.nc.dram_tensor(name, shape, dt, kind="Internal").ap()

    def build(self):
        nc, C, NP, NCOL, HALF = self.nc, self.C, self.NP, self.NCOL, self.HALF
        self.table = self.dram("gat_table", (NP, AW))
        self.aux = self.dram("gat_aux", (NP, 2))
        self.agg = self.dram("aggregate", (NP, AW))
        self.pre = self.dram("edge_sums", (NP, 8))
        self.rec_d = self.dram("records", (C * P, REC))
        self.dst_d = self.dram("dst_sorted", (C * P + 2,))
        nodes = [self.dram(f"nodes_{n}", (NP, D)) for n in range(5)]
        with ExitStack() as ctx:
            def keep(name, shape, dt=F32):
                return ctx.enter_context(nc.sbuf_tensor(name, shape, dt))

            self.ident = keep("ident", [P, P])
            self.same = keep("same_run", [P, C * P], BF16)
            self.src_i = keep("src_i", [P, C], U32)
            self.dst_i = keep("dst_i", [P, C], U32)
            self.put_i = keep("put_i", [P, C], U32)
            self.te = keep("te", [P, 4, C])
            self.typ = keep("typ", [P, C])
            self.reach = keep("reach", [P, C])
            self.iota_f = keep("iota_f", [P, P])
            self.tmean = keep("tmean", [P, 4, NCOL])
            self.inv_cnt = keep("inv_cnt", [P, NCOL])
            self.no_edge = keep("no_edge", [P, NCOL])
            self.asad = keep("asad", [P, NCOL, 2])
            self.pen = keep("pen", [HALF, 2, 2, P])
            self.pen_carry = keep("pen_carry", [HALF, 2, 2, P])
            self.pen_row = keep("pen_row", [1, 2, C])
            self.mhalf = keep("mhalf", [P, KT])
            self.neg1 = keep("neg1", [P, KT])
            self.eps_t = keep("eps_t", [P, KT])

            self.records()
            self.order()
            self.graph()
            self.edge_pass("pre", "pre", None, None)
            self.counts()
            a, n = self.a, nodes
            self.node_pass("x0", "lin", a["x"], layer=0)
            for l in range(4):
                self.self_loops(l)
                self.attention(l)
                if l < 3:
                    self.node_pass(f"g{l + 1}", "gat", None, layer=l + 1)
            self.node_pass("g4", "gat_end", a["x"], layer=4, dst=n[0])
            self.edge_pass("r0", "rel", n[0], 0)
            self.node_pass("r0n", "rel0", None, layer=0, dst=n[1], dst2=n[2])
            self.edge_pass("r1", "rel", n[2], 1)
            self.node_pass("r1n", "rel1", n[1], layer=1, dst=n[3], dst2=n[2])
            self.edge_pass("r2", "rel", n[2], 2)
            self.node_pass("r2n", "rel2", n[3], layer=2, dst=n[1], extra=n[0])
            self.edge_pass("s0", "sage", n[1], 0)
            self.node_pass("s0n", "sage0", n[1], layer=0, dst=n[2])
            self.edge_pass("s1", "sage", n[2], 1)
            self.node_pass("s1n", "sage1", n[2], layer=1, dst=n[3])
            self.edge_pass("s2", "sage", n[3], 2)
            self.node_pass("s2n", "sage2", n[3], layer=2, dst=n[0], dst2=n[2], extra=n[1])
            self.edge_pass("tp", "tp", n[2], 0)
            self.node_pass("fin", "fin", n[0], layer=0, dst=self.out)

    def records(self):
        a, C, G, NP, pre, rec_d, ident = self.a, self.C, self.G, self.NP, self.pre, self.rec_d, self.ident
        with Pass(self.nc, "rec") as q:
            zero = q.sb("zero", [P, NP // P * 8])
            rec = q.sb("rec", [P, C, REC])
            raw = q.sb("raw", [P, 3, C], I32)
            len16 = q.sb("len16", [P, C, 16])
            sh4 = q.sb("sh4", [P, C, 4])
            ea = q.sb("ea", [P, 2, KT, D])
            junk = q.sb("junk", [P, 2, 4 * KT, D])
            dots = q.sb("dots", [P, 2, KT, 4])
            wet = q.sb("wet", [P, 4, D])
            we = q.sb("we", [P, 4, D])
            att = q.sb("att", [P, 4])
            attb = q.sb("attb", [P, 4, P])
            vte = q.sb("vte", [P, 4, D])
            pst, psv = q.ps("we_t"), q.ps("vte_p")
            wld, ld, zs, zst, eld = q.sem("weights_in"), q.sem("loaded"), q.sem("zeroed"), q.sem("zero_stored"), q.sems("edges_in", 2)
            idr, wt, wts = q.sem("ident_ready"), q.sem("we_turned"), q.sem("we_kept")
            vr, vs, used = q.sem("vte_made"), q.sem("vte_kept"), q.sem("edges_used")
            ch, recr, rst, ar, rz = q.sem("dve_steps"), q.sem("rec_ready"), q.sem("rec_stored"), q.sem("att_spread"), q.sem("rec_zeroed")
            block = q.block()
            e_v = a["edge_attr_128"].rearrange("(g k p) d -> g p k d", k=KT, p=P)

            @block.sync
            def _(sp):
                sp.dma_start(we[:, :, :], a["L0_gnn_We"].rearrange("l i j -> i l j")).then_inc(wld, 16)
                sp.dma_start(att[:, :], a["L0_gnn_att_edge"]).then_inc(wld, 16)
                for g in range(2):
                    sp.dma_start(ea[:, g, :, :], e_v[g]).then_inc(eld[g], 16)
                for n, name in enumerate(("dst", "src", "edge_type_5")):
                    sp.dma_start(raw[:, n, :], a[name]).then_inc(ld, 16)
                sp.dma_start(len16[:, :, :], a["edge_attr_16"]).then_inc(ld, 16)
                sp.dma_start(sh4[:, :, :], a["edge_attr_4"]).then_inc(ld, 16)
                with sp.Fori(0, (G - 3) // 2) as i:
                    for j in range(2):
                        sp.wait_ge(used, i * 2 + j + 1)
                        sp.dma_start(ea[:, j, :, :], e_v[bass.ds(i * 2 + 2 + j, 1)].rearrange("g p k d -> (g p) k d")).then_inc(eld[j], 16)
                sp.wait_ge(used, G - 2)
                sp.dma_start(ea[:, 0, :, :], e_v[G - 1]).then_inc(eld[0], 16)
                sp.wait_ge(recr, 1)
                sp.dma_start(rec_d.rearrange("(c p) w -> p c w", p=P), rec[:, :, :]).then_inc(rst, 16)
                sp.wait_ge(rst, 16)

            @block.scalar
            def _(act):
                act.wait_ge(zs, 1)
                act.dma_start(pre.rearrange("(p n) w -> p (n w)", p=P), zero[:, :]).then_inc(zst, 16)
                act.wait_ge(wt, 1)
                act.activation(wet[:, :, :].rearrange("p l d -> p (l d)"), pst[:, :], ACT.Copy).then_inc(wts, 1)
                act.wait_ge(vr, 1)
                act.activation(vte[:, :, :].rearrange("p l d -> p (l d)"), psv[:, :], ACT.Copy).then_inc(vs, 1)
                act.wait_ge(zst, 16)

            @block.gpsimd
            def _(pool):
                pool.memset(ident[:, :], 0.0).then_inc(idr, 1)
                pool.wait_ge(idr, 1)
                pool.affine_select(out=ident[:, :], in_=ident[:, :], compare_op=ALU.not_equal, fill=1.0,
                                   base=0, pattern=[[-1, P]], channel_multiplier=1).then_inc(idr, 1)
                pool.iota(self.iota_f[:, :], [[1, P]], base=0, channel_multiplier=0, allow_small_or_imprecise_dtypes=True)
                pool.memset(self.mhalf[:, :], -0.5)
                pool.memset(self.neg1[:, :], -1.0)
                pool.memset(self.eps_t[:, :], LN_EPS)

            @block.tensor
            def _(pe):
                pe.wait_ge(idr, 2)
                pe.wait_ge(wld, 32)
                for l in range(4):
                    mm = pe.transpose(pst[:, l * D:(l + 1) * D], we[:, l, :], ident[:, :])
                mm.then_inc(wt, 1)
                pe.wait_ge(wts, 1)
                pe.wait_ge(ar, 1)
                for l in range(4):
                    mm = pe.matmul(psv[:, l * D:(l + 1) * D], attb[:, l, :], wet[:, l, :], start=True, stop=True)
                mm.then_inc(vr, 1)

            @block.vector
            def _(v):
                v.memset(zero[:, :], 0.0).then_inc(zs, 1)
                v.memset(rec[:, :, :], 0.0).then_inc(rz, 1)
                v.wait_ge(wld, 32)
                v.tensor_copy(attb[:, :, :], fan(att[:, :], P)).then_inc(ar, 1)
                v.wait_ge(rz, 1)
                v.wait_ge(vs, 1)

                def group(g, j, n, st):
                    v.wait_ge(eld[j], n)
                    if not isinstance(g, int) or g >= 2:
                        v.wait_ge(used, g - 1)
                    for k in range(KT):
                        for l in range(4):
                            m = st.mark(v.tensor_tensor_reduce(junk[:, j, 4 * k + l, :], ea[:, j, k, :], vte[:, l, :], 1.0, 0.0,
                                                               ALU.mult, ALU.add, dots[:, j, k, l:l + 1]))
                    st.need(m)
                    v.tensor_copy(rec[:, bass.ds(g * KT, KT), R_TE:R_TE + 4], dots[:, j]).then_inc(used, 1)

                def pair(i):
                    st = Chain(v, ch, i, 8 * KT)
                    for j in range(2):
                        group(i * 2 + j, j, (i + 1) * 16, st)
                    st.close()

                pair(0)
                with v.Fori(1, (G - 1) // 2) as i:
                    pair(i)
                group(G - 1, 0, ((G - 1) // 2 + 1) * 16, Chain(v, ch, (G - 1) // 2, 8 * KT))
                v.wait_ge(ld, 16 * 5)
                for n, r in enumerate((R_DST, R_SRC, R_TYPE)):
                    v.tensor_copy(rec[:, :, r], raw[:, n, :])
                v.tensor_copy(rec[:, :, R_SH:R_SH + 4], sh4[:, :, :])
                v.tensor_copy(rec[:, :, R_LEN:R_LEN + 16], len16[:, :, :])
                v.wait_ge(used, G)
                v.drain().then_inc(recr, 1)

    def order(self):
        a, C, G, ident, rec_d = self.a, self.C, self.G, self.ident, self.rec_d
        moved = self.dram("records_moved", (C * P, REC))
        with Pass(self.nc, "order") as q:
            pair_i = q.sb("pair_i", [P, 2, C], I32)
            pair = q.sb("pair", [P, 3, C])
            drops = q.sb("drops", [P, 1])
            ones = q.sb("ones", [P, 1])
            flag = q.sb("flag", [1, 1], I32)
            own_i = q.sb("own_i", [P, C], I32)
            own = q.sb("own", [P, C])
            number = q.sb("number", [P, C])
            rank = q.sb("rank", [P, C])
            rank_i = q.sb("rank_i", [P, C], U32)
            local = q.sb("local", [P, BLOCK])
            row_i = q.sb("row_i", [P, BLOCK], I32)
            row = q.sb("row", [P, BLOCK])
            before = q.sb("before", [P, BLOCK])
            hit = q.sb("hit", [P, 2, BLOCK])
            got = q.sb("got", [P, 1])
            rec = q.sb("rec", [P, REC])
            ix = q.sb("ix", [P, 1], U32)
            pd = q.ps("drops_sum")
            ld, on, io, dr, dm, fl = (q.sem(n) for n in ("loaded", "ones_ready", "numbers_ready", "drops_ready", "drops_summed", "flag_ready"))
            row_in, row_used, ch, ixr, rec_in, put, gate, mvd, num, vgate = (q.sem(n) for n in ("row_in", "row_used", "steps", "index_ready", "record_in",
                                                                                   "record_put", "gate", "records_moved", "numbers_less", "vector_gate"))
            block = q.block()

            @block.sync
            def _(sp):
                for o in range(2):
                    sp.dma_start(pair_i[:, o, :], a["dst_rows"][o:o + C * P].rearrange("(p c) -> p c", c=C)).then_inc(ld, 16)
                sp.dma_start(own_i[:, :], a["dst"]).then_inc(ld, 16)
                sp.wait_ge(fl, 1)
                unordered = sp.value_load(flag[0:1, 0:1], min_val=0, max_val=1)
                with sp.If(unordered > 0):
                    with sp.Fori(0, G) as g:
                        sp.wait_ge(row_used, g + 1)
                        sp.dma_start(row_i[:, :], a["dst_rows"][bass.ds(g * BLOCK, BLOCK)].partition_broadcast(P)).then_inc(row_in, 16)

                    def bring(c):
                        sp.wait_ge(put, c * 16)
                        sp.dma_start(rec[:, :], rec_d[bass.ds(c * P, P), :]).then_inc(rec_in, 16)

                    bring(0)
                    with sp.Fori(1, C) as c:
                        bring(c)
                    sp.wait_ge(put, C * 16)
                    sp.dma_start(rec_d.rearrange("(n p) w -> p n w", p=P), moved.rearrange("(n p) w -> p n w", p=P)).then_inc(mvd, 16)
                    sp.wait_ge(mvd, 16)

            @block.gpsimd
            def _(pool):
                pool.memset(ones[:, :], 1.0).then_inc(on, 1)
                pool.iota(number[:, :], [[P, C]], base=0, channel_multiplier=1, allow_small_or_imprecise_dtypes=True).then_inc(io, 1)
                pool.iota(local[:, :], [[1, BLOCK]], base=0, channel_multiplier=0, allow_small_or_imprecise_dtypes=True).then_inc(io, 1)
                bound = pool.to_reg(C * P - 1)
                pool.wait_ge(fl, 1)
                unordered = pool.value_load(flag[0:1, 0:1], min_val=0, max_val=1)
                with pool.If(unordered > 0):
                    with pool.Fori(0, C) as c:
                        pool.wait_ge(ixr, c + 1)
                        pool.sem_inc(gate, 1)
                        pool.wait_ge(rec_in, c * 16 + 16)
                        pool.sem_inc(gate, 1)
                        pool.indirect_dma_start(moved, bass.IndirectOffsetOnAxis(ix[:, 0:1], 0), rec[:, :], None,
                                                bounds_check=bound, oob_is_err=False).then_inc(put, 16)

            @block.tensor
            def _(pe):
                pe.wait_ge(on, 1)
                pe.wait_ge(dr, 1)
                pe.matmul(pd[0:1, 0:1], drops[:, :], ones[:, :], start=True, stop=True).then_inc(dm, 1)

            @block.vector
            def _(v):
                v.wait_ge(ld, 48)
                st = Chain(v, ch, 0, 10)
                v.tensor_copy(own[:, :], own_i[:, :])
                st.run(v.tensor_copy(pair[:, 0:2, :], pair_i[:, :, :]))
                st.run(v.tensor_tensor(pair[:, 2, :], pair[:, 0, :], pair[:, 1, :], ALU.is_gt))
                v.tensor_reduce(drops[:, :], pair[:, 2, :], AX_X, ALU.max).then_inc(dr, 1)
                v.wait_ge(dm, 1)
                v.wait_ge(io, 2)
                st.run(v.tensor_scalar(drops[0:1, :], pd[0:1, 0:1], 1.0, None, ALU.min))
                v.tensor_copy(flag[:, :], drops[0:1, :]).then_inc(fl, 1)
                st.run(v.memset(rank[:, :], 0.0))
                v.wait_ge(fl, 1)
                st.close()
                v.wait_ge(ch, 10)
                unordered = v.value_load(flag[0:1, 0:1], min_val=0, max_val=1)
                with v.If(unordered > 0):
                    v.sem_inc(row_used, 1)
                    with v.Fori(0, G) as g:
                        v.wait_ge(row_in, g * 16 + 16)
                        v.tensor_copy(row[:, :], row_i[:, :]).then_inc(row_used, 1)
                        v.wait_ge(row_used, g + 2)
                        v.sem_inc(vgate, 1)
                        with v.Fori(0, C) as c:
                            st = Chain(v, ch, g * C + c, 5)
                            st.base = st.base + 10
                            d_, n_, r_ = own[:, bass.ds(c, 1)], number[:, bass.ds(c, 1)], rank[:, bass.ds(c, 1)]
                            st.run(v.tensor_scalar(before[:, :], local[:, :], n_, None, ALU.is_lt))
                            st.mark(v.scalar_tensor_tensor(hit[:, 0, :], row[:, :], d_, before[:, :], ALU.is_equal, ALU.mult))
                            st.run(v.tensor_scalar(hit[:, 1, :], row[:, :], d_, None, ALU.is_lt))
                            st.run(v.tensor_reduce(got[:, :], hit[:, :, :].rearrange("p a n -> p (a n)"), AX_X, ALU.add))
                            st.run(v.tensor_tensor(r_, r_, got[:, :], ALU.add))
                        v.tensor_scalar(number[:, :], number[:, :], float(-BLOCK), None, ALU.add).then_inc(num, 1)
                        v.wait_ge(num, g + 1)
                    v.tensor_copy(rank_i[:, :], rank[:, :]).then_inc(fl, 1)
                    v.wait_ge(fl, 2)

                    def index(c):
                        v.wait_ge(put, c * 16)
                        v.tensor_copy(ix[:, :], rank_i[:, bass.ds(c, 1)]).then_inc(ixr, 1)

                    index(0)
                    with v.Fori(1, C) as c:
                        index(c)

    def graph(self):
        C, G, HALF, ident, rec_d, dst_d = self.C, self.G, self.HALF, self.ident, self.rec_d, self.dst_d
        with Pass(self.nc, "graph") as q:
            rec = q.sb("rec", [P, C, REC])
            dcol = q.sb("dcol", [P, C])
            drow = q.sb("drow", [HALF, 3, 2, P])
            flag = q.sb("flag", [HALF, 3, 2])
            edge_row = q.sb("edge_row", [1, 4, C])
            row_f = q.sb("row_f", [1, 3, C])
            put_r = q.sb("put_r", [HALF, 2, P])
            last_col = q.sb("last_col", [HALF, 2, P])
            sent = q.sb("sent", [1, 1])
            wide = q.sb("wide", [P, 2, KT * P])
            psr, psc, psl = q.ps("rows"), q.ps("cols"), q.ps("reach_t")
            ld, rt, rk, dst_st, dl, el = q.sem("loaded"), q.sem("rows_turned"), q.sem("rows_kept"), q.sem("dst_stored"), q.sem("neighbours_in"), q.sem("edge_row_in")
            dc, pr, pt, wl, wu, sr, ch = q.sem("dcol_ready"), q.sem("put_ready"), q.sem("put_turned"), q.sems("wide_in", 2), q.sem("wide_used"), q.sem("sent_ready"), q.sem("steps")
            lr = q.sem("reach_ready")
            block = q.block()
            body = dst_d[1:1 + C * P]

            def shifted(o):
                return dst_d[o:o + C * P].rearrange("(g r p) -> r g p", g=2, p=P)

            @block.sync
            def _(sp):
                sp.dma_start(rec[:, :, :], rec_d.rearrange("(c p) w -> p c w", p=P)).then_inc(ld, 16)
                sp.wait_ge(rk, 1)
                sp.wait_ge(sr, 1)
                sp.dma_start(shifted(1), drow[:, 1, :, :]).then_inc(dst_st, 16)
                for o in (0, C * P + 1):
                    sp.dma_start(dst_d[o:o + 1].unsqueeze(0), sent[:, :]).then_inc(dst_st, 16)
                sp.wait_ge(dst_st, 48)
                for o in (0, 2):
                    sp.dma_start(drow[:, o, :, :], shifted(o)).then_inc(dl, 16)
                for n, o in enumerate((0, 1, P, P + 1)):
                    last = dst_d[o:o + (C - 1) * P + 1:P].unsqueeze(0)
                    sp.dma_start(edge_row[:, n, :].unsqueeze(2), last.unsqueeze(2), allow_slow_non_contiguous=True).then_inc(el, 16)
                for j in range(2):
                    sp.dma_start(wide[:, j, :], body[j * BLOCK:(j + 1) * BLOCK].partition_broadcast(P)).then_inc(wl[j], 16)
                with sp.Fori(0, (G - 3) // 2) as i:
                    for j in range(2):
                        sp.wait_ge(wu, i * 2 + j + 1)
                        sp.dma_start(wide[:, j, :], body[bass.ds((i * 2 + 2 + j) * BLOCK, BLOCK)].partition_broadcast(P)).then_inc(wl[j], 16)
                sp.wait_ge(wu, G - 2)
                sp.dma_start(wide[:, 0, :], body[(G - 1) * BLOCK:].partition_broadcast(P)).then_inc(wl[0], 16)

            @block.tensor
            def _(pe):
                pe.wait_ge(dc, 1)
                for g in range(2):
                    mm = pe.transpose(psr[0:HALF, g * P:(g + 1) * P], dcol[:, g * HALF:(g + 1) * HALF], ident[:, :])
                mm.then_inc(rt, 1)
                pe.wait_ge(pr, 1)
                for g in range(2):
                    mm = pe.transpose(psc[:, g * HALF:(g + 1) * HALF], put_r[:, g, :], ident[0:HALF, 0:HALF])
                mm.then_inc(pt, 1)
                pe.wait_ge(lr, 1)
                for g in range(2):
                    mm = pe.transpose(psl[:, g * HALF:(g + 1) * HALF], last_col[:, g, :], ident[0:HALF, 0:HALF])
                mm.then_inc(pt, 1)

            @block.vector
            def _(v):
                st = Chain(v, ch, 0, 100)
                v.memset(sent[:, :], -1.0).then_inc(sr, 1)
                v.wait_ge(ld, 16)
                v.tensor_copy(dcol[:, :], rec[:, :, R_DST]).then_inc(dc, 1)
                v.tensor_copy(self.dst_i[:, :], rec[:, :, R_DST])
                v.tensor_copy(self.src_i[:, :], rec[:, :, R_SRC])
                v.tensor_copy(self.typ[:, :], rec[:, :, R_TYPE])
                v.tensor_copy(self.te[:, :, :], rec[:, :, R_TE:R_TE + 4].rearrange("p c l -> p l c"))
                v.wait_ge(rt, 1)
                v.tensor_copy(drow[:, 1, :, :].rearrange("r g p -> r (g p)"), psr[0:HALF, 0:2 * P]).then_inc(rk, 1)
                v.wait_ge(rk, 1)
                v.wait_ge(dl, 32)
                v.wait_ge(el, 64)
                st.run(v.tensor_tensor(put_r[:, :, :], drow[:, 1], drow[:, 2], ALU.is_equal))
                st.run(v.scalar_tensor_tensor(put_r[:, :, :].rearrange("r g p -> r (g p)"), put_r[:, :, :].rearrange("r g p -> r (g p)"),
                                              float(SKIP), drow[:, 1].rearrange("r g p -> r (g p)"), ALU.mult, ALU.add))
                v.sem_inc(pr, 1)
                for d, o in ((0, 0), (1, 2)):
                    st.run(v.tensor_tensor(self.pen[:, d], drow[:, 1], drow[:, o], ALU.is_equal))
                    st.run(v.tensor_tensor(flag[:, d, :].unsqueeze(2), drow[:, 1, :, (0, P - 1)[d]].unsqueeze(2),
                                           drow[:, o, :, (0, P - 1)[d]].unsqueeze(2), ALU.is_equal))
                    for g in range(2):
                        e = (0, P - 1)[d]
                        st.run(v.tensor_scalar(self.pen_carry[:, d, g, :], drow[:, 1, g, :], drow[:, 1, g, e:e + 1],
                                               flag[:, d, g:g + 1], ALU.is_equal, ALU.mult))
                    if d == 0:
                        st.run(v.memset(last_col[:, :, :], 0.0))
                        for g in range(2):
                            last = v.tensor_reduce(last_col[:, g, P - 1:P], self.pen_carry[:, 0, g, :], AX_X, ALU.add)
                        last.then_inc(lr, 1)
                    for t in (self.pen, self.pen_carry):
                        st.run(v.tensor_scalar(t[:, d], t[:, d], -1.0, BIG, ALU.add, ALU.mult))
                for n, (x, y) in enumerate(((0, 1), (3, 2), (1, 2))):
                    st.run(v.tensor_tensor(row_f[:, n, :], edge_row[:, x, :], edge_row[:, y, :], ALU.is_equal))
                for d in range(2):
                    st.run(v.tensor_tensor(self.pen_row[:, d, :], row_f[:, d, :], row_f[:, 2, :], ALU.mult))
                    st.run(v.tensor_scalar(self.pen_row[:, d, :], self.pen_row[:, d, :], -1.0, BIG, ALU.add, ALU.mult))
                v.wait_ge(pt, 2)
                v.tensor_copy(self.put_i[:, :], psc[:, 0:C])
                v.tensor_copy(self.reach[:, :], psl[:, 0:C])

                def group(g, j, n):
                    v.wait_ge(wl[j], n)
                    for k in range(KT):
                        last = v.tensor_scalar(self.same[:, bass.ds((g * KT + k) * P, P)], wide[:, j, k * P:(k + 1) * P],
                                               dcol[:, bass.ds(g * KT + k, 1)], None, ALU.is_equal)
                    last.then_inc(wu, 1)

                with v.Fori(0, (G - 1) // 2) as i:
                    for j in range(2):
                        group(i * 2 + j, j, (i + 1) * 16)
                group(G - 1, 0, ((G - 1) // 2 + 1) * 16)

    def counts(self):
        NCOL = self.NCOL
        with Pass(self.nc, "cnt") as q:
            s = q.sb("s", [P, NCOL, 8])
            c1 = q.sb("c1", [P, NCOL])
            ld, ch = q.sem("loaded"), q.sem("steps")
            block = q.block()

            @block.sync
            def _(sp):
                sp.dma_start(s[:, :, :].rearrange("p (b k) w -> p b (k w)", k=KT),
                             self.pre.rearrange("(b p k) w -> p b (k w)", p=P, k=KT)).then_inc(ld, 16)

            @block.vector
            def _(v):
                st = Chain(v, ch, 0, 100)
                v.wait_ge(ld, 16)
                st.run(v.tensor_scalar(self.no_edge[:, :], s[:, :, 4], 0.0, None, ALU.is_equal))
                st.run(v.tensor_scalar(c1[:, :], s[:, :, 4], 1.0, None, ALU.max))
                st.run(v.reciprocal(self.inv_cnt[:, :], c1[:, :]))
                for l in range(4):
                    st.run(v.tensor_tensor(self.tmean[:, l, :], s[:, :, l], self.inv_cnt[:, :], ALU.mult))

    def self_loops(self, l):
        NCOL = self.NCOL
        with Pass(self.nc, f"loop{l}") as q:
            t = q.sb("t", [P, NCOL])
            au = q.sb("au", [P, NCOL, 2])
            ch, st_ = q.sem("steps"), q.sem("stored")
            block = q.block()

            @block.vector
            def _(v):
                st = Chain(v, ch, 0, 4)
                v.tensor_copy(au[:, :, 0], self.asad[:, :, 1])
                st.run(v.tensor_tensor(t[:, :], self.asad[:, :, 0], self.asad[:, :, 1], ALU.add))
                st.run(v.tensor_tensor(t[:, :], t[:, :], self.tmean[:, l, :], ALU.add))
                st.run(v.scalar_tensor_tensor(au[:, :, 1], t[:, :], NEG_SLOPE, t[:, :], ALU.mult, ALU.max))
                v.drain().then_inc(ch, 1)

            @block.sync
            def _(sp):
                sp.wait_ge(ch, 4)
                sp.dma_start(self.aux.rearrange("(b p k) w -> p b (k w)", p=P, k=KT),
                             au[:, :, :].rearrange("p (b k) w -> p b (k w)", k=KT)).then_inc(st_, 16)
                sp.wait_ge(st_, 16)

    def attention(self, l):
        C, G, HALF, ident = self.C, self.G, self.HALF, self.ident
        with Pass(self.nc, f"att{l}") as q:
            H = q.sb("H", [P, C, AW])
            auxE = q.sb("auxE", [P, C, 2])
            lg = q.sb("lg", [P, C])
            cand = q.sb("cand", [P, C])
            pw = q.sb("pw", [P, C])
            pl = q.sb("pl", [P, C])
            with Pass(self.nc, f"gather{l}") as g_:
                hr = g_.sb("hr", [P, KT, AW])
                ar = g_.sb("ar", [P, KT, 2])
                ix = g_.sb("ix", [P, KT, 2], U32)
                gh, ga = g_.sems("h_in", KT), g_.sems("aux_in", KT)
                ixr, hk, ak, gate = g_.sem("index_ready"), g_.sem("h_kept"), g_.sem("aux_kept"), g_.sem("gate")
                block = g_.block()

                @block.gpsimd
                def _(pool):
                    bound = pool.to_reg(self.NP - 1)
                    def body(i):
                        for k in range(KT):
                            pool.wait_ge(ixr, i * KT + k + 1)
                            pool.sem_inc(gate, 1)
                            pool.wait_ge(hk, i * KT + k)
                            pool.sem_inc(gate, 1)
                            pool.wait_ge(ak, i * KT + k)
                            pool.sem_inc(gate, 1)
                            pool.indirect_dma_start(hr[:, k, :], None, self.table, bass.IndirectOffsetOnAxis(ix[:, k, 0:1], 0),
                                                    bounds_check=bound, oob_is_err=False).then_inc(gh[k], 16)
                            pool.indirect_dma_start(ar[:, k, :], None, self.aux, bass.IndirectOffsetOnAxis(ix[:, k, 1:2], 0),
                                                    bounds_check=bound, oob_is_err=False).then_inc(ga[k], 16)

                    body(0)
                    with pool.Fori(1, G) as i:
                        body(i)

                @block.scalar
                def _(act):
                    act.sem_inc(hk, KT - 1)
                    with act.Fori(0, G) as i:
                        for k in range(KT):
                            act.wait_ge(gh[k], i * 16 + 16)
                            act.activation(H[:, bass.ds(i * KT + k, 1), :], hr[:, k:k + 1, :], ACT.Copy).then_inc(hk, 1)

                @block.vector
                def _(v):
                    def index(c, k):
                        v.tensor_copy(ix[:, k, 0:1], self.src_i[:, bass.ds(c, 1)])
                        v.tensor_copy(ix[:, k, 1:2], self.dst_i[:, bass.ds(c, 1)]).then_inc(ixr, 1)

                    def body(i, last):
                        for k in range(KT):
                            v.wait_ge(ga[k], i * 16 + 16)
                            v.wait_ge(gh[k], i * 16 + 16)
                            if not last:
                                index(i * KT + KT + k, k)
                            v.tensor_copy(auxE[:, bass.ds(i * KT + k, 1), :], ar[:, k:k + 1, :]).then_inc(ak, 1)

                    v.sem_inc(ak, KT - 1)
                    for k in range(KT):
                        index(k, k)
                    with v.Fori(0, G - 1) as i:
                        body(i, False)
                    body(G - 1, True)

            with Pass(self.nc, f"soft{l}") as s_:
                lt = s_.sb("lt", [HALF, 2, P])
                F = s_.sb("F", [HALF, 2, 2, P])
                ends = s_.sb("ends", [HALF, 4])
                erow = s_.sb("erow", [1, 2, C])
                crow = s_.sb("crow", [1, 2, C + 2])
                ccol = s_.sb("ccol", [HALF, 4])
                one = s_.sb("one", [1, 2])
                psa, psb, psc, psd = (s_.ps(n) for n in ("a", "b", "c", "d"))
                ch, pe_s, ex, dn = s_.sem("steps"), s_.sem("turned"), s_.sem("exps"), s_.sem("weights_shifted")
                block = s_.block()

                @block.vector
                def _(v):
                    st = Chain(v, ch, 0, 100)
                    v.memset(one[:, :], 1.0)
                    v.memset(crow[:, :, :], -BIG)
                    st.run(v.tensor_tensor(lg[:, :], H[:, :, D], auxE[:, :, 0], ALU.add))
                    st.run(v.tensor_tensor(lg[:, :], lg[:, :], self.te[:, l, :], ALU.add))
                    st.run(v.scalar_tensor_tensor(lg[:, :], lg[:, :], NEG_SLOPE, lg[:, :], ALU.mult, ALU.max))
                    st.run(v.tensor_tensor(cand[:, :], lg[:, :], auxE[:, :, 1], ALU.max))
                    v.memset(H[:, :, D:D + 1], 1.0)
                    v.wait_ge(pe_s, 1)
                    st.run(v.tensor_copy(lt[:, :, :].rearrange("r g p -> r (g p)"), psa[0:HALF, 0:2 * P]))
                    for g in range(2):
                        v.tensor_tensor_scan(F[:, 0, g, :], self.pen[:, 0, g, :], lt[:, g, :], -BIG, ALU.add, ALU.max)
                        st.run(v.tensor_tensor_scan(backward(F[:, 1, g, :]), backward(self.pen[:, 1, g, :]), backward(lt[:, g, :]),
                                                    -BIG, ALU.add, ALU.max))
                    st.run(v.tensor_copy(ends[:, 0:2], F[:, 0, :, P - 1]))
                    st.run(v.tensor_copy(ends[:, 2:4], F[:, 1, :, 0]))
                    v.wait_ge(pe_s, 2)
                    st.run(v.tensor_copy(erow[:, :, :].rearrange("o d c -> o (d c)"), psb[0:1, 0:2 * C]))
                    v.tensor_tensor_scan(crow[:, 0, 1:C + 1], self.pen_row[:, 0, :], erow[:, 0, :], -BIG, ALU.add, ALU.max)
                    st.run(v.tensor_tensor_scan(backward(crow[:, 1, 0:C]), backward(self.pen_row[:, 1, :]), backward(erow[:, 1, :]),
                                                -BIG, ALU.add, ALU.max))
                    v.wait_ge(pe_s, 3)
                    st.run(v.tensor_copy(ccol[:, :], psc[0:HALF, 0:4]))
                    for d in range(2):
                        for g in range(2):
                            st.run(v.scalar_tensor_tensor(F[:, d, g, :], self.pen_carry[:, d, g, :], ccol[:, 2 * d + g:2 * d + g + 1],
                                                          F[:, d, g, :], ALU.add, ALU.max))
                    st.run(v.tensor_tensor(lt[:, :, :], F[:, 0], F[:, 1], ALU.max))
                    v.wait_ge(pe_s, 4)
                    v.tensor_tensor(pw[:, :], lg[:, :], psd[:, 0:C], ALU.subtract)
                    v.tensor_tensor(pl[:, :], auxE[:, :, 1], psd[:, 0:C], ALU.subtract).then_inc(dn, 1)

                @block.tensor
                def _(pe):
                    pe.wait_ge(ch, 4)
                    for g in range(2):
                        mm = pe.transpose(psa[0:HALF, g * P:(g + 1) * P], cand[:, g * HALF:(g + 1) * HALF], ident[:, :])
                    mm.then_inc(pe_s, 1)
                    pe.wait_ge(ch, 9)
                    for n in range(4):
                        mm = pe.matmul(psb[0:1, n * HALF:(n + 1) * HALF], ends[:, n:n + 1], ident[0:HALF, 0:HALF], start=True, stop=True)
                    mm.then_inc(pe_s, 1)
                    pe.wait_ge(ch, 11)
                    for d in range(2):
                        for g in range(2):
                            o = g * HALF + d
                            mm = pe.matmul(psc[0:HALF, 2 * d + g:2 * d + g + 1], crow[:, d, o:o + HALF], one[:, 0:1], start=True, stop=True)
                    mm.then_inc(pe_s, 1)
                    pe.wait_ge(ch, 17)
                    for g in range(2):
                        mm = pe.transpose(psd[:, g * HALF:(g + 1) * HALF], lt[:, g, :], ident[0:HALF, 0:HALF])
                    mm.then_inc(pe_s, 1)

                @block.scalar
                def _(act):
                    act.wait_ge(dn, 1)
                    act.activation(pw[:, :], pw[:, :], ACT.Exp)
                    act.activation(pl[:, :], pl[:, :], ACT.Exp)

            self.edge_pass(f"sum{l}", "gat", H, l, weights=pw, loop_w=pl)

    def edge_pass(self, name, kind, table, layer, weights=None, loop_w=None):
        nc, a, C, G, ident = self.nc, self.a, self.C, self.G, self.ident
        gathers = kind in ("rel", "sage", "tp")
        two_step = gathers
        side = kind in ("rel", "tp")
        halves = 2 if kind == "tp" else 1
        W = {"pre": 5, "gat": D + 1, "rel": D, "sage": D, "tp": D + 1}[kind]
        OW = 8 if kind == "pre" else AW
        dest = self.pre if kind == "pre" else self.agg
        with Pass(nc, name) as q:
            outs = q.sb("outs", [P, KT, OW])
            sf = q.sb("sf", [P, KT, P])
            link = q.sb("link", [P, KT, P])
            pix = q.sb("pix", [P, KT], U32)
            pso = [q.ps(f"o{k}") for k in range(2)]
            if kind == "pre":
                m5 = q.sb("m5", [P, KT, 8])
            if gathers:
                gr = q.sb("gr", [P, KT, D])
                gix = q.sb("gix", [P, KT], U32)
                msg = q.sb("msg", [P, KT, 2 if kind == "tp" else 1, D])
                aT = q.sb("aT", [P, 2, halves * P])
                Wm = q.sb("Wm", [P, halves, W])
                psa = [q.ps(f"a{k}") for k in range(2)]
            if kind == "rel":
                relb = q.sb("relb", [KT * 8, KT * D])
                iota8 = q.sb("iota8", [P, 8])
                sd = q.sb("sd", [P, KT * 8])
                sdT = q.sb("sdT", [KT * 8, P])
                psr, pst = q.ps("rel"), q.ps("sideT")
                sw = KT * 8
            if kind == "tp":
                rec = q.sb("rec", [P, C, REC])
                sd = q.sb("sd", [P, KT * 16])
                sdT = q.sb("sdT", [KT * 16, P])
                W1 = q.sb("W1", [KT * 16, KT, 64])
                W2 = q.sb("W2", [64, D + 64])
                hs = q.sb("hs", [64, KT, P])
                tA = q.sb("tA", [P, 2, D])
                psh, psw = q.ps("hid"), [q.ps(f"wexp{k}") for k in range(2)]
                sw = KT * 16
            gin, sst = q.sems("rows_in", KT), q.sems("sums_stored", KT)
            gixr, gate, pgate = q.sem("gather_index"), q.sem("gate"), q.sem("tensor_gate")
            sfr, linkr, msgr, turned, kept = q.sem("same_ready"), q.sem("link_ready"), q.sem("messages"), q.sem("sums_turned"), q.sem("turned_kept")
            outm, evac = q.sem("sums_made"), q.sem("sums_out")
            extra, cst, ch, added = q.sem("last_columns"), q.sem("constants"), q.sem("dve_steps"), q.sem("relation_added")
            sdr, sdt, sdk, relm, hidm, hidk, wxm, init = (q.sem(n) for n in ("side_ready", "side_turned", "side_kept", "relations",
                                                                           "hidden_made", "hidden_kept", "weights_made", "cleared"))
            block = q.block()
            cleared = 2 if kind == "pre" else 1

            @block.sync
            def _(sp):
                if kind == "rel":
                    sp.dma_start(relb[:, :], a["L1_gnn_relvecs"][layer]).then_inc(cst, 16)
                    sp.dma_start(Wm[:, 0, :], a["L1_gnn_lin_w"][layer]).then_inc(cst, 16)
                    sp.dma_start(iota8[:, :], a["iota8"]).then_inc(cst, 16)
                if kind == "sage":
                    sp.dma_start(Wm[:, 0, :], a[f"L2_gnn_Wn{layer}"]).then_inc(cst, 16)
                if kind == "tp":
                    sp.dma_start(rec[:, :, :], self.rec_d.rearrange("(c p) w -> p c w", p=P)).then_inc(cst, 16)
                    sp.dma_start(W1[:, :, :], a["L3_gnn_W_mlp1"]).then_inc(cst, 16)
                    sp.dma_start(W2[:, :], a["L3_gnn_W_mlp2"]).then_inc(cst, 16)
                    sp.dma_start(Wm[:, :, :], a["L3_out"]).then_inc(cst, 16)

            n_cst = {"rel": 3, "sage": 1, "tp": 4}.get(kind, 0) * 16

            @block.gpsimd
            def _(pool):
                bound_g, bound_s = pool.to_reg(self.NP - 1), pool.to_reg(self.NP - 1)

                def gather(cnt, k):
                    pool.wait_ge(gixr, cnt + 1)
                    pool.sem_inc(gate, 1)
                    if not isinstance(cnt, int) or cnt >= KT:
                        if kind == "sage":
                            pool.wait_ge(turned, cnt)
                        else:
                            pool.wait_ge(msgr, cnt - 3)
                        pool.sem_inc(gate, 1)
                    pool.indirect_dma_start(gr[:, k, :], None, table, bass.IndirectOffsetOnAxis(gix[:, k:k + 1], 0),
                                            bounds_check=bound_g, oob_is_err=False).then_inc(gin[k], 16)

                def scatter(cnt, k):
                    pool.wait_ge(extra, cnt + 1)
                    pool.sem_inc(gate, 1)
                    pool.wait_ge(evac, cnt + 3)
                    pool.sem_inc(gate, 1)
                    pool.indirect_dma_start(dest, bass.IndirectOffsetOnAxis(pix[:, k:k + 1], 0), outs[:, k, :], None,
                                            bounds_check=bound_s, oob_is_err=False).then_inc(sst[k], 16)

                if gathers:
                    for k in range(KT):
                        gather(k, k)

                    def both(i, first=False):
                        for k in range(KT):
                            gather((i + 1) * KT + k, k)
                            if not (first and k < LATE):
                                scatter(i * KT + (k - LATE), (k - LATE) % KT)

                    both(0, True)
                    with pool.Fori(1, G - 1) as i:
                        both(i)
                    for c in range(C - KT - LATE, C):
                        scatter(c, c % KT)
                else:
                    with pool.Fori(0, G) as i:
                        for k in range(KT):
                            scatter(i * KT + k, k)
                for k in range(KT):
                    pool.wait_ge(sst[k], 16 * G)

            @block.vector
            def _(v):
                v.memset(outs[:, :, :], 0.0).then_inc(init, 1)
                if kind == "pre":
                    v.memset(m5[:, :, :], 1.0).then_inc(init, 1)
                v.wait_ge(init, cleared)
                if n_cst:
                    v.wait_ge(cst, n_cst)
                if kind == "tp":
                    v.tensor_scalar(Wm[:, :, :], Wm[:, :, :], 1.0 / 8 / 4 / 8, None, ALU.mult).then_inc(init, 1)
                    v.wait_ge(init, 2)
                    v.tensor_scalar(Wm[0:MUL, 1, :], Wm[0:MUL, 1, :], 3.0 ** -0.5, None, ALU.mult).then_inc(init, 1)
                    v.wait_ge(init, 3)

                def g_index(c, k):
                    v.tensor_copy(gix[:, k:k + 1], self.src_i[:, bass.ds(c, 1)]).then_inc(gixr, 1)

                def side_of(g):
                    if kind == "rel":
                        v.tensor_tensor(sd[:, :].rearrange("p (k t) -> p k t", k=KT), fan(self.typ[:, bass.ds(g * KT, KT)], 8),
                                        spread(iota8[:, :], KT), ALU.is_equal).then_inc(sdr, 1)
                    else:
                        v.tensor_copy(sd[:, :].rearrange("p (k t) -> p k t", k=KT),
                                      rec[:, bass.ds(g * KT, KT), R_LEN:R_LEN + 16]).then_inc(sdr, 1)

                PER = 4 * KT

                def body(i, last):
                    st = Chain(v, ch, i, PER) if kind == "tp" else None
                    for k in range(KT):
                        c = i * KT + k
                        if gathers:
                            v.wait_ge(gin[k], i * 16 + 16)
                            if not last:
                                g_index(c + KT, k)
                        if side and not last and k == 0:
                            v.wait_ge(sdt, i + 1)
                            side_of(i + 1)
                        if kind == "gat":
                            v.wait_ge(outm, i * KT + k)
                            v.tensor_scalar(sf[:, k, :], self.same[:, bass.ds(c * P, P)], weights[:, bass.ds(c, 1)], None,
                                            ALU.mult).then_inc(sfr, 1)
                        if kind == "pre":
                            v.wait_ge(outm, i * KT + k)
                            v.tensor_copy(m5[:, k, 0:4], self.te[:, :, bass.ds(c, 1)].rearrange("p l o -> p (l o)")).then_inc(msgr, 1)
                        if kind == "rel":
                            v.wait_ge(relm, i + 1)
                            v.wait_ge(turned, i * KT + k)
                            v.tensor_tensor(msg[:, k, 0, :], gr[:, k, :], psr[:, k * D:(k + 1) * D], ALU.add).then_inc(added, 1)
                        if kind == "tp":
                            v.wait_ge(wxm, i * KT + k + 1)
                            v.wait_ge(turned, i * KT + k)
                            wx = psw[k % 2][:, 0:192]
                            sh = rec[:, bass.ds(c, 1), R_SH:R_SH + 4].rearrange("p o w -> p (o w)")
                            g1 = gr[:, k, MUL:].rearrange("p (u m) -> p u m", m=3)
                            t3 = tA[:, k % 2, MUL:].rearrange("p (u m) -> p u m", m=3)
                            n1 = st.mark(v.tensor_tensor(t3, g1, spread(sh[:, 1:4], MUL), ALU.mult))
                            n2 = st.mark(v.tensor_tensor(tA[:, k % 2, 0:MUL], gr[:, k, 0:MUL], wx[:, D + MUL:D + 2 * MUL], ALU.mult))
                            v.scalar_tensor_tensor(msg[:, k, 0, :], gr[:, k, :], sh[:, 0:1], wx[:, 0:D], ALU.mult, ALU.mult)
                            st.need(n1)
                            n3 = st.mark(v.tensor_reduce(msg[:, k, 1, 0:MUL], t3, AX_X, ALU.add))
                            st.need(n2)
                            v.tensor_tensor(msg[:, k, 1, MUL:].rearrange("p (u m) -> p u m", m=3), fan(tA[:, k % 2, 0:MUL], 3),
                                            spread(sh[:, 1:4], MUL), ALU.mult)
                            st.need(n3)
                            v.tensor_tensor(msg[:, k, 1, 0:MUL], msg[:, k, 1, 0:MUL], wx[:, D:D + MUL], ALU.mult).then_inc(msgr, 1)
                        v.wait_ge(outm, i * KT + k)
                        v.tensor_scalar(link[LAST, k, :], self.iota_f[LAST, :], self.reach[LAST, bass.ds(c, 1)], None,
                                        ALU.is_lt).then_inc(linkr, 1)
                        v.wait_ge(sst[k], i * 16)
                        if kind == "gat":
                            v.tensor_copy(outs[:, k, D + 1:D + 2], loop_w[:, bass.ds(c, 1)])
                        v.tensor_copy(pix[:, k:k + 1], self.put_i[:, bass.ds(c, 1)]).then_inc(extra, 1)
                    if st:
                        st.close()

                if gathers:
                    for k in range(KT):
                        g_index(k, k)
                if side:
                    side_of(0)
                body(0, False)
                with v.Fori(1, G - 1) as i:
                    body(i, False)
                body(G - 1, True)

            @block.scalar
            def _(act):
                act.sem_inc(evac, 2)
                if n_cst:
                    act.wait_ge(cst, n_cst)
                act.wait_ge(init, cleared)

                def side_keep(i):
                    act.wait_ge(sdt, i + 1)
                    act.activation(sdT[:, :], (pst if kind == "rel" else psh)[0:sw, 0:P], ACT.Copy).then_inc(sdk, 1)

                def hidden(i):
                    act.wait_ge(hidm, i + 1)
                    act.activation(hs[:, :, :].rearrange("h k e -> h (k e)"), psh[0:64, :], ACT.Silu, scale=0.25).then_inc(hidk, 1)

                def prepare(c, k):
                    if kind != "gat":
                        act.wait_ge(outm, c)
                        act.activation(sf[:, k, :], self.same[:, bass.ds(c * P, P)], ACT.Copy).then_inc(sfr, 1)
                    if kind == "rel":
                        act.wait_ge(added, c + 1)
                        act.activation(msg[:, k, 0, :], msg[:, k, 0, :], ACT.Relu).then_inc(msgr, 1)

                def keep(c, k):
                    act.wait_ge(turned, c + KT)
                    act.activation(aT[:, k % 2, :], psa[k % 2][:, 0:halves * P], ACT.Copy).then_inc(kept, 1)

                def body(i, last):
                    for k in range(KT):
                        c = i * KT + k
                        if not (last and k >= KT - 2):
                            prepare(c + 2, (k + 2) % KT)
                        if two_step and not (last and k == KT - 1):
                            keep(c + 1, k + 1)
                        if side and not last and k == 0:
                            side_keep(i + 1)
                        if kind == "tp" and not last and k == 1:
                            hidden(i + 1)
                        act.wait_ge(outm, c + KT)
                        act.wait_ge(sst[k], i * 16)
                        act.activation(outs[:, k, 0:W], pso[k % 2][:, 0:W], ACT.Copy).then_inc(evac, 1)

                if side:
                    side_keep(0)
                if kind == "tp":
                    hidden(0)
                prepare(0, 0)
                prepare(1, 1)
                if two_step:
                    keep(0, 0)
                body(0, False)
                with act.Fori(1, G - 1) as i:
                    body(i, False)
                body(G - 1, True)

            @block.tensor
            def _(pe):
                pe.sem_inc(outm, KT - 1)
                pe.wait_ge(init, cleared)
                if two_step:
                    pe.sem_inc(turned, KT - 1)
                if n_cst:
                    pe.wait_ge(cst, n_cst)
                if kind == "tp":
                    pe.wait_ge(init, 3)

                def until(sem, n):
                    pe.wait_ge(sem, n)
                    pe.sem_inc(pgate, 1)

                def side_turn(i):
                    until(sdr, i + 1)
                    if kind == "tp":
                        until(hidk, i)
                    pe.transpose((pst if kind == "rel" else psh)[0:sw, 0:P], sd[:, :], ident[:, :]).then_inc(sdt, 1)

                def side_use(i):
                    until(sdk, i + 1)
                    if kind == "rel":
                        until(msgr, i * KT)
                        pe.matmul(psr[:, :], sdT[:, :], relb[:, :], start=True, stop=True).then_inc(relm, 1)
                    else:
                        for k in range(KT):
                            mm = pe.matmul(psh[0:64, k * P:(k + 1) * P], W1[:, k, :], sdT[:, :], start=True, stop=True)
                        mm.then_inc(hidm, 1)

                def path_weights(c, k, i):
                    if k % KT == 0:
                        until(hidk, i + 1)
                    if not isinstance(c, int) or c >= 2:
                        until(msgr, c - 1)
                    pe.matmul(psw[k % 2][:, 0:192], hs[:, k % KT, :], W2[:, :], start=True, stop=True).then_inc(wxm, 1)

                def turn(c, k, it):
                    pe.wait_ge(sfr, c + 1)
                    if kind == "sage":
                        pe.wait_ge(gin[k], it * 16 + 16)
                    else:
                        pe.wait_ge(msgr, c + 1)
                    if not isinstance(c, int) or c >= 2:
                        pe.wait_ge(kept, c - 1)
                    for h in range(halves):
                        lhs = gr[:, k, :] if kind == "sage" else msg[:, k, h, :]
                        mm = pe.matmul(psa[k % 2][:, h * P:(h + 1) * P], lhs, sf[:, k, :], start=True, stop=True)
                    mm.then_inc(turned, 1)

                def sums(c, k):
                    pe.wait_ge(evac, c + 1)
                    if two_step:
                        pe.wait_ge(kept, c + 1)
                        pairs = [(aT[:, k % 2, h * P:(h + 1) * P], Wm[:, h, :]) for h in range(halves)]
                    elif kind == "gat":
                        pe.wait_ge(sfr, c + 1)
                        pairs = [(sf[:, k, :], table[:, bass.ds(c, 1), 0:W].rearrange("p o w -> p (o w)"))]
                    else:
                        pe.wait_ge(sfr, c + 1)
                        pe.wait_ge(msgr, c + 1)
                        pairs = [(sf[:, k, :], m5[:, k, 0:W])]
                    for n, (x, y) in enumerate(pairs):
                        pe.matmul(pso[k % 2][:, 0:W], x, y, start=(n == 0), stop=False)
                    pe.wait_ge(evac, c + 2)
                    pe.wait_ge(linkr, c + 1)
                    pe.matmul(pso[k % 2][:, 0:W], link[LAST, k, :], outs[LAST, (k - 1) % KT, 0:W], start=False, stop=True).then_inc(outm, 1)

                def body(i, last):
                    for k in range(KT):
                        c = i * KT + k
                        if side and not last and k == 0:
                            side_turn(i + 1)
                        sums(c, k)
                        if two_step and not (last and k >= KT - 2):
                            turn(c + 2, (k + 2) % KT, i + (k + 2) // KT)
                        if kind == "tp" and not (last and k >= 1):
                            path_weights(c + 3, k + 3, i + (k + 3) // KT)
                        if side and not last and k == (0 if kind == "tp" else 1):
                            side_use(i + 1)

                if side:
                    side_turn(0)
                    side_use(0)
                for c in range(2):
                    if kind == "tp":
                        path_weights(c, c, 0)
                    if two_step:
                        turn(c, c, 0)
                if kind == "tp":
                    path_weights(2, 2, 0)
                body(0, False)
                with pe.Fori(1, G - 1) as i:
                    body(i, False)
                body(G - 1, True)

    def node_pass(self, name, kind, src, layer, dst=None, dst2=None, extra=None):
        nc, a, NBLK, ident = self.nc, self.a, self.NBLK, self.ident
        gat, rel, sage = kind in ("gat", "gat_end"), kind[:3] == "rel", kind[:4] == "sage"
        linear = kind in ("lin", "gat")
        two_norms = kind in ("gat_end", "rel2")
        normed = kind not in ("lin", "sage0", "sage1")
        affine = kind == "gat_end" or rel
        relu2 = kind in ("rel0", "rel1")
        src_w = AW if gat else D
        res_w = AW if linear else D
        with Pass(nc, name) as q:
            x = q.sb("x", [P, 4, KT, src_w])
            ag = q.sb("ag", [P, 4, KT, AW])
            ex = q.sb("ex", [P, 4, KT, D])
            y = q.sb("y", [P, 4, KT, D])
            z = q.sb("z", [P, 4, KT, D])
            res = q.sb("res", [P, 4, KT, res_w])
            res2 = q.sb("res2", [P, 4, KT, D])
            xT = q.sb("xT", [P, 2, KT, P])
            zT = q.sb("zT", [P, 2, KT, P])
            bn = q.sb("bn", [P, 4, 2, KT, 6])
            mv = q.sb("mv", [P, 4, 2, KT, 2])
            rs = q.sb("rs", [P, 4, 2, 4, KT])
            sm = q.sb("sm", [P, 4, 3, KT])
            bias = q.sb("bias", [P, D])
            ln_w = q.sb("ln_w", [P, 2, D])
            ln_c = q.sb("ln_c", [P, 2])
            Wn = q.sb("Wn", [P, D])
            WT = q.sb("WT", [P, D])
            att = q.sb("att", [P, 2])
            Wl = q.sb("Wl", [P, 2 * D])
            na = q.sb("na", [P, NBLK * KT])
            pT = [q.ps(f"T{j}") for j in range(2)]
            pM = [[q.ps(f"M{j}{h}") for h in range(2)] for j in range(2)]
            pN = [q.ps(f"N{j}") for j in range(2)]
            lin_, exin, stored, stored2 = q.sems("rows_in", 4), q.sems("outer_rows_in", 4), q.sems("result_stored", 4), q.sems("second_stored", 4)
            cst, wat, wak, wam, wrd = (q.sem(n) for n in ("constants", "w_turned", "w_kept", "w_att", "w_ready"))
            names = ("scale_ready", "normed", "affine_done", "scale2_ready", "result_ready", "second_ready",
                     "turned", "turned_kept", "product_made", "turned2", "turned2_kept", "product2_made", "bias_added",
                     "weight_ready", "total_ready", "reciprocal_ready", "mixed", "stats_made", "aggregated", "deviation_ready",
                     "weighted", "outer_added", "stats2_made", "aggregated2", "deviation2_ready", "total_added", "variance_ready", "variance2_ready")
            (sr, zr, af, sr2, rr, rr2, tr, tk, mr, tr2, tk2, mr2, bx, wa, wb, wc, mx, bs, ag_, dv, aw, ao, bs2, ag2, dv2,
             tb, ep, ep2) = [q.sem(n) for n in names]
            gate, zrd, zst = q.sem("gate"), q.sem("zeros_ready"), q.sem("zeros_stored")
            block = q.block()

            def done(eng, sem, b, back=0):
                if not isinstance(b.n, int) or b.n >= back:
                    eng.wait_ge(sem, b.n + (1 - back))

            def stored_all(eng, sems, b):
                if not isinstance(b.n, int) or b.n >= 4:
                    eng.wait_ge(sems[b.s4], b.t4 * 16)

            def times(eng, steps):
                span = max(lag for _, lag in steps)

                def at_time(t, i=None, m=0):
                    for step, lag in steps:
                        if i is not None:
                            step(Block(t - lag, i, m - lag))
                        elif 0 <= t - lag < NBLK:
                            step(Block(t - lag, 0, t - lag))

                for t in range(PEEL):
                    at_time(t)
                with eng.Fori(0, (NBLK - PEEL) // 4) as i:
                    for u in range(4):
                        at_time(i * 4 + (PEEL + u), i, PEEL + u)
                for t in range(NBLK, NBLK + span):
                    at_time(t)

            consts = []
            if gat or rel:
                r, pre = (layer - 1, "L0_gnn_") if gat else (layer, "L1_gnn_")
                consts.append((bias[:, :], a[pre + ("bias" if gat else "lin_b")][r].partition_broadcast(P)))
                if affine:
                    g_, b_ = ("ln_gamma", "ln_beta") if gat else ("ln_w", "ln_b")
                    consts.append((ln_w[:, 0, :], a[pre + g_][r].partition_broadcast(P)))
                    consts.append((ln_w[:, 1, :], a[pre + b_][r].partition_broadcast(P)))
                if kind == "gat":
                    consts.append((ln_c[:, :], a["L0_ln_cols"][r]))
            if sage:
                consts.append((bias[:, :], a[f"L2_gnn_b{layer}"].partition_broadcast(P)))
                consts.append((Wn[:, :], a[f"L2_gnn_Ws{layer}"]))
            if linear:
                consts.append((Wl[:, 0:D], a["L0_gnn_W"][layer]))
                consts.append((att[:, :], a["L0_att_cols"][layer]))
            if kind == "sage2":
                consts.append((Wl[:, :], a["L3_in"]))
            if kind in ("sage2", "fin"):
                consts.append((na[:, :], a["node_vec1"]))
            loads = []
            if kind != "rel0":
                loads.append((x, self.table if gat else src, src_w))
            if kind != "lin":
                loads.append((ag, self.agg, AW))
            if kind == "sage2":
                loads.append((ex, extra, D))
            outer = [(ex, extra if extra is not None else src, D)] if two_norms else []
            last_use = tr if kind == "lin" else tb if kind in ("sage1", "sage2") else mx
            lag_store, lag_second = (9, 9) if kind == "sage2" else (4, 8) if relu2 else (5, 8) if kind == "lin" else (8, 8)
            first = dst if not linear else self.table
            second = dst2
            first_buf = y if relu2 else res

            def at(ap, n):
                return ap.rearrange("(b p k) d -> b p k d", p=P, k=KT)[bass.ds(n, 1)].rearrange("b p k d -> (b p) k d")

            @block.sync
            def _(sp):
                for t_, s_ in consts:
                    sp.dma_start(t_, s_).then_inc(cst, 16)

                def load(b):
                    done(sp, last_use, b, 4)
                    for buf, ap, w in loads:
                        sp.dma_start(buf[:, b.s4, :, :], at(ap, b.n)).then_inc(lin_[b.s4], 16)

                def load_outer(b):
                    done(sp, ao, b, 4)
                    for buf, ap, w in outer:
                        sp.dma_start(buf[:, b.s4, :, :], at(ap, b.n)).then_inc(exin[b.s4], 16)

                def store_zeros(b):
                    sp.dma_start(at(self.agg, b.n), ag[:, 0, :, :]).then_inc(zst, 16)

                def store(b):
                    done(sp, (mx if kind == "rel0" else tb) if relu2 else af if kind == "sage2" else rr, b)
                    sp.dma_start(at(first, b.n), first_buf[:, b.s4, :, :]).then_inc(stored[b.s4], 16)

                def store_second(b):
                    done(sp, rr2, b)
                    sp.dma_start(at(second, b.n), res2[:, b.s4, :, :]).then_inc(stored2[b.s4], 16)

                if kind == "lin":
                    sp.wait_ge(zrd, 1)
                times(sp, [(load, 0)] + ([(store_zeros, 0)] if kind == "lin" else []) + ([(load_outer, 3)] if outer else []) + [(store, lag_store)] +
                      ([(store_second, lag_second)] if second is not None else []))
                if kind == "lin":
                    sp.wait_ge(zst, NBLK * 16)
                for j in range(4):
                    n = len(range(j, NBLK, 4)) * 16
                    sp.wait_ge(stored[j], n)
                    if second is not None:
                        sp.wait_ge(stored2[j], n)

            def arrived(eng, b):
                eng.wait_ge(lin_[b.s4], (b.t4 + 1) * 16 * len(loads))

            @block.tensor
            def _(pe):
                pe.wait_ge(cst, 16 * len(consts))
                if linear:
                    pe.transpose(pT[0][:, 0:D], Wl[:, 0:D], ident[:, :]).then_inc(wat, 1)
                    pe.wait_ge(wak, 1)
                    pe.matmul(pN[0][:, 0:2], WT[:, :], att[:, :], start=True, stop=True).then_inc(wam, 1)
                    pe.wait_ge(wrd, 1)

                def turn_x(b):
                    arrived(pe, b)
                    done(pe, tk, b, 2)
                    if kind == "sage2":
                        done(pe, tk2, b, 4)
                    for k in range(KT):
                        mm = pe.transpose(pT[b.s2][:, k * P:(k + 1) * P], x[:, b.s4, k, 0:D], ident[:, :])
                    mm.then_inc(tr, 1)

                def turn_z(b):
                    done(pe, zr, b)
                    done(pe, tk2, b, 2)
                    for k in range(KT):
                        mm = pe.transpose(pT[b.s2][:, k * P:(k + 1) * P], z[:, b.s4, k, :], ident[:, :])
                    mm.then_inc(tr2, 1)

                def own(b):
                    done(pe, tk, b)
                    done(pe, mx, b, 2)
                    for k in range(KT):
                        mm = pe.matmul(pN[b.s2][:, k * D:(k + 1) * D], xT[:, b.s2, k, :], Wn[:, :], start=True, stop=True)
                    mm.then_inc(mr, 1)

                def product(b):
                    w = AW if linear else 2 * D
                    done(pe, tk if kind == "lin" else tk2, b)
                    done(pe, rr if linear else rr2, b, 2)
                    if kind == "sage2":
                        done(pe, af, b, 2)
                    for k in range(KT):
                        mm = pe.matmul(pM[b.s2][k // 2][:, (k % 2) * w:(k % 2 + 1) * w], (xT if kind == "lin" else zT)[:, b.s2, k, :],
                                       Wl[:, 0:w], start=True, stop=True)
                    mm.then_inc(mr2, 1)

                steps = {"lin": [(turn_x, 0), (product, 1)], "gat": [(turn_z, 0), (product, 0)],
                         "sage0": [(turn_x, 0), (own, 1)], "sage1": [(turn_x, 0), (own, 1)],
                         "sage2": [(turn_x, 0), (own, 0), (product, 4), (turn_z, 3)]}.get(kind)
                if steps:
                    times(pe, steps)

            @block.gpsimd
            def _(pool):
                pool.wait_ge(cst, 16 * len(consts))

                def scale(stage):
                    def step(b):
                        done(pool, (ag_, ag2)[stage], b)
                        t = rs[:, b.s4, stage]
                        pool.tensor_tensor(t[:, 2, :], mv[:, b.s4, stage, :, 1], self.eps_t[:, :], ALU.add).then_inc((ep, ep2)[stage], 1)
                        done(pool, (ep, ep2)[stage], b)
                        pool.tensor_tensor(t[:, 0, :], t[:, 2, :], self.mhalf[:, :], ALU.pow)
                        pool.tensor_tensor(t[:, 3, :], mv[:, b.s4, stage, :, 0], self.neg1[:, :], ALU.mult).then_inc((dv, dv2)[stage], 1)
                        done(pool, (dv, dv2)[stage], b)
                        pool.tensor_tensor(t[:, 1, :], t[:, 3, :], t[:, 0, :], ALU.mult).then_inc((sr, sr2)[stage], 1)
                    return step

                def outer_bias(b):
                    pool.wait_ge(exin[b.s4], (b.t4 + 1) * 16)
                    pool.tensor_tensor(ex[:, b.s4], ex[:, b.s4], spread(ln_w[:, 1, :], KT), ALU.add).then_inc(bx, 1)

                def rows_bias(b):
                    arrived(pool, b)
                    if kind == "sage1":
                        done(pool, tb, b, 4)
                        pool.tensor_tensor(z[:, b.s4], x[:, b.s4], spread(bias[:, :], KT), ALU.add).then_inc(bx, 1)
                    else:
                        pool.tensor_tensor(ex[:, b.s4], ex[:, b.s4], spread(bias[:, :], KT), ALU.add).then_inc(bx, 1)

                def affine_bias(b):
                    done(pool, aw, b)
                    pool.tensor_tensor(z[:, b.s4], z[:, b.s4], spread(ln_w[:, 1, :], KT), ALU.add).then_inc(af, 1)

                steps = {"gat": [(scale(0), 0)], "fin": [(scale(0), 0)], "gat_end": [(scale(1), 3), (scale(0), 0), (outer_bias, 1)],
                         "rel2": [(scale(1), 3), (scale(0), 0), (outer_bias, 1)],
                         "rel0": [(affine_bias, 3), (scale(0), 0)], "rel1": [(affine_bias, 3), (scale(0), 0)],
                         "sage1": [(rows_bias, 0)], "sage2": [(rows_bias, 0), (scale(0), 2)]}.get(kind)
                if steps:
                    times(pool, steps)

            @block.vector
            def _(v):
                if kind == "lin":
                    v.memset(ag[:, 0, :, :], 0.0).then_inc(zrd, 1)
                v.wait_ge(cst, 16 * len(consts))
                if linear:
                    v.wait_ge(wat, 1)
                    v.tensor_copy(WT[:, :], pT[0][:, 0:D]).then_inc(wak, 1)
                    v.wait_ge(wam, 1)
                    v.tensor_copy(Wl[:, D:AW], pN[0][:, 0:2]).then_inc(wrd, 1)
                if kind == "sage2":
                    v.tensor_scalar(na[:, :], na[:, :], MUL ** -0.5, None, ALU.mult).then_inc(wrd, 1)
                    v.wait_ge(wrd, 1)
                if kind == "fin":
                    v.tensor_tensor(na[:, :], na[:, :], na[:, :], ALU.mult).then_inc(wrd, 1)
                    v.wait_ge(wrd, 1)

                def weight(b):
                    arrived(v, b)
                    done(v, mx, b, 4)
                    cols = bass.ds(b.n * KT, KT)
                    to = sm[:, b.s4, 0, :]
                    if gat:
                        v.tensor_tensor(to, ag[:, b.s4, :, D + 1], self.no_edge[:, cols], ALU.add).then_inc(wa, 1)
                    elif kind == "fin":
                        v.tensor_tensor(to, ag[:, b.s4, :, D], na[:, cols], ALU.mult).then_inc(wa, 1)
                    else:
                        v.tensor_copy(to, self.inv_cnt[:, cols]).then_inc(wa, 1)

                def total(b):
                    done(v, wa, b)
                    v.scalar_tensor_tensor(sm[:, b.s4, 1, :], sm[:, b.s4, 0, :], 1e-16, ag[:, b.s4, :, D], ALU.add, ALU.add).then_inc(wb, 1)

                def reciprocal(b):
                    done(v, wb, b)
                    v.reciprocal(sm[:, b.s4, 2, :], sm[:, b.s4, 1, :]).then_inc(wc, 1)

                def mix(b):
                    j = b.s4
                    arrived(v, b)
                    done(v, wa, b)
                    done(v, rr if kind in ("fin", "sage0", "sage1") else zr, b, 4)
                    if relu2:
                        stored_all(v, stored, b)
                    if sage:
                        done(v, mr, b)
                    for k in range(KT):
                        if gat:
                            last = v.scalar_tensor_tensor(y[:, j, k, :], x[:, j, k, 0:D], sm[:, j, 0, k:k + 1], ag[:, j, k, 0:D],
                                                          ALU.mult, ALU.add)
                        else:
                            to = bias[:, :] if kind == "rel0" else pN[b.s2][:, k * D:(k + 1) * D] if sage else x[:, j, k, :]
                            last = v.scalar_tensor_tensor(y[:, j, k, :], ag[:, j, k, 0:D], sm[:, j, 0, k:k + 1], to, ALU.mult, ALU.add)
                    last.then_inc(mx, 1)

                def complete(b):
                    j = b.s4
                    done(v, mx, b)
                    if gat:
                        done(v, wc, b)
                        for k in range(KT):
                            last = v.scalar_tensor_tensor(y[:, j, k, :], y[:, j, k, :], sm[:, j, 2, k:k + 1], bias[:, :], ALU.mult, ALU.add)
                    elif kind in ("sage1", "sage2"):
                        done(v, bx, b)
                        last = v.tensor_tensor(y[:, j], y[:, j], (z if kind == "sage1" else ex)[:, j], ALU.add)
                    else:
                        last = v.tensor_tensor(y[:, j], y[:, j], spread(bias[:, :], KT), ALU.add)
                    last.then_inc(tb, 1)

                def stats(stage):
                    def step(b):
                        done(v, (mx if kind in ("rel0", "fin") else tb, ao)[stage], b)
                        for k in range(KT):
                            last = v.bn_stats(bn[:, b.s4, stage, k, :], (y, z)[stage][:, b.s4, k, :])
                        last.then_inc((bs, bs2)[stage], 1)
                    return step

                def aggregate(stage):
                    def step(b):
                        done(v, (bs, bs2)[stage], b)
                        v.sem_inc(gate, 1)
                        for k in range(KT):
                            last = v.bn_aggr(mv[:, b.s4, stage, k, :], bn[:, b.s4, stage, k, :])
                        last.then_inc((ag_, ag2)[stage], 1)
                    return step

                def affine_weight(b):
                    done(v, zr, b)
                    v.tensor_tensor(z[:, b.s4], z[:, b.s4], spread(ln_w[:, 0, :], KT), ALU.mult).then_inc(aw, 1)

                def outer_add(b):
                    done(v, aw, b)
                    done(v, bx, b)
                    v.tensor_tensor(z[:, b.s4], z[:, b.s4], ex[:, b.s4], ALU.add).then_inc(ao, 1)

                def shortcut_scale(b):
                    done(v, rr2, b, 4)
                    v.tensor_copy(sm[:, b.s4, 1, :], na[:, bass.ds(b.n * KT, KT)]).then_inc(wb, 1)

                def shortcut(b):
                    j = b.s4
                    done(v, mr2, b)
                    done(v, wb, b)
                    stored_all(v, stored, b)
                    for k in range(KT):
                        last = v.scalar_tensor_tensor(res[:, j, k, :], pM[b.s2][k // 2][:, (k % 2) * 2 * D:(k % 2) * 2 * D + D],
                                                      sm[:, j, 1, k:k + 1], z[:, j, k, :], ALU.mult, ALU.add)
                    last.then_inc(af, 1)

                steps = {
                    "gat": [(weight, 0), (aggregate(0), 2), (total, 0), (complete, 1), (reciprocal, 0),
                            (stats(0), 1), (mix, 0)],
                    "gat_end": [(weight, 0), (aggregate(0), 2), (total, 0), (complete, 1), (reciprocal, 0),
                                (affine_weight, 4), (stats(0), 1), (aggregate(1), 5), (outer_add, 4), (mix, 0),
                                (stats(1), 4)],
                    "rel0": [(weight, 0), (aggregate(0), 2), (affine_weight, 4), (mix, 0), (stats(0), 1)],
                    "rel1": [(weight, 0), (aggregate(0), 2), (complete, 1), (mix, 0), (stats(0), 1),
                             (affine_weight, 4)],
                    "rel2": [(weight, 0), (aggregate(0), 2), (complete, 1), (affine_weight, 4), (stats(0), 1),
                             (aggregate(1), 5), (outer_add, 4), (mix, 0), (stats(1), 4)],
                    "sage0": [(weight, 0), (complete, 1), (mix, 0)],
                    "sage1": [(weight, 0), (complete, 1), (mix, 0)],
                    "sage2": [(weight, 0), (aggregate(0), 2), (shortcut_scale, 4), (complete, 1), (shortcut, 5),
                              (stats(0), 1), (mix, 0)],
                    "fin": [(weight, 0), (aggregate(0), 2), (mix, 0), (stats(0), 1)]}.get(kind)
                if steps:
                    times(v, steps)

            @block.scalar
            def _(act):
                act.wait_ge(cst, 16 * len(consts))

                def keep_x(b):
                    done(act, tr, b)
                    act.activation(xT[:, b.s2].rearrange("f k n -> f (k n)"), pT[b.s2][:, :], ACT.Copy).then_inc(tk, 1)

                def keep_z(b):
                    done(act, tr2, b)
                    o, p_ = zT[:, b.s2].rearrange("f k n -> f (k n)"), pT[b.s2][:, :]
                    done(act, mr2, b, 2)
                    if kind == "gat":
                        act.activation(o, p_, ACT.Identity, scale=ln_c[:, 0:1], bias=ln_c[:, 1:2]).then_inc(tk2, 1)
                    else:
                        act.activation(o, p_, ACT.Copy).then_inc(tk2, 1)

                def norm(stage):
                    def step(b):
                        j = b.s4
                        done(act, (sr, sr2)[stage], b)
                        to, frm, sem = (z, y, zr) if stage == 0 else (res, z, rr)
                        if kind == "fin":
                            to, sem = res, rr
                        if to is res:
                            stored_all(act, stored, b)
                        elif kind in ("gat", "sage2"):
                            done(act, tr2, b, 4)
                            if kind == "sage2":
                                done(act, af, b, 4)
                        else:
                            done(act, rr if two_norms else rr2, b, 4)
                        for k in range(KT):
                            last = act.activation(to[:, j, k, :], frm[:, j, k, :], ACT.Identity, scale=rs[:, j, stage, 0, k:k + 1],
                                                  bias=rs[:, j, stage, 1, k:k + 1])
                        last.then_inc(sem, 1)
                    return step

                def heads(b):
                    done(act, mr2, b)
                    stored_all(act, stored, b)
                    for h in range(2):
                        p_ = pM[b.s2][h][:, 0:2 * AW].rearrange("p (k w) -> p k w", k=2)
                        act.activation(res[:, b.s4, 2 * h:2 * h + 2, :], p_, ACT.Copy)
                        last = act.activation(self.asad[:, bass.ds(b.n * KT + 2 * h, 2), :], p_[:, :, D:AW], ACT.Copy)
                    last.then_inc(rr, 1)

                def relu_affine(b):
                    done(act, af, b)
                    stored_all(act, stored2, b)
                    act.activation(res2[:, b.s4], z[:, b.s4], ACT.Relu).then_inc(rr2, 1)

                def relu_sum(b):
                    done(act, tb, b)
                    stored_all(act, stored, b)
                    act.activation(res[:, b.s4], y[:, b.s4], ACT.Relu).then_inc(rr, 1)

                def features(b):
                    done(act, mr2, b)
                    done(act, af, b)
                    stored_all(act, stored2, b)
                    for k in range(KT):
                        last = act.activation(res2[:, b.s4, k, :], pM[b.s2][k // 2][:, (k % 2) * 2 * D + D:(k % 2) * 2 * D + 2 * D],
                                              ACT.Copy, scale=sm[:, b.s4, 1, k:k + 1])
                    last.then_inc(rr2, 1)

                times(act, {"lin": [(keep_x, 0), (heads, 1)], "gat": [(norm(0), 0), (heads, 2), (keep_z, 0)],
                            "gat_end": [(norm(1), 4), (norm(0), 0)], "rel0": [(relu_affine, 3), (norm(0), 0)],
                            "rel1": [(relu_affine, 3), (norm(0), 0)], "rel2": [(norm(1), 4), (norm(0), 0)],
                            "sage0": [(keep_x, 0), (relu_sum, 3)], "sage1": [(keep_x, 0), (relu_sum, 3)],
                            "sage2": [(keep_z, 4), (keep_x, 0), (features, 6), (norm(0), 3)], "fin": [(norm(0), 0)]}[kind])


def gnn_kernel(nc, a, out, N, E):
    Kernel(nc, a, out, N, E).build()


def kernel(**inputs):
    import numpy as _np
    import concourse.bacc as _bacc
    from concourse import mybir as _mybir
    from concourse.bass_utils import run_bass_kernel_spmd as _run

    t = {k: _np.asarray(v) for k, v in inputs.items()}
    N, E = t["x"].shape[0], t["src"].shape[0]
    C = -(-E // BLOCK) * KT
    NP = -(-N // BLOCK) * BLOCK

    def edges(v, fill=0):
        w = _np.full((C * P,) + v.shape[1:], fill, v.dtype)
        w[:E] = v
        return _np.ascontiguousarray(_np.moveaxis(w.reshape((C, P) + v.shape[1:]), 0, 1))

    def rows(v, n):
        w = _np.zeros((n,) + v.shape[1:], v.dtype)
        w[:v.shape[0]] = v
        return w

    def vectors(w):
        o = _np.zeros((96, 96), w.dtype)
        for m in range(3):
            o[m::3, m::3] = w
        return o

    d = {"x": rows(t["x"], NP), "src": edges(t["src"]), "dst": edges(t["dst"], NP - 1), "edge_type_5": edges(t["edge_type_5"]),
         "edge_attr_4": edges(t["edge_attr_4"]), "edge_attr_16": edges(t["edge_attr_16"]),
         "edge_attr_128": rows(t["edge_attr_128"], C * P)}
    d["node_vec1"] = _np.ascontiguousarray(rows(t["node_vec1"], NP).reshape(-1, P, KT).transpose(1, 0, 2).reshape(P, -1))
    for n in ("W", "We", "bias", "ln_gamma", "ln_beta"):
        d["L0_gnn_" + n] = t["L0_gnn_" + n]
    d["L0_gnn_att_edge"] = _np.ascontiguousarray(t["L0_gnn_att_edge"].T)
    d["L0_att_cols"] = _np.stack([t["L0_gnn_att_src"], t["L0_gnn_att_dst"]], axis=-1)
    d["L0_ln_cols"] = _np.stack([t["L0_gnn_ln_gamma"], t["L0_gnn_ln_beta"]], axis=-1)
    d["dst_rows"] = _np.concatenate([t["dst"], _np.full(C * P + 1 - E, NP - 1, t["dst"].dtype)])
    rel = t["L1_gnn_relvecs"]
    d["L1_gnn_relvecs"] = _np.zeros((rel.shape[0], KT * 8, KT * D), rel.dtype)
    for k in range(KT):
        d["L1_gnn_relvecs"][:, 8 * k:8 * k + rel.shape[1], k * D:(k + 1) * D] = rel
    d["L1_gnn_lin_w"] = _np.ascontiguousarray(t["L1_gnn_lin_w"].transpose(0, 2, 1))
    for n in ("lin_b", "ln_w", "ln_b"):
        d["L1_gnn_" + n] = t["L1_gnn_" + n]
    for l in range(3):
        d[f"L2_gnn_Ws{l}"] = _np.ascontiguousarray(t[f"L2_gnn_Ws{l}"].T)
        d[f"L2_gnn_Wn{l}"] = _np.ascontiguousarray(t[f"L2_gnn_Wn{l}"].T)
        d[f"L2_gnn_b{l}"] = t[f"L2_gnn_b{l}"]
    d["iota8"] = _np.tile(_np.arange(8, dtype=_np.float32), (P, 1))
    f32 = t["x"].dtype
    d["L3_in"] = _np.zeros((D, 2 * D), f32)
    for o, (s, v) in ((0, ("W_sc0", "W_sc1")), (D, ("W_l10", "W_l11"))):
        d["L3_in"][:MUL, o:o + MUL] = t["L3_gnn_" + s]
        d["L3_in"][MUL:, o + MUL:o + D] = vectors(t["L3_gnn_" + v])
    d["L3_out"] = _np.zeros((D, 2, D + 1), f32)
    for h, (s, v, al) in enumerate((("W_l2a", "W_l2d", "A0"), ("W_l2b", "W_l2c", "A1"))):
        d["L3_out"][:MUL, h, :MUL] = t["L3_gnn_" + s]
        d["L3_out"][MUL:, h, MUL:D] = vectors(t["L3_gnn_" + v])
        d["L3_out"][:MUL, h, D] = t["L3_gnn_" + al][:, 0]
    w1 = t["L3_gnn_W_mlp1"]
    d["L3_gnn_W_mlp1"] = _np.zeros((KT * 16, KT, 64), f32)
    for k in range(KT):
        d["L3_gnn_W_mlp1"][16 * k:16 * k + 16, k] = w1
    w2 = t["L3_gnn_W_mlp2"]
    d["L3_gnn_W_mlp2"] = _np.concatenate([w2[:, 0:32], _np.repeat(w2[:, 64:96], 3, axis=1), w2[:, 96:128], w2[:, 32:64]], axis=1)

    nc = _bacc.Bacc("TRN2", target_bir_lowering=False, num_devices=1)
    arrays, args = {}, {}
    for name, v in d.items():
        arrays[f"in_{name}"] = v
        args[name] = nc.dram_tensor(f"in_{name}", v.shape, _mybir.dt.from_np(v.dtype), kind="ExternalInput").ap()
    out = nc.dram_tensor("out_0_dram", (NP, D), F32, kind="ExternalOutput").ap()
    gnn_kernel(nc, args, out, N, E)
    r = _run(nc, [arrays], core_ids=[0])
    return r.results[0]["out_0_dram"][:N]
```
